# Optimizing a Trainium2 kernel written in Bass

```python
import numpy as np
import jax
import jax.numpy as jnp

def _softmax(x, axis=-1):
    return jax.nn.softmax(x, axis=axis)

def _gelu(x):
    return jax.nn.gelu(x, approximate=True)

def _silu(x):
    return jax.nn.silu(x)

def _sigmoid(x):
    return jax.nn.sigmoid(x)

def _layernorm(x, axis=-1, eps=1e-05):
    m = jnp.mean(x, axis=axis, keepdims=True)
    v = jnp.var(x, axis=axis, keepdims=True)
    return (x - m) / jnp.sqrt(v + eps)

def _scatter_add(tgt, idx, src, axis=0):
    return tgt.at[idx].add(src)

def _segment_sum(src, seg, n):
    return jax.ops.segment_sum(src, seg, n)
kernel_name = 'mk_prb_d1_jaxref_r4_01b11c'

def setup_inputs(seed: int=0):
    np.random.seed(seed)
    _w = jnp.asarray

    def _L0_attn_setup():
        import jax, jax.numpy as jnp
        import numpy as np
        B, S, HID = (1, 512, 512)
        H, NOPE, ROPE, VDIM = (16, 128, 64, 128)
        QR, KVR = (384, 128)
        IH, ID = (16, 128)
        TOPK = 128
        THETA = 10000.0
        EPS = 1e-06
        SCALE = (NOPE + ROPE) ** (-0.5)
        NEG = -1000000000.0

        def _cos_sin(s, dim, dtype):
            inv = 1.0 / THETA ** (np.arange(0, dim, 2, dtype=np.float32) / dim)
            t = np.arange(s, dtype=np.float32)
            f = np.outer(t, inv)
            emb = np.concatenate([f, f], -1)
            return (jnp.asarray(np.cos(emb), dtype), jnp.asarray(np.sin(emb), dtype))

        def _rope(x, cos, sin):
            x1, x2 = jnp.split(x, 2, axis=-1)
            rot = jnp.concatenate([-x2, x1], axis=-1)
            return x * cos[None, :, None, :] + rot * sin[None, :, None, :]

        def _rmsnorm(x, w):
            v = jnp.mean(x.astype(jnp.float32) ** 2, -1, keepdims=True)
            return (x.astype(jnp.float32) * jax.lax.rsqrt(v + EPS)).astype(x.dtype) * w

        def _layernorm(x, w, b):
            m = jnp.mean(x, -1, keepdims=True)
            v = jnp.var(x, -1, keepdims=True)
            return (x - m) * jax.lax.rsqrt(v + EPS) * w + b
        key = jax.random.key(seed)
        ks = jax.random.split(key, 12)
        g = lambda k, shp: jax.random.normal(k, shp, jnp.float32) * 0.02
        return {'hidden_states': jax.random.normal(ks[0], (B, S, HID), jnp.float32), 'q_a_w': g(ks[1], (QR, HID)), 'q_a_ln_w': jnp.ones((QR,), jnp.float32), 'q_b_w': g(ks[2], (H * (NOPE + ROPE), QR)), 'kv_a_w': g(ks[3], (KVR + ROPE, HID)), 'kv_a_ln_w': jnp.ones((KVR,), jnp.float32), 'kv_b_w': g(ks[4], (H * (NOPE + VDIM), KVR)), 'o_w': g(ks[5], (HID, H * VDIM)), 'idx_wq_b_w': g(ks[6], (IH * ID, QR)), 'idx_wk_w': g(ks[7], (ID, HID)), 'idx_kn_w': jnp.ones((ID,), jnp.float32), 'idx_kn_b': jnp.zeros((ID,), jnp.float32), 'idx_wproj_w': g(ks[8], (IH, HID))}
    _L0_attn_in = _L0_attn_setup()

    def _L0_ffn_setup():
        import jax, jax.numpy as jnp
        import numpy as np
        E = 8
        TOP_K = 2
        D = 512
        M = 1792
        B, S = (2, 512)
        key = jax.random.key(seed)
        kx, kg, k1, k2, k3 = jax.random.split(key, 5)
        x = jax.random.normal(kx, (B, S, D), dtype=jnp.float32)
        gate_w = jax.random.normal(kg, (D, E), dtype=jnp.float32) / np.sqrt(D)
        w1 = jax.random.normal(k1, (E, D, M), dtype=jnp.float32) / np.sqrt(D)
        w2 = jax.random.normal(k2, (E, M, D), dtype=jnp.float32) / np.sqrt(M)
        w3 = jax.random.normal(k3, (E, D, M), dtype=jnp.float32) / np.sqrt(D)
        return {'x': x, 'gate_w': gate_w, 'w1': w1, 'w2': w2, 'w3': w3}
    _L0_ffn_in = _L0_ffn_setup()
    _d = {'L0_attn_hidden_states': _L0_attn_in['hidden_states'], 'L0_attn_q_a_w': _L0_attn_in['q_a_w'], 'L0_attn_q_a_ln_w': _L0_attn_in['q_a_ln_w'], 'L0_attn_q_b_w': _L0_attn_in['q_b_w'], 'L0_attn_kv_a_w': _L0_attn_in['kv_a_w'], 'L0_attn_kv_a_ln_w': _L0_attn_in['kv_a_ln_w'], 'L0_attn_kv_b_w': _L0_attn_in['kv_b_w'], 'L0_attn_o_w': _L0_attn_in['o_w'], 'L0_attn_idx_wq_b_w': _L0_attn_in['idx_wq_b_w'], 'L0_attn_idx_wk_w': _L0_attn_in['idx_wk_w'], 'L0_attn_idx_kn_w': _L0_attn_in['idx_kn_w'], 'L0_attn_idx_kn_b': _L0_attn_in['idx_kn_b'], 'L0_attn_idx_wproj_w': _L0_attn_in['idx_wproj_w'], 'L0_ffn_gate_w': _L0_ffn_in['gate_w'], 'L0_ffn_w1': _L0_ffn_in['w1'], 'L0_ffn_w2': _L0_ffn_in['w2'], 'L0_ffn_w3': _L0_ffn_in['w3']}
    _x0 = _d['L0_attn_hidden_states']
    _d['L0_attn_hidden_states'] = jax.random.normal(jax.random.fold_in(jax.random.key(seed), 1), (2, 1024, 512), dtype=_x0.dtype)
    del _x0
    return _d

def reference(L0_attn_hidden_states, L0_attn_q_a_w, L0_attn_q_a_ln_w, L0_attn_q_b_w, L0_attn_kv_a_w, L0_attn_kv_a_ln_w, L0_attn_kv_b_w, L0_attn_o_w, L0_attn_idx_wq_b_w, L0_attn_idx_wk_w, L0_attn_idx_kn_w, L0_attn_idx_kn_b, L0_attn_idx_wproj_w, L0_ffn_gate_w, L0_ffn_w1, L0_ffn_w2, L0_ffn_w3):

    def _L0_attn_ref(hidden_states, q_a_w, q_a_ln_w, q_b_w, kv_a_w, kv_a_ln_w, kv_b_w, o_w, idx_wq_b_w, idx_wk_w, idx_kn_w, idx_kn_b, idx_wproj_w):
        import jax, jax.numpy as jnp
        import numpy as np
        B, S, HID = (1, 512, 512)
        H, NOPE, ROPE, VDIM = (16, 128, 64, 128)
        QR, KVR = (384, 128)
        IH, ID = (16, 128)
        TOPK = 128
        THETA = 10000.0
        EPS = 1e-06
        SCALE = (NOPE + ROPE) ** (-0.5)
        NEG = -1000000000.0

        def _cos_sin(s, dim, dtype):
            inv = 1.0 / THETA ** (np.arange(0, dim, 2, dtype=np.float32) / dim)
            t = np.arange(s, dtype=np.float32)
            f = np.outer(t, inv)
            emb = np.concatenate([f, f], -1)
            return (jnp.asarray(np.cos(emb), dtype), jnp.asarray(np.sin(emb), dtype))

        def _rope(x, cos, sin):
            x1, x2 = jnp.split(x, 2, axis=-1)
            rot = jnp.concatenate([-x2, x1], axis=-1)
            return x * cos[None, :, None, :] + rot * sin[None, :, None, :]

        def _rmsnorm(x, w):
            v = jnp.mean(x.astype(jnp.float32) ** 2, -1, keepdims=True)
            return (x.astype(jnp.float32) * jax.lax.rsqrt(v + EPS)).astype(x.dtype) * w

        def _layernorm(x, w, b):
            m = jnp.mean(x, -1, keepdims=True)
            v = jnp.var(x, -1, keepdims=True)
            return (x - m) * jax.lax.rsqrt(v + EPS) * w + b
        b, s, _ = hidden_states.shape
        cos, sin = _cos_sin(s, ROPE, hidden_states.dtype)
        qr = _rmsnorm(hidden_states @ q_a_w.T, q_a_ln_w)
        q = (qr @ q_b_w.T).reshape(b, s, H, NOPE + ROPE)
        q_nope, q_pe = (q[..., :NOPE], q[..., NOPE:])
        q_pe = _rope(q_pe, cos, sin)
        ckv = hidden_states @ kv_a_w.T
        c_kv, k_pe = (ckv[..., :KVR], ckv[..., KVR:])
        k_pe = _rope(k_pe[:, :, None, :], cos, sin)
        kv = (_rmsnorm(c_kv, kv_a_ln_w) @ kv_b_w.T).reshape(b, s, H, NOPE + VDIM)
        k_nope, v = (kv[..., :NOPE], kv[..., NOPE:])
        iq = (qr @ idx_wq_b_w.T).reshape(b, s, IH, ID)
        iq = jnp.concatenate([_rope(iq[..., :ROPE], cos, sin), iq[..., ROPE:]], -1)
        ik = _layernorm(hidden_states @ idx_wk_w.T, idx_kn_w, idx_kn_b)
        ik_pe = _rope(ik[:, :, None, :ROPE], cos, sin)[:, :, 0, :]
        ik = jnp.concatenate([ik_pe, ik[..., ROPE:]], -1)
        iw = hidden_states @ idx_wproj_w.T * IH ** (-0.5)
        idx_scores = jnp.einsum('bqh,bhqk->bqk', iw, jax.nn.relu(jnp.einsum('bqhd,bkd->bhqk', iq, ik)))
        causal = jnp.tril(jnp.ones((s, s), bool))
        idx_scores = jnp.where(causal[None], idx_scores, -jnp.inf)
        _, top_idx = jax.lax.top_k(idx_scores, TOPK)
        bi = jnp.arange(b)[:, None, None]
        qi = jnp.arange(s)[None, :, None]
        keep = jnp.zeros((b, s, s), bool).at[bi, qi, top_idx].set(True)
        allowed = keep & causal[None]
        qh = jnp.concatenate([q_nope, q_pe], -1)
        kh = jnp.concatenate([k_nope, jnp.broadcast_to(k_pe, (b, s, H, ROPE))], -1)
        scores = jnp.einsum('bqhd,bkhd->bhqk', qh, kh) * SCALE
        scores = jnp.where(allowed[:, None], scores, NEG)
        attn = jax.nn.softmax(scores, -1)
        out = jnp.einsum('bhqk,bkhd->bqhd', attn, v).reshape(b, s, H * VDIM)
        return out @ o_w.T

    def _L0_ffn_ref(x, gate_w, w1, w2, w3):
        import jax, jax.numpy as jnp
        import numpy as np
        E = 8
        TOP_K = 2
        D = 512
        M = 1792
        B, S = (2, 512)
        b, s, d = x.shape
        x_flat = x.reshape(-1, d)
        router_logits = x_flat @ gate_w
        router_probs = jax.nn.softmax(router_logits, axis=-1)
        topk_w, topk_idx = jax.lax.top_k(router_probs, TOP_K)
        topk_w = topk_w / jnp.sum(topk_w, axis=-1, keepdims=True)
        idx_flat = topk_idx.reshape(-1)
        sort_idx = jnp.argsort(idx_flat)
        x_rep_sort = jnp.take(x_flat, sort_idx // TOP_K, axis=0)
        group_sizes = jnp.bincount(idx_flat, length=E).astype(jnp.int32)
        h = jax.lax.ragged_dot(x_rep_sort, w1, group_sizes)
        h = jax.nn.silu(h) * jax.lax.ragged_dot(x_rep_sort, w3, group_sizes)
        out_sort = jax.lax.ragged_dot(h, w2, group_sizes)
        inv_sort_idx = jnp.argsort(sort_idx)
        out_rep = jnp.take(out_sort, inv_sort_idx, axis=0).reshape(-1, TOP_K, d)
        out = jnp.einsum('tkd,tk->td', out_rep, topk_w)
        return out.reshape(b, s, d)
    x = L0_attn_hidden_states
    xn = _layernorm(x, axis=-1)
    x = x + _L0_attn_ref(xn, L0_attn_q_a_w, L0_attn_q_a_ln_w, L0_attn_q_b_w, L0_attn_kv_a_w, L0_attn_kv_a_ln_w, L0_attn_kv_b_w, L0_attn_o_w, L0_attn_idx_wq_b_w, L0_attn_idx_wk_w, L0_attn_idx_kn_w, L0_attn_idx_kn_b, L0_attn_idx_wproj_w) + _L0_ffn_ref(xn, L0_ffn_gate_w, L0_ffn_w1, L0_ffn_w2, L0_ffn_w3)
    return x

_drawn_inputs = setup_inputs


def setup_inputs(seed=0):
    import zlib

    import numpy as np

    out = dict(_drawn_inputs(seed))
    spreads = {'L0_attn_q_a_ln_w': (1.0, 0.6),
     'L0_attn_kv_a_ln_w': (1.0, 0.6),
     'L0_attn_idx_kn_w': (1.0, 0.6),
     'L0_attn_idx_kn_b': (0.0, 0.8)}
    factors = {'L0_attn_q_a_w': 3.689,
     'L0_attn_q_b_w': 8.0,
     'L0_attn_idx_wq_b_w': 3.75,
     'L0_attn_idx_wk_w': 3.749,
     'L0_attn_idx_wproj_w': 3.76}
    for name, (base, spread) in spreads.items():
        noise = np.random.default_rng([zlib.crc32(name.encode()), seed]).standard_normal(out[name].shape)
        drawn = base * np.exp(spread * noise) if base else spread * noise
        out[name] = jnp.asarray(drawn.astype(out[name].dtype))
    for name, factor in factors.items():
        out[name] = (out[name] * factor).astype(out[name].dtype)
    return out
```

```python
import numpy as np
import concourse.bass as bass
from concourse import mybir
from contextlib import ExitStack

F32 = mybir.dt.float32
F32R = mybir.dt.float32r
I32 = mybir.dt.int32
U32 = mybir.dt.uint32
ALU = mybir.AluOpType
ACT = mybir.ActivationFunctionType
AX = mybir.AxisListType

P = 128
B, S, D = 2, 1024, 512
T = B * S
NT = S // P
KD = D // P
H, NOPE, ROPE, VD = 16, 128, 64, 128
QR, KVR = 384, 128
KQ = QR // P
ID = 128
TOPK = 128
HALF = ROPE // 2
SCALE = float(NOPE + ROPE) ** -0.5
EPS_LN, EPS_RMS = 1e-5, 1e-6
NE, MF = 8, 1792
KM = MF // P
CQ, CKV, CKP, CIK, CIW, CLG = 0, 384, 512, 576, 704, 720
NA = 728
NB = NA - QR
BLK = 256
NBLK = (2 * T - NE) // BLK + NE
ROWS = NBLK * BLK
MASKED = -1.0e30
TAKEN = -3.0e38
EXT = [(i + 1) * P for i in range(NT)]
OFF = [sum(EXT[:i]) for i in range(NT + 1)]
PAIRS = H // 2
NWR = 7
SLAB = 204 * 1024
RT_SHIFTED, RT_MARKED = 1, 14
NPE, NPR, NTP = 2, 6, 12
SHARED = NPE + 2 * (NPR + NTP)


class Ev:

    def __init__(self, sem, credit=0, step=1):
        self.sem, self.credit, self.step = sem, credit, step

    def at(self, n, back=0):
        return (n - (back - 1 - self.credit)) * self.step


def build(nc, io):
    ctx = ExitStack()
    with ctx:
        evs = {"act": [], "dve": [], "pool": [], "pe": [], "sp": []}

        def ev(name, owner, credit=0, step=1):
            e = Ev(ctx.enter_context(nc.semaphore(name)), credit, step)
            evs[owner].append(e)
            return e

        def dma_ev(name, owner, credit=0):
            return ev(name, owner, credit, 16)

        cursor = [(nc.sbuf_base + 31) // 32 * 32]
        ctx.enter_context(nc.sbuf_tensor("slab", [P, SLAB // 4], F32))

        def place(name, shape, dt=F32):
            t = nc.alloc_sbuf_tensor_at(name, shape, dt, offset=cursor[0])
            cursor[0] += (int(np.prod(shape[1:])) * 4 + 31) // 32 * 32
            return t

        def pair(name, shape):
            return place(name + "_hi", shape, F32R), place(name + "_lo", shape, F32R)

        ident = place("ident", [P, P])
        causal = place("causal", [P, P])
        upper = place("upper", [P, P])
        ones = place("ones", [P, P])
        rope_c = place("rope_c", [P, S])
        rope_s = place("rope_s", [P, S])
        idx_c = place("idx_c", [P, S])
        nat_c = place("nat_c", [P, NT, HALF])
        nat_s = place("nat_s", [P, NT, HALF])
        kn_w = place("kn_w", [P, ID])
        kn_b = place("kn_b", [P, ID])
        q_ln = place("q_ln", [P, KQ])
        kv_ln = place("kv_ln", [P, 1])
        eps_ln = place("eps_ln", [P, 1])
        eps_rms = place("eps_rms", [P, 1])
        logits = place("logits", [P, B * NT, NE])
        iw = place("iw", [P, NT, H])
        qrT = pair("qrT", [P, KQ, S])
        ckvT = pair("ckvT", [P, S])
        kpT = pair("kpT", [P, 2, S])
        ikT = pair("ikT", [P, S])
        acc = place("acc", [P, OFF[NT]])
        REGION = cursor[0]
        const_tiles = [("ident", ident), ("causal", causal), ("upper", upper), ("ones", ones), ("rope_c", rope_c),
                       ("rope_s", rope_s), ("idx_c", idx_c), ("nat_c", nat_c), ("nat_s", nat_s),
                       ("kn_w", kn_w), ("kn_b", kn_b), ("q_ln", q_ln), ("kv_ln", kv_ln)]

        wa_raw = place("wa_raw", [P, KD, NA])
        wa = pair("wa", [P, KD, NA])
        x_sb = place("x_sb", [P, 2, D])
        xn = place("xn", [P, 2, D])
        xT = pair("xT", [P, 2, D])
        ln_st = place("ln_st", [P, 2, 6])
        ln_mv = place("ln_mv", [P, 2, 2])
        ln_sd = place("ln_sd", [P, 2, 1])
        ln_r = place("ln_r", [P, 2, 1])
        junk = place("junk", [P, 2, QR])
        junk2 = place("junk2", [P, 2, KVR])
        bs = place("bs", [P, 2, NB])
        ssq = place("ssq", [P, 2, 2])
        ik_st = place("ik_st", [P, 2, 6])
        ik_mv = place("ik_mv", [P, 2, 2])
        sd3 = place("sd3", [P, 2, 3])
        r3 = place("r3", [P, 2, 3])
        nat_q = place("nat_q", [P, 2, QR + KVR])
        nat_k = place("nat_k", [P, 2, 3, P])
        ikn = place("ikn", [P, ID])
        rk1 = place("rk1", [P, 2, HALF])
        rk2 = place("rk2", [P, 2, HALF])
        ri1 = place("ri1", [P, 2, HALF])
        ri2 = place("ri2", [P, 2, HALF])

        cursor[0] = REGION
        wi_raw = place("wi_raw", [P, 2, KQ, P])
        wi = pair("wi", [P, 2, KQ, P])
        iy = place("iy", [P, 2, 512])
        scaled = place("scaled", [P, 512])
        turned = place("turned", [P, 512])
        iqT = pair("iqT", [P, 2, S])
        relu = place("relu", [P, 2, S])
        m8 = place("m8", [P, 8])

        cursor[0] = REGION
        wh_raw = place("wh_raw", [P, 2, 640])
        wp_raw = place("wp_raw", [P, KQ, P])
        wh = pair("wh", [P, 2, 640])
        wp = pair("wp", [P, KQ, P])
        qn = pair("qn", [P, S])
        qp = pair("qp", [P, S])
        kT = pair("kT", [P, S])
        v_ = pair("v", [P, NT, VD])
        py = place("py", [P, 2, 512])
        p_scaled = place("p_scaled", [P, 512])
        p_turned = place("p_turned", [P, 512])
        probs = place("probs", [P, OFF[NT]])
        nmax = place("nmax", [P, NT])
        row_sum = place("row_sum", [P, NT])
        rinv = place("rinv", [P, NT])
        PT = pair("PT", [P, 2, 512])
        oT = place("oT", [P, 2, 512])

        cursor[0] = REGION
        oT_raw = place("oT_raw", [P, 2, S])
        ow_raw = place("ow_raw", [P, 2, D])
        oTr = pair("oTr", [P, 2, S])
        ow = pair("ow", [P, 2, D])
        xo = place("xo", [P, 2, D])
        po = place("po", [P, 2, D])

        cursor[0] = REGION
        slots = place("slots", [P, 2, B * NT], I32)
        gates = place("gates", [P, 2, B * NT])
        owner = place("owner", [1, NBLK], I32)
        MOE = cursor[0]
        r_e = place("r_e", [P, B * NT, NE])
        r_t = place("r_t", [P, B * NT])
        r_m = place("r_m", [P, B * NT, 8])
        r_i = place("r_i", [P, B * NT, 8], U32)
        r_if = place("r_if", [P, B * NT, 8])
        r_oh = place("r_oh", [P, 2, B * NT, NE])
        r_mk = place("r_mk", [P, B * NT, NE])
        r_a = place("r_a", [P, B * NT, NE])
        r_b = place("r_b", [P, B * NT, NE])
        r_cnt = place("r_cnt", [P, NE, NE])
        r_n = place("r_n", [P, 3, NE])
        r_sl = place("r_sl", [P, 2, B * NT])
        r_ow = place("r_ow", [P, NBLK, NE])
        r_of = place("r_of", [P, NBLK])
        iota8 = place("iota8", [P, NE])
        lim8 = place("lim8", [P, NE])
        iotab = place("iotab", [P, NBLK])
        rows = place("rows", [P, 2, D])
        zero = place("zero", [P, 2, D])
        cursor[0] = MOE
        xe = place("xe", [P, 2, D])
        xeT = pair("xeT", [P, KD, BLK])
        we = place("we", [P, NWR, 3 * D])
        wgu = pair("wgu", [P, 2, 2 * D])
        wdn = pair("wdn", [P, 2, D])
        sg = place("sg", [P, 2, BLK])
        hf = place("hf", [P, 2, BLK])
        hT = pair("hT", [P, 2, BLK])
        ye = place("ye", [P, 2, D])
        g_a = place("g_a", [P, 2, D])
        g_b = place("g_b", [P, 2, D])
        part_sb = place("part_sb", [P, 2, D])
        mix = place("mix", [P, 2, D])
        fin = place("fin", [P, 2, D])
    
        def projection(c, part):
            if c < 4:
                return (qn if c < 2 else kT)[part][:, c % 2 * 512:c % 2 * 512 + 512]
            return v_[part][:, (c - 4) * 4:(c - 4) * 4 + 4, :]

        banks = ctx.enter_context(nc.psum_tensor("banks", [P, 8, 512]))

        xn_d = nc.dram_tensor("xn_d", (B * NT, P, D), F32, kind="Internal").ap()
        oT_d = nc.dram_tensor("oT_d", (B, H, P, S), F32, kind="Internal").ap()
        part_d = nc.dram_tensor("part_d", (B * NT, P, D), F32, kind="Internal").ap()
        xs_d = nc.dram_tensor("xs_d", (ROWS, D), F32, kind="Internal").ap()
        ys_d = nc.dram_tensor("ys_d", (ROWS, D), F32, kind="Internal").ap()
        xs_blk = xs_d.rearrange("(k a p) d -> k p a d", p=P, a=2)
        ys_blk = ys_d.rearrange("(k a p) d -> k p a d", p=P, a=2)
        x_t = io["x"].rearrange("b (t p) d -> (b t) p d", p=P)
        out_t = io["out"].rearrange("b (t p) d -> (b t) p d", p=P)

        phase_end = ctx.enter_context(nc.semaphore("phase_end"))
        consts = dma_ev("consts", "sp")
        wa_in = dma_ev("wa_in", "sp")
        x_in = [dma_ev(f"x_in{j}", "sp") for j in range(2)]
        wi_in = [dma_ev(f"wi_in{j}", "sp") for j in range(2)]
        wh_in = [dma_ev(f"wh_in{j}", "sp") for j in range(2)]
        wp_in = dma_ev("wp_in", "sp")
        oT_out = [dma_ev(f"oT_out{j}", "sp", 1) for j in range(2)]
        o_in = [dma_ev(f"o_in{j}", "sp") for j in range(2)]
        ow_in = [dma_ev(f"ow_in{j}", "sp") for j in range(2)]
        xo_in = [dma_ev(f"xo_in{j}", "sp") for j in range(2)]
        zero_out = dma_ev("zero_out", "sp")
        row_in = [dma_ev(f"row_in{j}", "sp") for j in range(2)]
        xe_in = dma_ev("xe_in", "sp")
        we_in = [dma_ev(f"we_in{j}", "sp") for j in range(NWR)]
        part_in = [dma_ev(f"part_in{j}", "sp") for j in range(2)]
        wa_hi_ok = ev("wa_hi_ok", "act")
        deviation = ev("deviation", "act")
        xn_out = [dma_ev(f"xn_out{j}", "act", 1) for j in range(2)]
        xhi_ok = ev("xhi_ok", "act")
        squares = ev("squares", "act")
        roots = ev("roots", "act")
        nhi_ok = ev("nhi_ok", "act")
        wi_hi_ok = ev("wi_hi_ok", "act")
        iqhi_ok = ev("iqhi_ok", "act")
        relu_ok = ev("relu_ok", "act", 2)
        wh_hi_ok = ev("wh_hi_ok", "act")
        wp_hi_ok = ev("wp_hi_ok", "act")
        qphi_ok = ev("qphi_ok", "act")
        sh_hi = ev("sh_hi", "act")
        exps = ev("exps", "act")
        oT_read = ev("oT_read", "act", 2)
        ohi_ok = ev("ohi_ok", "act")
        owhi_ok = ev("owhi_ok", "act")
        part_out = [dma_ev(f"part_out{j}", "act", 1) for j in range(2)]
        rt_exp = ev("rt_exp", "act")
        wguhi_ok = ev("wguhi_ok", "act")
        wdnhi_ok = ev("wdnhi_ok", "act")
        xehi_ok = ev("xehi_ok", "act")
        silu_ok = ev("silu_ok", "act")
        hhi_ok = ev("hhi_ok", "act")
        ye_ok = ev("ye_ok", "act", 1)
        ye_out = dma_ev("ye_out", "act", 1)
        fin_out = [dma_ev(f"fin_out{j}", "act", 1) for j in range(2)]
        eps_ok = ev("eps_ok", "dve")
        stats = ev("stats", "dve")
        moments = ev("moments", "dve")
        inverse = ev("inverse", "dve")
        normed = ev("normed", "dve", 2)
        xlo_ok = ev("xlo_ok", "dve", 2)
        copied = ev("copied", "dve")
        ik_stats = ev("ik_stats", "dve")
        ik_moments = ev("ik_moments", "dve")
        inverses = ev("inverses", "dve")
        natq_ok = ev("natq_ok", "dve", 2)
        nlo_ok = ev("nlo_ok", "dve", 2)
        acc_clear = ev("acc_clear", "dve")
        i_parts = ev("i_parts", "dve", 2)
        iy_ok = ev("iy_ok", "dve", 1)
        acc_ok = ev("acc_ok", "dve", 2)
        diag_ok = ev("diag_ok", "dve")
        top8_ok = ev("top8_ok", "dve")
        taken_ok = ev("taken_ok", "dve", 1)
        mask_ok = ev("mask_ok", "dve")
        sh_read = ev("sh_read", "dve", 2)
        py_ok = ev("py_ok", "dve", 1)
        masked = ev("masked", "dve", 2)
        sums_inv = ev("sums_inv", "dve")
        olo_ok = ev("olo_ok", "dve", 2)
        po_ok = ev("po_ok", "dve", 2)
        rt = ev("rt", "dve")
        slots_ok = ev("slots_ok", "dve")
        wgulo_ok = ev("wgulo_ok", "dve", NWR)
        xelo_ok = ev("xelo_ok", "dve", 2)
        h_ok = ev("h_ok", "dve", 2)
        mix_ok = ev("mix_ok", "dve")
        fin_ok = ev("fin_ok", "dve", 2)
        wa_lo_ok = ev("wa_lo_ok", "pool")
        nat_clear = ev("nat_clear", "pool")
        key_step = [ev(f"key_step{j}", "pool") for j in range(5)]
        natk_ok = ev("natk_ok", "pool", 2)
        wi_lo_ok = ev("wi_lo_ok", "pool", 2)
        iqlo_ok = ev("iqlo_ok", "pool", 2)
        wh_lo_ok = ev("wh_lo_ok", "pool", 2)
        wp_lo_ok = ev("wp_lo_ok", "pool", 1)
        qplo_ok = ev("qplo_ok", "pool", 2)
        p_norm = ev("p_norm", "pool")
        owlo_ok = ev("owlo_ok", "pool", 2)
        zero_ok = ev("zero_ok", "pool")
        rt_pool = ev("rt_pool", "pool")
        row_sc = [dma_ev(f"row_sc{j}", "pool") for j in range(2)]
        wdnlo_ok = ev("wdnlo_ok", "pool", NWR)
        hlo_ok = ev("hlo_ok", "pool", 2)
        g_in = [dma_ev(f"g_in{j}", "pool") for j in range(2)]
        xt_full = ev("xt_full", "pe", 2)
        projected = ev("projected", "pe")
        nt_full = ev("nt_full", "pe", 2)
        iq_full = ev("iq_full", "pe", 4)
        is_full = ev("is_full", "pe", 1)
        sh_full = ev("sh_full", "pe")
        sc_full = ev("sc_full", "pe")
        pv_done = ev("pv_done", "pe", 2)
        o_mm = ev("o_mm", "pe", 2)
        rt_pe = ev("rt_pe", "pe")
        xeT_full = ev("xeT_full", "pe", 2)
        gu_full = ev("gu_full", "pe")
        down = ev("down", "pe", 2)

        spare = {}

        def in_register(eng, value):
            if eng not in spare:
                spare[eng] = eng.alloc_register(name="behind")
            eng.reg_mov(spare[eng], value)
            return spare[eng]

        block = ctx.enter_context(nc.Block())

        def barrier(eng, k, b=None):
            eng.drain().then_inc(phase_end, 1)
            if b is None:
                eng.wait_ge(phase_end, 5 * (4 * B + 1 + k))
            else:
                behind = in_register(eng, b * 20 + 5 * (k + 1))
                eng.wait_ge(phase_end, 5)
                eng.wait_ge(phase_end, behind)

        def three(pe, out, left, right, start=True, stop=True):
            pe.matmul(out, left[0], right[0], start=start, stop=False, skip_group_check=True)
            pe.matmul(out, left[0], right[1], start=False, stop=False, skip_group_check=True)
            return pe.matmul(out, left[1], right[0], start=False, stop=stop, skip_group_check=True)

        def cut(parts, *at):
            return parts[0][at], parts[1][at]

        def scores_psum(r, width):
            return banks[:, 2 * r:2 * r + 2, :].rearrange("p a c -> p (a c)")[:, 0:width]

        def plain(part):
            return part.bitcast(F32)

        @block.sync
        def _(sp):
            for e in evs["sp"]:
                if e.credit:
                    sp.sem_inc(e.sem, e.credit * e.step)
            for name, tile in const_tiles:
                sp.dma_start(tile[:], io[name]).then_inc(consts.sem, consts.step)
            with sp.Fori(0, B) as b:
                sp.dma_start(wa_raw[:], io["wa"]).then_inc(wa_in.sem, wa_in.step)
                with sp.Fori(0, NT // 2) as it:
                    for j in range(2):
                        n = b * NT + it * 2 + j
                        sp.wait_ge(normed.sem, normed.at(n, 2))
                        sp.dma_start(x_sb[:, j, :], x_t[n]).then_inc(x_in[j].sem, x_in[j].step)
                barrier(sp, 0, b)
                with sp.Fori(0, PAIRS) as hp:
                    for u in range(2):
                        sp.wait_ge(wi_lo_ok.sem, wi_lo_ok.at(b * (H + 1) + hp * 2 + u, 2))
                        sp.dma_start(wi_raw[:, u], io["wi"][hp * 2 + u]).then_inc(wi_in[u].sem, wi_in[u].step)
                sp.wait_ge(wi_lo_ok.sem, wi_lo_ok.at(b * (H + 1) + H, 2))
                sp.dma_start(wi_raw[:, 0], io["wi"][0]).then_inc(wi_in[0].sem, wi_in[0].step)
                barrier(sp, 1, b)
                sp.wait_ge(wp_lo_ok.sem, wp_lo_ok.at(b * (PAIRS + 1), 1))
                sp.dma_start(wp_raw[:], io["wp"][0]).then_inc(wp_in.sem, wp_in.step)
                sp.wait_ge(wh_lo_ok.sem, wh_lo_ok.at(b * (H + 1), 2))
                sp.dma_start(wh_raw[:, 0], io["wh"][0]).then_inc(wh_in[0].sem, wh_in[0].step)
                with sp.Fori(0, PAIRS) as hp:
                    for u in range(2):
                        h = hp * 2 + u
                        sp.wait_ge(wh_lo_ok.sem, wh_lo_ok.at(b * (H + 1) + h + 1, 2))
                        sp.dma_start(wh_raw[:, 1 - u], io["wh"][h + 1]).then_inc(wh_in[1 - u].sem, wh_in[1 - u].step)
                        if u == 1:
                            sp.wait_ge(wp_lo_ok.sem, wp_lo_ok.at(b * (PAIRS + 1) + hp + 1, 1))
                            sp.dma_start(wp_raw[:], io["wp"][hp + 1]).then_inc(wp_in.sem, wp_in.step)
                        for s in range(2):
                            sp.wait_ge(oT_read.sem, oT_read.at((b * H + h) * 2 + s))
                            sp.dma_start(oT_d[b, h, :, s * 512:s * 512 + 512], oT[:, s, :]).then_inc(oT_out[s].sem, oT_out[s].step)
                for s in range(2):
                    behind = in_register(sp, oT_out[s].at(b * H + H - 1))
                    sp.wait_ge(oT_out[s].sem, oT_out[s].step)
                    sp.wait_ge(oT_out[s].sem, behind)
                barrier(sp, 2, b)
                with sp.Fori(0, H // 2) as hp:
                    for j in range(2):
                        h = hp * 2 + j
                        sp.wait_ge(olo_ok.sem, olo_ok.at(b * H + h, 2))
                        sp.wait_ge(owlo_ok.sem, owlo_ok.at(b * H + h, 2))
                        sp.dma_start(oT_raw[:, j, :], oT_d[b, h]).then_inc(o_in[j].sem, o_in[j].step)
                        sp.dma_start(ow_raw[:, j, :], io["ow"][h]).then_inc(ow_in[j].sem, ow_in[j].step)
                with sp.Fori(0, NT // 2) as it:
                    for j in range(2):
                        n = b * NT + it * 2 + j
                        sp.wait_ge(po_ok.sem, po_ok.at(n, 2))
                        sp.dma_start(xo[:, j, :], x_t[n]).then_inc(xo_in[j].sem, xo_in[j].step)
                barrier(sp, 3, b)
            sp.wait_ge(zero_ok.sem, zero_ok.at(0))
            with sp.Fori(0, NBLK) as k:
                sp.dma_start(xs_blk[k], zero[:]).then_inc(zero_out.sem, zero_out.step)
            sp.wait_ge(zero_out.sem, zero_out.at(NBLK - 1))
            for n in range(B * NT):
                if n >= 2:
                    sp.wait_ge(row_sc[n % 2].sem, row_sc[n % 2].at((n // 2) * 2 - 1))
                sp.dma_start(rows[:, n % 2, :], xn_d[n]).then_inc(row_in[n % 2].sem, row_in[n % 2].step)
            barrier(sp, 0)
            with sp.Fori(0, NBLK) as k:
                e = sp.value_load(owner[0:1, bass.ds(k, 1)], min_val=0, max_val=NE - 1)
                sp.wait_ge(xeT_full.sem, xeT_full.at(k * 2 + 1, 2))
                sp.dma_start(xe[:], xs_blk[k]).then_inc(xe_in.sem, xe_in.step)
                for m in range(KM):
                    r = m % NWR
                    sp.wait_ge(wgulo_ok.sem, wgulo_ok.at(k * KM + m, NWR))
                    sp.wait_ge(wdnlo_ok.sem, wdnlo_ok.at(k * KM + m, NWR))
                    sp.dma_start(we[:, r, :], io["we"][e * KM + m]).then_inc(we_in[r].sem, we_in[r].step)
            for m in range(2):
                sp.wait_ge(wgulo_ok.sem, wgulo_ok.at(NBLK * KM + m, NWR))
                sp.wait_ge(wdnlo_ok.sem, wdnlo_ok.at(NBLK * KM + m, NWR))
                sp.dma_start(we[:, m, :], io["we"][m]).then_inc(we_in[m].sem, we_in[m].step)
            barrier(sp, 1)
            with sp.Fori(0, B * NT // 2) as it:
                for j in range(2):
                    n = it * 2 + j
                    sp.wait_ge(fin_ok.sem, fin_ok.at(n, 2))
                    sp.dma_start(part_sb[:, j, :], part_d[n]).then_inc(part_in[j].sem, part_in[j].step)

        @block.scalar
        def _(act):
            for e in evs["act"]:
                if e.credit:
                    act.sem_inc(e.sem, e.credit * e.step)
            act.wait_ge(eps_ok.sem, eps_ok.at(0))
            act.wait_ge(consts.sem, consts.at(len(const_tiles) - 1))
            with act.Fori(0, B) as b:
                act.wait_ge(wa_in.sem, wa_in.at(b))
                act.activation(wa[0][:], wa_raw[:], ACT.Copy).then_inc(wa_hi_ok.sem, wa_hi_ok.step)
                with act.Fori(0, NT // 2) as it:
                    for j in range(2):
                        n = b * NT + it * 2 + j
                        act.wait_ge(moments.sem, moments.at(n))
                        act.activation(ln_sd[:, j, :], ln_mv[:, j, 1:2], ACT.Sqrt, bias=eps_ln[:, 0:1]).then_inc(deviation.sem, deviation.step)
                        act.wait_ge(normed.sem, normed.at(n))
                        act.dma_start(xn_d[n], xn[:, j, :]).then_inc(xn_out[j].sem, xn_out[j].step)
                    for j in range(2):
                        n = b * NT + it * 2 + j
                        act.wait_ge(xt_full.sem, xt_full.at(n))
                        act.activation(xT[0][:, j, :], banks[:, j, :], ACT.Copy).then_inc(xhi_ok.sem, xhi_ok.step)
                    for j in range(2):
                        n = b * NT + it * 2 + j
                        act.wait_ge(projected.sem, projected.at(n))
                        act.activation(junk[:, j, :], banks[:, 2 + 2 * j, 0:QR], ACT.Square, accum_out=ssq[:, j, 0:1])
                        act.wait_ge(copied.sem, copied.at(n))
                        act.activation(junk2[:, j, :], bs[:, j, 0:KVR], ACT.Square, accum_out=ssq[:, j, 1:2]).then_inc(squares.sem, squares.step)
                        act.wait_ge(ik_moments.sem, ik_moments.at(n))
                        act.wait_ge(squares.sem, squares.at(n))
                        act.activation(sd3[:, j, 0:1], ssq[:, j, 0:1], ACT.Sqrt, bias=eps_rms[:, 0:1], scale=1.0 / QR)
                        act.activation(sd3[:, j, 1:2], ssq[:, j, 1:2], ACT.Sqrt, bias=eps_rms[:, 0:1], scale=1.0 / KVR)
                        act.activation(sd3[:, j, 2:3], ik_mv[:, j, 1:2], ACT.Sqrt, bias=eps_rms[:, 0:1]).then_inc(roots.sem, roots.step)
                    for j in range(2):
                        n = b * NT + it * 2 + j
                        cols = bass.ds((it * 2 + j) * P, P)
                        act.wait_ge(nt_full.sem, nt_full.at(n))
                        for c in range(KQ):
                            act.activation(qrT[0][:, c, cols], banks[:, 6, c * P:c * P + P], ACT.Identity, scale=q_ln[:, c:c + 1])
                        act.activation(ckvT[0][:, cols], banks[:, 6, QR:QR + KVR], ACT.Identity, scale=kv_ln[:, 0:1])
                        act.activation(kpT[0][:, :, cols], banks[:, 7, 0:2 * P].rearrange("p (a c) -> p a c", a=2), ACT.Copy)
                        act.activation(ikT[0][:, cols], banks[:, 7, 2 * P:3 * P], ACT.Copy).then_inc(nhi_ok.sem, nhi_ok.step)
                for j in range(2):
                    behind = in_register(act, xn_out[j].at(b * (NT // 2) + NT // 2 - 1))
                    act.wait_ge(xn_out[j].sem, xn_out[j].step)
                    act.wait_ge(xn_out[j].sem, behind)
                barrier(act, 0, b)

                def index_queries(q, u):
                    for c in range(2):
                        act.wait_ge(iy_ok.sem, iy_ok.at(q * 2 + c))
                        act.activation(iqT[0][:, u, c * 512:c * 512 + 512], iy[:, c, :], ACT.Copy).then_inc(iqhi_ok.sem, iqhi_ok.step)

                act.wait_ge(wi_in[0].sem, wi_in[0].at(b * (PAIRS + 1)))
                act.activation(wi[0][:, 0], wi_raw[:, 0], ACT.Copy).then_inc(wi_hi_ok.sem, wi_hi_ok.step)
                index_queries(b * (H + 1), 0)
                with act.Fori(0, PAIRS) as hp:
                    for u in range(2):
                        h, v = hp * 2 + u, 1 - u
                        q = b * (H + 1) + h + 1
                        act.wait_ge(wi_in[v].sem, wi_in[v].at(b * PAIRS + hp if u == 0 else b * (PAIRS + 1) + hp + 1))
                        act.wait_ge(iq_full.sem, iq_full.at(q * 2 + 1, 4))
                        act.activation(wi[0][:, v], wi_raw[:, v], ACT.Copy).then_inc(wi_hi_ok.sem, wi_hi_ok.step)
                        act.wait_ge(is_full.sem, is_full.at((b * H + h) * (NT - 1), 1))
                        index_queries(q, v)
                        for i in range(1, NT):
                            n = (b * H + h) * (NT - 1) + i - 1
                            r = (u * (NT - 1) + i - 1) % 2
                            act.wait_ge(is_full.sem, is_full.at(n))
                            act.wait_ge(acc_ok.sem, acc_ok.at(n, 2))
                            act.activation(relu[:, r, 0:EXT[i]], scores_psum(r, EXT[i]), ACT.Relu).then_inc(relu_ok.sem, relu_ok.step)
                barrier(act, 1, b)

                act.wait_ge(wp_in.sem, wp_in.at(b * (PAIRS + 1)))
                act.activation(wp[0][:], wp_raw[:], ACT.Copy).then_inc(wp_hi_ok.sem, wp_hi_ok.step)
                act.wait_ge(wh_in[0].sem, wh_in[0].at(b * (PAIRS + 1)))
                act.activation(wh[0][:, 0], wh_raw[:, 0], ACT.Copy).then_inc(wh_hi_ok.sem, wh_hi_ok.step)
                with act.Fori(0, PAIRS) as hp:
                    pp = b * PAIRS + hp
                    for c in range(NPE):
                        act.wait_ge(py_ok.sem, py_ok.at(pp * 2 + c))
                        act.activation(qp[0][:, c * 512:c * 512 + 512], py[:, c, :], ACT.Copy).then_inc(qphi_ok.sem, qphi_ok.step)
                    for u in range(2):
                        hh = pp * 2 + u
                        g0 = NPE + u * (NPR + NTP)
                        for c in range(NPR):
                            dst, src = projection(c, 0), banks[:, 4 + (g0 + c) % 2, :]
                            if c >= 4:
                                src = src.rearrange("p (t d) -> p t d", t=4)
                            act.wait_ge(sh_full.sem, sh_full.at(pp * SHARED + g0 + c))
                            act.activation(dst, src, ACT.Copy).then_inc(sh_hi.sem, sh_hi.step)

                        def exponentials(i):
                            act.wait_ge(masked.sem, masked.at(hh * NT + i))
                            a = probs[:, OFF[i]:OFF[i + 1]]
                            act.activation(a, a, ACT.Exp, bias=nmax[:, i:i + 1], scale=-1.0,
                                                    accum_out=row_sum[:, i:i + 1]).then_inc(exps.sem, exps.step)

                        def block_hi(jj, lo):
                            act.wait_ge(sh_full.sem, sh_full.at(pp * SHARED + g0 + NPR + jj))
                            act.wait_ge(pv_done.sem, pv_done.at(hh * NTP + jj, 2))
                            act.activation(PT[0][:, jj % 2, lo:512], banks[:, 4 + (g0 + NPR + jj) % 2, lo:512], ACT.Copy).then_inc(sh_hi.sem, sh_hi.step)

                        def out_rows(s):
                            act.wait_ge(pv_done.sem, pv_done.at(hh * NTP + 4 + 8 * s - 1))
                            act.wait_ge(oT_out[s].sem, oT_out[s].at(hh, 1))
                            act.activation(oT[:, s, :], banks[:, 6 + s, :], ACT.Copy).then_inc(oT_read.sem, oT_read.step)

                        for i in range(6):
                            exponentials(i)
                        for kt in range(4):
                            block_hi(kt, kt * P)
                        exponentials(6)
                        out_rows(0)
                        exponentials(7)
                        for kt in range(NT):
                            block_hi(4 + kt, max(0, kt - 4) * P)
                            if kt == 3:
                                act.wait_ge(wh_in[1 - u].sem, wh_in[1 - u].at(b * PAIRS + hp if u == 0 else b * (PAIRS + 1) + hp + 1))
                                act.activation(wh[0][:, 1 - u], wh_raw[:, 1 - u], ACT.Copy).then_inc(wh_hi_ok.sem, wh_hi_ok.step)
                                if u == 1:
                                    act.wait_ge(wp_in.sem, wp_in.at(b * (PAIRS + 1) + hp + 1))
                                    act.activation(wp[0][:], wp_raw[:], ACT.Copy).then_inc(wp_hi_ok.sem, wp_hi_ok.step)
                        out_rows(1)
                barrier(act, 2, b)

                with act.Fori(0, H // 2) as hp:
                    for j in range(2):
                        n = b * H + hp * 2 + j
                        act.wait_ge(o_in[j].sem, o_in[j].at(b * (H // 2) + hp))
                        act.wait_ge(o_mm.sem, o_mm.at(n, 2))
                        act.activation(oTr[0][:, j, :], oT_raw[:, j, :], ACT.Copy).then_inc(ohi_ok.sem, ohi_ok.step)
                        act.wait_ge(ow_in[j].sem, ow_in[j].at(b * (H // 2) + hp))
                        act.activation(ow[0][:, j, :], ow_raw[:, j, :], ACT.Copy).then_inc(owhi_ok.sem, owhi_ok.step)
                with act.Fori(0, NT // 2) as it:
                    for j in range(2):
                        n = b * NT + it * 2 + j
                        act.wait_ge(po_ok.sem, po_ok.at(n))
                        act.dma_start(part_d[n], po[:, j, :]).then_inc(part_out[j].sem, part_out[j].step)
                for j in range(2):
                    behind = in_register(act, part_out[j].at(b * (NT // 2) + NT // 2 - 1))
                    act.wait_ge(part_out[j].sem, part_out[j].step)
                    act.wait_ge(part_out[j].sem, behind)
                barrier(act, 3, b)

            act.wait_ge(rt.sem, rt.at(RT_SHIFTED))
            act.activation(r_e[:], r_e[:], ACT.Exp).then_inc(rt_exp.sem, rt_exp.step)
            barrier(act, 0)

            def up_hi(c, r, q, k_in):
                act.wait_ge(we_in[r].sem, we_in[r].at(k_in))
                act.activation(wgu[0][:, q, :], we[:, r, 0:2 * D], ACT.Copy).then_inc(wguhi_ok.sem, wguhi_ok.step)

            up_hi(0, 0, 0, 0)
            up_hi(1, 1, 1, 0)
            act.activation(wdn[0][:, 0, :], we[:, 0, 2 * D:], ACT.Copy).then_inc(wdnhi_ok.sem, wdnhi_ok.step)
            with act.Fori(0, NBLK) as k:
                for a in range(2):
                    act.wait_ge(xeT_full.sem, xeT_full.at(k * 2 + a))
                    act.activation(xeT[0][:, :, a * P:a * P + P],
                                               banks[:, a, :].rearrange("p (k t) -> p k t", k=KD), ACT.Copy).then_inc(xehi_ok.sem, xehi_ok.step)
                for m in range(KM):
                    c, q = k * KM + m, m % 2
                    act.wait_ge(gu_full.sem, gu_full.at(c))
                    act.activation(sg[:, q, :], banks[:, 2 + q, 0:BLK], ACT.Silu).then_inc(silu_ok.sem, silu_ok.step)
                    r = (m + 2) % NWR
                    act.wait_ge(we_in[r].sem, we_in[r].at(k * (KM // NWR) + (m + 2) // NWR))
                    act.activation(wgu[0][:, q, :], we[:, r, 0:2 * D], ACT.Copy).then_inc(wguhi_ok.sem, wguhi_ok.step)
                    act.wait_ge(h_ok.sem, h_ok.at(c))
                    act.activation(hT[0][:, q, :], hf[:, q, :], ACT.Copy).then_inc(hhi_ok.sem, hhi_ok.step)
                    act.wait_ge(down.sem, down.at(c, 1))
                    act.activation(wdn[0][:, 1 - q, :], we[:, (m + 1) % NWR, 2 * D:], ACT.Copy).then_inc(wdnhi_ok.sem, wdnhi_ok.step)
                act.wait_ge(down.sem, down.at(k * KM + KM - 1))
                act.wait_ge(ye_out.sem, ye_out.at(k, 1))
                act.activation(ye[:], banks[:, 6:8, :], ACT.Copy).then_inc(ye_ok.sem, ye_ok.step)
                act.wait_ge(ye_ok.sem, ye_ok.at(k))
                act.dma_start(ys_blk[k], ye[:]).then_inc(ye_out.sem, ye_out.step)
            act.wait_ge(ye_out.sem, ye_out.at(NBLK - 1))
            barrier(act, 1)
            with act.Fori(0, B * NT // 2) as it:
                for j in range(2):
                    act.wait_ge(fin_ok.sem, fin_ok.at(it * 2 + j))
                    act.dma_start(out_t[it * 2 + j], fin[:, j, :]).then_inc(fin_out[j].sem, fin_out[j].step)
            for j in range(2):
                act.wait_ge(fin_out[j].sem, fin_out[j].at(B * NT // 2 - 1))

        @block.vector
        def _(dve):
            for e in evs["dve"]:
                if e.credit:
                    dve.sem_inc(e.sem, e.credit * e.step)
            dve.memset(eps_ln[:], EPS_LN)
            dve.memset(eps_rms[:], EPS_RMS).then_inc(eps_ok.sem, eps_ok.step)
            dve.wait_ge(consts.sem, consts.at(len(const_tiles) - 1))
            with dve.Fori(0, B) as b:
                with dve.Fori(0, NT // 2) as it:
                    for j in range(2):
                        n = b * NT + it * 2 + j
                        dve.wait_ge(x_in[j].sem, x_in[j].at(b * (NT // 2) + it))
                        dve.bn_stats(ln_st[:, j, :], x_sb[:, j, :]).then_inc(stats.sem, stats.step)
                        behind = in_register(dve, stats.at(n))
                        dve.wait_ge(stats.sem, stats.step)
                        dve.wait_ge(stats.sem, behind)
                        dve.bn_aggr(ln_mv[:, j, :], ln_st[:, j, :]).then_inc(moments.sem, moments.step)
                        dve.wait_ge(deviation.sem, deviation.at(n))
                        dve.reciprocal(ln_r[:, j, :], ln_sd[:, j, :]).then_inc(inverse.sem, inverse.step)
                        dve.wait_ge(inverse.sem, inverse.at(n))
                        dve.wait_ge(xt_full.sem, xt_full.at(n, 2))
                        dve.wait_ge(xn_out[j].sem, xn_out[j].at(b * (NT // 2) + it, 1))
                        dve.tensor_scalar(xn[:, j, :], x_sb[:, j, :], ln_mv[:, j, 0:1], ln_r[:, j, 0:1],
                                                     ALU.subtract, ALU.mult).then_inc(normed.sem, normed.step)
                    for j in range(2):
                        n = b * NT + it * 2 + j
                        dve.wait_ge(xhi_ok.sem, xhi_ok.at(n))
                        dve.tensor_tensor(xT[1][:, j, :], banks[:, j, :], plain(xT[0][:, j, :]), ALU.subtract).then_inc(xlo_ok.sem, xlo_ok.step)
                    for j in range(2):
                        n = b * NT + it * 2 + j
                        dve.wait_ge(projected.sem, projected.at(n))
                        dve.wait_ge(natk_ok.sem, natk_ok.at(n, 2))
                        dve.tensor_copy(bs[:, j, :], banks[:, 3 + 2 * j, 0:NB]).then_inc(copied.sem, copied.step)
                        dve.wait_ge(copied.sem, copied.at(n))
                        dve.bn_stats(ik_st[:, j, :], bs[:, j, CIK - QR:CIW - QR]).then_inc(ik_stats.sem, ik_stats.step)
                        behind = in_register(dve, ik_stats.at(n))
                        dve.wait_ge(ik_stats.sem, ik_stats.step)
                        dve.wait_ge(ik_stats.sem, behind)
                        dve.bn_aggr(ik_mv[:, j, :], ik_st[:, j, :]).then_inc(ik_moments.sem, ik_moments.step)
                        dve.tensor_scalar(iw[:, bass.ds(it * 2 + j, 1), :], bs[:, j:j + 1, CIW - QR:CLG - QR], float(H) ** -0.5, None, ALU.mult)
                        dve.tensor_copy(logits[:, bass.ds(n, 1), :], bs[:, j:j + 1, CLG - QR:NB])
                        dve.wait_ge(roots.sem, roots.at(n))
                        dve.reciprocal(r3[:, j, :], sd3[:, j, :]).then_inc(inverses.sem, inverses.step)
                        dve.wait_ge(inverses.sem, inverses.at(n))
                        dve.wait_ge(nt_full.sem, nt_full.at(n, 2))
                        dve.tensor_scalar(nat_q[:, j, 0:QR], banks[:, 2 + 2 * j, 0:QR], r3[:, j, 0:1], None, ALU.mult)
                        dve.tensor_scalar(nat_q[:, j, QR:], bs[:, j, 0:KVR], r3[:, j, 1:2], None, ALU.mult).then_inc(natq_ok.sem, natq_ok.step)
                    for j in range(2):
                        n = b * NT + it * 2 + j
                        cols = bass.ds((it * 2 + j) * P, P)
                        dve.wait_ge(nhi_ok.sem, nhi_ok.at(n))
                        for c in range(KQ):
                            dve.scalar_tensor_tensor(qrT[1][:, c, cols], banks[:, 6, c * P:c * P + P], q_ln[:, c:c + 1],
                                                     plain(qrT[0][:, c, cols]), ALU.mult, ALU.subtract)
                        dve.scalar_tensor_tensor(ckvT[1][:, cols], banks[:, 6, QR:QR + KVR], kv_ln[:, 0:1],
                                                 plain(ckvT[0][:, cols]), ALU.mult, ALU.subtract)
                        dve.tensor_tensor(kpT[1][:, :, cols], banks[:, 7, 0:2 * P].rearrange("p (a c) -> p a c", a=2),
                                          plain(kpT[0][:, :, cols]), ALU.subtract)
                        dve.tensor_tensor(ikT[1][:, cols], banks[:, 7, 2 * P:3 * P], plain(ikT[0][:, cols]), ALU.subtract).then_inc(nlo_ok.sem, nlo_ok.step)
                barrier(dve, 0, b)

                dve.memset(turned[:], 0.0)
                dve.memset(acc[:], 0.0).then_inc(acc_clear.sem, acc_clear.step)
                behind = in_register(dve, acc_clear.at(b))
                dve.wait_ge(acc_clear.sem, acc_clear.step)
                dve.wait_ge(acc_clear.sem, behind)

                def index_queries(q):
                    for c in range(2):
                        g, tok = q * 2 + c, slice(c * 512, c * 512 + 512)
                        dve.wait_ge(iq_full.sem, iq_full.at(g))
                        dve.wait_ge(iy_ok.sem, iy_ok.at(g, 1))
                        dve.tensor_tensor(scaled[:], banks[:, 4 + c, :], idx_c[:, tok], ALU.mult)
                        dve.tensor_tensor(turned[0:32, :], banks[64:96, 4 + c, :], rope_s[64:96, tok], ALU.mult)
                        dve.tensor_tensor(turned[64:96, :], banks[0:32, 4 + c, :], rope_s[0:32, tok], ALU.mult).then_inc(i_parts.sem, i_parts.step)
                        dve.wait_ge(i_parts.sem, i_parts.at(g))
                        dve.wait_ge(iqlo_ok.sem, iqlo_ok.at(g, 2))
                        dve.tensor_tensor(iy[:, c, :], scaled[:], turned[:], ALU.add).then_inc(iy_ok.sem, iy_ok.step)

                index_queries(b * (H + 1))
                with dve.Fori(0, PAIRS) as hp:
                    for u in range(2):
                        h = hp * 2 + u
                        index_queries(b * (H + 1) + h + 1)
                        for i in range(1, NT):
                            n = (b * H + h) * (NT - 1) + i - 1
                            r = (u * (NT - 1) + i - 1) % 2
                            a = acc[:, OFF[i]:OFF[i + 1]]
                            dve.wait_ge(relu_ok.sem, relu_ok.at(n))
                            dve.scalar_tensor_tensor(a, relu[:, r, 0:EXT[i]], iw[:, i, bass.ds(h, 1)], a, ALU.mult, ALU.add).then_inc(acc_ok.sem, acc_ok.step)
                dve.wait_ge(acc_ok.sem, acc_ok.at((b + 1) * H * (NT - 1) - 1))
                for i in range(1, NT):
                    n = b * (NT - 1) + i - 1
                    a = acc[:, OFF[i]:OFF[i + 1]]
                    diag = acc[:, OFF[i + 1] - P:OFF[i + 1]]
                    dve.tensor_tensor(diag, diag, causal[:], ALU.add).then_inc(diag_ok.sem, diag_ok.step)
                    behind = in_register(dve, diag_ok.at(n))
                    dve.wait_ge(diag_ok.sem, diag_ok.step)
                    dve.wait_ge(diag_ok.sem, behind)
                    with dve.Fori(0, TOPK // 8) as k:
                        behind = in_register(dve, taken_ok.at(n * (TOPK // 8) + k, 1))
                        dve.wait_ge(taken_ok.sem, taken_ok.step)
                        dve.wait_ge(taken_ok.sem, behind)
                        dve.max(m8[:], a).then_inc(top8_ok.sem, top8_ok.step)
                        behind = in_register(dve, top8_ok.at(n * (TOPK // 8) + k))
                        dve.wait_ge(top8_ok.sem, top8_ok.step)
                        dve.wait_ge(top8_ok.sem, behind)
                        dve.match_replace(a, m8[:], a, TAKEN).then_inc(taken_ok.sem, taken_ok.step)
                    dve.wait_ge(taken_ok.sem, taken_ok.at(n * (TOPK // 8) + TOPK // 8 - 1))
                    dve.tensor_scalar(a, a, TAKEN, MASKED, ALU.not_equal, ALU.mult)
                dve.tensor_copy(acc[:, 0:P], causal[:]).then_inc(mask_ok.sem, mask_ok.step)
                barrier(dve, 1, b)

                with dve.Fori(0, PAIRS) as hp:
                    pp = b * PAIRS + hp
                    for c in range(NPE):
                        g, tok = pp * 2 + c, slice(c * 512, c * 512 + 512)
                        dve.wait_ge(sh_full.sem, sh_full.at(pp * SHARED + c))
                        dve.wait_ge(py_ok.sem, py_ok.at(g, 1))
                        dve.tensor_tensor(p_scaled[:], banks[:, 4 + c, :], rope_c[:, tok], ALU.mult)
                        dve.tensor_tensor(p_turned[0:64, :], banks[64:128, 4 + c, :], rope_s[64:128, tok], ALU.mult)
                        dve.tensor_tensor(p_turned[64:128, :], banks[0:64, 4 + c, :], rope_s[0:64, tok], ALU.mult).then_inc(sh_read.sem, sh_read.step)
                        dve.wait_ge(sh_read.sem, sh_read.at(pp * SHARED + c))
                        dve.wait_ge(qplo_ok.sem, qplo_ok.at(g, 2))
                        dve.tensor_tensor(py[:, c, :], p_scaled[:], p_turned[:], ALU.add).then_inc(py_ok.sem, py_ok.step)
                    for u in range(2):
                        hh = pp * 2 + u
                        g0 = NPE + u * (NPR + NTP)
                        for c in range(NPR):
                            dst, src, hi = projection(c, 1), banks[:, 4 + (g0 + c) % 2, :], projection(c, 0)
                            if c >= 4:
                                src = src.rearrange("p (t d) -> p t d", t=4)
                            dve.wait_ge(sh_hi.sem, sh_hi.at(pp * (SHARED - NPE) + g0 - NPE + c))
                            dve.tensor_tensor(dst, src, plain(hi), ALU.subtract).then_inc(sh_read.sem, sh_read.step)

                        def mask_and_max(i):
                            behind = in_register(dve, sc_full.at(hh * NT + i))
                            dve.wait_ge(sc_full.sem, sc_full.step)
                            dve.wait_ge(sc_full.sem, behind)
                            dve.tensor_tensor_reduce(probs[:, OFF[i]:OFF[i + 1]], scores_psum(i % 2, EXT[i]),
                                                                acc[:, OFF[i]:OFF[i + 1]], -SCALE, 3.0e38, ALU.add, ALU.min,
                                                                nmax[:, i:i + 1]).then_inc(masked.sem, masked.step)

                        def invert(i):
                            dve.wait_ge(exps.sem, exps.at(hh * NT + i))
                            dve.reciprocal(rinv[:, i:i + 1], row_sum[:, i:i + 1]).then_inc(sums_inv.sem, sums_inv.step)

                        def block_lo(jj, lo):
                            dve.wait_ge(sh_hi.sem, sh_hi.at(pp * (SHARED - NPE) + g0 - NPE + NPR + jj))
                            dve.tensor_tensor(PT[1][:, jj % 2, lo:512], banks[:, 4 + (g0 + NPR + jj) % 2, lo:512],
                                                          plain(PT[0][:, jj % 2, lo:512]), ALU.subtract).then_inc(sh_read.sem, sh_read.step)

                        mask_and_max(0)
                        for i in range(1, 6):
                            mask_and_max(i)
                            invert(i - 1)
                        for kt in range(4):
                            block_lo(kt, kt * P)
                        mask_and_max(6)
                        invert(5)
                        mask_and_max(7)
                        invert(6)
                        invert(7)
                        for kt in range(NT):
                            block_lo(4 + kt, max(0, kt - 4) * P)
                barrier(dve, 2, b)

                with dve.Fori(0, H // 2) as hp:
                    for j in range(2):
                        n = b * H + hp * 2 + j
                        dve.wait_ge(ohi_ok.sem, ohi_ok.at(n))
                        dve.tensor_tensor(oTr[1][:, j, :], oT_raw[:, j, :], plain(oTr[0][:, j, :]), ALU.subtract).then_inc(olo_ok.sem, olo_ok.step)
                behind = in_register(dve, o_mm.at(b * H + H - 1))
                dve.wait_ge(o_mm.sem, o_mm.step)
                dve.wait_ge(o_mm.sem, behind)
                with dve.Fori(0, NT // 2) as it:
                    for j in range(2):
                        dve.wait_ge(xo_in[j].sem, xo_in[j].at(b * (NT // 2) + it))
                        dve.wait_ge(part_out[j].sem, part_out[j].at(b * (NT // 2) + it, 1))
                        dve.tensor_tensor(po[:, j, :], banks[:, bass.ds(it * 2 + j, 1), :].rearrange("p a c -> p (a c)"), xo[:, j, :], ALU.add).then_inc(po_ok.sem, po_ok.step)
                barrier(dve, 3, b)

            step = [0]

            def link(ins):
                step[0] += 1
                ins.then_inc(rt.sem, 1)
                dve.wait_ge(rt.sem, step[0])

            def over(ap, shape):
                return ap.broadcast_to(shape)

            NTT = B * NT
            full = [P, NTT, NE]
            link(dve.tensor_reduce(r_t[:], logits[:], AX.X, ALU.max))
            link(dve.tensor_tensor(r_e[:], logits[:], over(r_t[:].unsqueeze(2), full), ALU.subtract))
            assert step[0] == RT_SHIFTED + 1
            dve.wait_ge(rt_exp.sem, rt_exp.at(0))
            link(dve.tensor_reduce(r_t[:], r_e[:], AX.X, ALU.add))
            link(dve.reciprocal(r_t[:], r_t[:]))
            link(dve.tensor_tensor(r_e[:], r_e[:], over(r_t[:].unsqueeze(2), full), ALU.mult))
            for n in range(NTT):
                last = dve.max(r_m[:, n, :], r_e[:, n, :])
            link(last)
            for n in range(NTT):
                last = dve.max_index(r_i[:, n, :], r_m[:, n, :], r_e[:, n, :])
            link(last)
            link(dve.tensor_tensor(r_t[:], r_m[:, :, 0], r_m[:, :, 1], ALU.add))
            link(dve.reciprocal(r_t[:], r_t[:]))
            for k in range(2):
                link(dve.tensor_tensor(gates[:, k, :], r_m[:, :, k], r_t[:], ALU.mult))
            link(dve.tensor_copy(r_if[:], r_i[:]))
            dve.wait_ge(rt_pool.sem, rt_pool.at(0))
            for k in range(2):
                link(dve.tensor_tensor(r_oh[:, k], over(iota8[:].unsqueeze(1), full), over(r_if[:, :, k:k + 1], full), ALU.is_equal))
            link(dve.tensor_tensor(r_mk[:], r_oh[:, 0], r_oh[:, 1], ALU.add))
            assert step[0] == RT_MARKED + 1
            dve.wait_ge(rt_pe.sem, rt_pe.at(0))
            link(dve.tensor_copy(r_a[:], banks[:, 1, 0:NTT * NE].rearrange("p (n e) -> p n e", e=NE)))
            src, dst, w = r_a, r_b, 1
            while w < NTT:
                link(dve.tensor_copy(dst[:, 0:w, :], src[:, 0:w, :]))
                link(dve.tensor_tensor(dst[:, w:, :], src[:, w:, :], src[:, 0:NTT - w, :], ALU.add))
                src, dst, w = dst, src, 2 * w
            link(dve.tensor_tensor(r_cnt[:], over(src[:, NTT - 1, :].unsqueeze(2), [P, NE, NE]), over(lim8[:].unsqueeze(1), [P, NE, NE]), ALU.is_gt))
            link(dve.tensor_reduce(r_n[:, 0, :], r_cnt[:], AX.X, ALU.add))
            link(dve.tensor_copy(r_n[:, 1, :], r_n[:, 0, :]))
            at, to, w = 1, 2, 1
            while w < NE:
                link(dve.tensor_copy(r_n[:, to, 0:w], r_n[:, at, 0:w]))
                link(dve.tensor_tensor(r_n[:, to, w:], r_n[:, at, w:], r_n[:, at, 0:NE - w], ALU.add))
                at, to, w = to, at, 2 * w
            link(dve.tensor_tensor(r_ow[:], over(iotab[:].unsqueeze(2), [P, NBLK, NE]), over(r_n[:, at, :].unsqueeze(1), [P, NBLK, NE]), ALU.is_ge))
            link(dve.tensor_reduce(r_of[:], r_ow[:], AX.X, ALU.add))
            link(dve.tensor_scalar(r_of[:], r_of[:], float(NE - 1), None, ALU.min))
            link(dve.tensor_copy(owner[:], r_of[0:1, :]))
            link(dve.tensor_tensor(r_n[:, to, :], r_n[:, at, :], r_n[:, 0, :], ALU.subtract))
            link(dve.tensor_scalar(r_n[:, to, :], r_n[:, to, :], float(BLK), None, ALU.mult))
            link(dve.tensor_tensor(dst[:], banks[:, 0, 0:NTT * NE].rearrange("p (n e) -> p n e", e=NE), over(r_n[:, to, :].unsqueeze(1), full), ALU.add))
            link(dve.tensor_tensor(dst[:, 1:, :], dst[:, 1:, :], src[:, 0:NTT - 1, :], ALU.add))
            for k in range(2):
                link(dve.tensor_tensor(r_mk[:], r_oh[:, k], dst[:], ALU.mult))
                link(dve.tensor_reduce(r_sl[:, k, :], r_mk[:], AX.X, ALU.add))
            link(dve.tensor_copy(slots[:], r_sl[:]))
            dve.tensor_copy(r_t[:], r_m[:, :, 0]).then_inc(slots_ok.sem, slots_ok.step)
            barrier(dve, 0)

            def up_lo(c, r, q):
                dve.wait_ge(wguhi_ok.sem, wguhi_ok.at(c))
                dve.tensor_tensor(wgu[1][:, q, :], we[:, r, 0:2 * D], plain(wgu[0][:, q, :]), ALU.subtract).then_inc(wgulo_ok.sem, wgulo_ok.step)

            up_lo(0, 0, 0)
            up_lo(1, 1, 1)
            with dve.Fori(0, NBLK) as k:
                for a in range(2):
                    dve.wait_ge(xehi_ok.sem, xehi_ok.at(k * 2 + a))
                    dve.tensor_tensor(xeT[1][:, :, a * P:a * P + P], banks[:, a, :].rearrange("p (k t) -> p k t", k=KD),
                                                  plain(xeT[0][:, :, a * P:a * P + P]), ALU.subtract).then_inc(xelo_ok.sem, xelo_ok.step)
                for m in range(KM):
                    c, q = k * KM + m, m % 2
                    dve.wait_ge(silu_ok.sem, silu_ok.at(c))
                    dve.wait_ge(hlo_ok.sem, hlo_ok.at(c, 2))
                    dve.tensor_tensor(hf[:, q, :], banks[:, 2 + q, BLK:2 * BLK], sg[:, q, :], ALU.mult).then_inc(h_ok.sem, h_ok.step)
                    up_lo(c + 2, (m + 2) % NWR, q)
            barrier(dve, 1)

            with dve.Fori(0, B * NT // 2) as it:
                for j in range(2):
                    n = it * 2 + j
                    dve.wait_ge(part_in[j].sem, part_in[j].at(it))
                    dve.wait_ge(g_in[j].sem, g_in[j].at(it * 2 + 1))
                    dve.scalar_tensor_tensor(mix[:, j, :], g_a[:, j, :], gates[:, 0, bass.ds(n, 1)], part_sb[:, j, :], ALU.mult, ALU.add).then_inc(mix_ok.sem, mix_ok.step)
                    dve.wait_ge(mix_ok.sem, mix_ok.at(n))
                    dve.wait_ge(fin_out[j].sem, fin_out[j].at(it, 1))
                    dve.scalar_tensor_tensor(fin[:, j, :], g_b[:, j, :], gates[:, 1, bass.ds(n, 1)], mix[:, j, :], ALU.mult, ALU.add).then_inc(fin_ok.sem, fin_ok.step)

        @block.gpsimd
        def _(pool):
            for e in evs["pool"]:
                if e.credit:
                    pool.sem_inc(e.sem, e.credit * e.step)
            pool.wait_ge(consts.sem, consts.at(len(const_tiles) - 1))
            with pool.Fori(0, B) as b:
                pool.memset(nat_k[:], 0.0).then_inc(nat_clear.sem, nat_clear.step)
                pool.wait_ge(nat_clear.sem, nat_clear.at(b))
                pool.wait_ge(wa_hi_ok.sem, wa_hi_ok.at(b))
                pool.tensor_tensor(wa[1][:], wa_raw[:], plain(wa[0][:]), ALU.subtract).then_inc(wa_lo_ok.sem, wa_lo_ok.step)
                with pool.Fori(0, NT // 2) as it:
                    for j in range(2):
                        n = b * NT + it * 2 + j
                        both = [P, 2, HALF]
                        cos = nat_c[:, bass.ds(it * 2 + j, 1), :].broadcast_to(both)
                        sin = nat_s[:, bass.ds(it * 2 + j, 1), :].broadcast_to(both)
                        kp = bs[:, j, CKP - QR:CIK - QR].rearrange("p (a c) -> p a c", a=2)
                        behind = in_register(pool, inverses.at(n))
                        pool.wait_ge(inverses.sem, inverses.step)
                        pool.wait_ge(inverses.sem, behind)
                        behind = in_register(pool, natk_ok.at(n, 1))
                        pool.wait_ge(natk_ok.sem, natk_ok.step)
                        pool.wait_ge(natk_ok.sem, behind)
                        behind = in_register(pool, nt_full.at(n, 2))
                        pool.wait_ge(nt_full.sem, nt_full.step)
                        pool.wait_ge(nt_full.sem, behind)
                        pool.tensor_scalar(ikn[:], bs[:, j, CIK - QR:CIW - QR], ik_mv[:, j, 0:1], r3[:, j, 2:3],
                                                           ALU.subtract, ALU.mult).then_inc(key_step[0].sem, key_step[0].step)
                        pool.tensor_tensor(rk1[:], kp, cos, ALU.mult)
                        pool.tensor_tensor(rk2[:], kp, sin, ALU.mult).then_inc(key_step[1].sem, key_step[1].step)
                        pool.wait_ge(key_step[0].sem, key_step[0].at(n))
                        pool.tensor_tensor(ikn[:], ikn[:], kn_w[:], ALU.mult).then_inc(key_step[2].sem, key_step[2].step)
                        pool.wait_ge(key_step[1].sem, key_step[1].at(n))
                        for odd in range(2):
                            o = HALF * odd
                            pool.tensor_tensor(nat_k[:, j, odd, o:o + HALF], rk1[:, 0, :], rk2[:, 1, :], ALU.subtract)
                            pool.tensor_tensor(nat_k[:, j, odd, 64 + o:64 + o + HALF], rk1[:, 1, :], rk2[:, 0, :], ALU.add)
                        pool.wait_ge(key_step[2].sem, key_step[2].at(n))
                        pool.tensor_tensor(ikn[:], ikn[:], kn_b[:], ALU.add).then_inc(key_step[3].sem, key_step[3].step)
                        behind = in_register(pool, key_step[3].at(n))
                        pool.wait_ge(key_step[3].sem, key_step[3].step)
                        pool.wait_ge(key_step[3].sem, behind)
                        rot = ikn[:, 0:ROPE].rearrange("p (a c) -> p a c", a=2)
                        pool.tensor_tensor(ri1[:], rot, cos, ALU.mult)
                        pool.tensor_tensor(ri2[:], rot, sin, ALU.mult).then_inc(key_step[4].sem, key_step[4].step)
                        pool.tensor_copy(nat_k[:, j, 2, HALF:2 * HALF], ikn[:, ROPE:ROPE + HALF])
                        pool.tensor_copy(nat_k[:, j, 2, 3 * HALF:], ikn[:, ROPE + HALF:])
                        pool.wait_ge(key_step[4].sem, key_step[4].at(n))
                        pool.tensor_tensor(nat_k[:, j, 2, 0:HALF], ri1[:, 0, :], ri2[:, 1, :], ALU.subtract)
                        pool.tensor_tensor(nat_k[:, j, 2, 2 * HALF:3 * HALF], ri1[:, 1, :], ri2[:, 0, :], ALU.add).then_inc(natk_ok.sem, natk_ok.step)
                barrier(pool, 0, b)

                def index_part(q, u):
                    pool.wait_ge(wi_hi_ok.sem, wi_hi_ok.at(q))
                    pool.tensor_tensor(wi[1][:, u], wi_raw[:, u], plain(wi[0][:, u]), ALU.subtract).then_inc(wi_lo_ok.sem, wi_lo_ok.step)
                    for c in range(2):
                        tok = slice(c * 512, c * 512 + 512)
                        pool.wait_ge(iqhi_ok.sem, iqhi_ok.at(q * 2 + c))
                        pool.tensor_tensor(iqT[1][:, u, tok], iy[:, c, :], plain(iqT[0][:, u, tok]), ALU.subtract).then_inc(iqlo_ok.sem, iqlo_ok.step)

                index_part(b * (H + 1), 0)
                with pool.Fori(0, PAIRS) as hp:
                    for u in range(2):
                        index_part(b * (H + 1) + hp * 2 + u + 1, 1 - u)
                barrier(pool, 1, b)

                pool.wait_ge(wp_hi_ok.sem, wp_hi_ok.at(b * (PAIRS + 1)))
                pool.tensor_tensor(wp[1][:], wp_raw[:], plain(wp[0][:]), ALU.subtract).then_inc(wp_lo_ok.sem, wp_lo_ok.step)
                pool.wait_ge(wh_hi_ok.sem, wh_hi_ok.at(b * (H + 1)))
                pool.tensor_tensor(wh[1][:, 0], wh_raw[:, 0], plain(wh[0][:, 0]), ALU.subtract).then_inc(wh_lo_ok.sem, wh_lo_ok.step)
                with pool.Fori(0, PAIRS) as hp:
                    pp = b * PAIRS + hp
                    for c in range(NPE):
                        tok = slice(c * 512, c * 512 + 512)
                        pool.wait_ge(qphi_ok.sem, qphi_ok.at(pp * 2 + c))
                        pool.tensor_tensor(qp[1][:, tok], py[:, c, :], plain(qp[0][:, tok]), ALU.subtract).then_inc(qplo_ok.sem, qplo_ok.step)
                    for u in range(2):
                        hh = pp * 2 + u
                        for i in range(NT):
                            a = probs[:, OFF[i]:OFF[i + 1]]
                            behind = in_register(pool, sums_inv.at(hh * NT + i))
                            pool.wait_ge(sums_inv.sem, sums_inv.step)
                            pool.wait_ge(sums_inv.sem, behind)
                            pool.tensor_scalar(a, a, rinv[:, i:i + 1], None, ALU.mult).then_inc(p_norm.sem, p_norm.step)
                        pool.wait_ge(wh_hi_ok.sem, wh_hi_ok.at(b * (H + 1) + hp * 2 + u + 1))
                        pool.tensor_tensor(wh[1][:, 1 - u], wh_raw[:, 1 - u], plain(wh[0][:, 1 - u]), ALU.subtract).then_inc(wh_lo_ok.sem, wh_lo_ok.step)
                    pool.wait_ge(wp_hi_ok.sem, wp_hi_ok.at(b * (PAIRS + 1) + hp + 1))
                    pool.tensor_tensor(wp[1][:], wp_raw[:], plain(wp[0][:]), ALU.subtract).then_inc(wp_lo_ok.sem, wp_lo_ok.step)
                barrier(pool, 2, b)

                with pool.Fori(0, H // 2) as hp:
                    for j in range(2):
                        n = b * H + hp * 2 + j
                        pool.wait_ge(owhi_ok.sem, owhi_ok.at(n))
                        pool.tensor_tensor(ow[1][:, j, :], ow_raw[:, j, :], plain(ow[0][:, j, :]), ALU.subtract).then_inc(owlo_ok.sem, owlo_ok.step)
                barrier(pool, 3, b)

            pool.memset(zero[:], 0.0).then_inc(zero_ok.sem, zero_ok.step)
            pool.iota(iota8[:], [[1, NE]], base=0, channel_multiplier=0, allow_small_or_imprecise_dtypes=True)
            pool.iota(lim8[:], [[BLK, NE]], base=0, channel_multiplier=0, allow_small_or_imprecise_dtypes=True)
            pool.iota(iotab[:], [[1, NBLK]], base=0, channel_multiplier=0, allow_small_or_imprecise_dtypes=True).then_inc(rt_pool.sem, rt_pool.step)
            pool.wait_ge(slots_ok.sem, slots_ok.at(0))
            pool.wait_ge(zero_out.sem, zero_out.at(NBLK - 1))
            for n in range(B * NT):
                pool.wait_ge(row_in[n % 2].sem, row_in[n % 2].at(n // 2))
                for k in range(2):
                    pool.indirect_dma_start(xs_d, bass.IndirectOffsetOnAxis(ap=slots[:, k, n:n + 1], axis=0),
                                                              rows[:, n % 2, :], None).then_inc(row_sc[n % 2].sem, row_sc[n % 2].step)
            for j in range(2):
                pool.wait_ge(row_sc[j].sem, row_sc[j].at(B * NT - 1))
            barrier(pool, 0)

            pool.wait_ge(wdnhi_ok.sem, wdnhi_ok.at(0))
            pool.tensor_tensor(wdn[1][:, 0, :], we[:, 0, 2 * D:], plain(wdn[0][:, 0, :]), ALU.subtract).then_inc(wdnlo_ok.sem, wdnlo_ok.step)
            with pool.Fori(0, NBLK) as k:
                for m in range(KM):
                    c, q = k * KM + m, m % 2
                    pool.wait_ge(hhi_ok.sem, hhi_ok.at(c))
                    pool.tensor_tensor(hT[1][:, q, :], hf[:, q, :], plain(hT[0][:, q, :]), ALU.subtract).then_inc(hlo_ok.sem, hlo_ok.step)
                    pool.wait_ge(wdnhi_ok.sem, wdnhi_ok.at(c + 1))
                    pool.tensor_tensor(wdn[1][:, 1 - q, :], we[:, (m + 1) % NWR, 2 * D:], plain(wdn[0][:, 1 - q, :]), ALU.subtract).then_inc(wdnlo_ok.sem, wdnlo_ok.step)
            barrier(pool, 1)
            for n in range(B * NT):
                j = n % 2
                if n >= 2:
                    pool.wait_ge(fin_ok.sem, fin_ok.at(n - 2))
                for k, g in enumerate((g_a, g_b)):
                    pool.indirect_dma_start(g[:, j, :], None, ys_d,
                                                        bass.IndirectOffsetOnAxis(ap=slots[:, k, n:n + 1], axis=0)).then_inc(g_in[j].sem, g_in[j].step)

        @block.tensor
        def _(pe):
            for e in evs["pe"]:
                if e.credit:
                    pe.sem_inc(e.sem, e.credit * e.step)
            pe.wait_ge(consts.sem, consts.at(len(const_tiles) - 1))
            with pe.Fori(0, B) as b:
                behind = in_register(pe, wa_lo_ok.at(b))
                pe.wait_ge(wa_lo_ok.sem, wa_lo_ok.step)
                pe.wait_ge(wa_lo_ok.sem, behind)
                with pe.Fori(0, NT // 2) as it:
                    for j in range(2):
                        n = b * NT + it * 2 + j
                        pe.wait_ge(normed.sem, normed.at(n))
                        pe.wait_ge(xlo_ok.sem, xlo_ok.at(n, 2))
                        for c in range(KD):
                            last = pe.transpose(banks[:, j, c * P:c * P + P], xn[:, j, c * P:c * P + P], ident[:])
                        last.then_inc(xt_full.sem, xt_full.step)
                    for j in range(2):
                        n = b * NT + it * 2 + j
                        pe.wait_ge(xlo_ok.sem, xlo_ok.at(n))
                        pe.wait_ge(natq_ok.sem, natq_ok.at(n, 2))
                        for bank, lo, hi in ((2 + 2 * j, 0, QR), (3 + 2 * j, QR, NA)):
                            for c in range(KD):
                                last = three(pe, banks[:, bank, 0:hi - lo], cut(xT, slice(None), j, slice(c * P, c * P + P)),
                                             cut(wa, slice(None), c, slice(lo, hi)), c == 0, c == KD - 1)
                        last.then_inc(projected.sem, projected.step)
                    for j in range(2):
                        n = b * NT + it * 2 + j
                        pe.wait_ge(natq_ok.sem, natq_ok.at(n))
                        pe.wait_ge(natk_ok.sem, natk_ok.at(n))
                        pe.wait_ge(nlo_ok.sem, nlo_ok.at(n, 1))
                        for c in range(4):
                            pe.transpose(banks[:, 6, c * P:c * P + P], nat_q[:, j, c * P:c * P + P], ident[:])
                        for c in range(3):
                            last = pe.transpose(banks[:, 7, c * P:c * P + P], nat_k[:, j, c, :], ident[:])
                        last.then_inc(nt_full.sem, nt_full.step)
                barrier(pe, 0, b)

                def index_queries(q, u):
                    pe.wait_ge(wi_lo_ok.sem, wi_lo_ok.at(q))
                    for c in range(2):
                        pe.wait_ge(i_parts.sem, i_parts.at(q * 2 + c, 2))
                        tok = slice(c * 512, c * 512 + 512)
                        for k in range(KQ):
                            last = three(pe, banks[:, 4 + c, :], cut(wi, slice(None), u, k), cut(qrT, slice(None), k, tok), k == 0, k == KQ - 1)
                        last.then_inc(iq_full.sem, iq_full.step)

                index_queries(b * (H + 1), 0)
                with pe.Fori(0, PAIRS) as hp:
                    for u in range(2):
                        h = hp * 2 + u
                        index_queries(b * (H + 1) + h + 1, 1 - u)
                        pe.wait_ge(iqlo_ok.sem, iqlo_ok.at((b * (H + 1) + h) * 2 + 1))
                        for i in range(1, NT):
                            n = (b * H + h) * (NT - 1) + i - 1
                            r = (u * (NT - 1) + i - 1) % 2
                            pe.wait_ge(relu_ok.sem, relu_ok.at(n, 2))
                            for lo in range(0, EXT[i], 512):
                                hi = min(EXT[i], lo + 512)
                                last = three(pe, banks[:, 2 * r + lo // 512, 0:hi - lo], cut(iqT, slice(None), u, slice(i * P, i * P + P)),
                                             cut(ikT, slice(None), slice(lo, hi)))
                            last.then_inc(is_full.sem, is_full.step)
                barrier(pe, 1, b)

                with pe.Fori(0, PAIRS) as hp:
                    pp = b * PAIRS + hp

                    def turn(g):
                        pe.wait_ge(sh_read.sem, sh_read.at(pp * SHARED + g, 2))
                        return banks[:, 4 + g % 2, :]

                    pe.wait_ge(wp_lo_ok.sem, wp_lo_ok.at(b * (PAIRS + 1) + hp))
                    for c in range(NPE):
                        out = turn(c)
                        for k in range(KQ):
                            last = three(pe, out, cut(wp, slice(None), k), cut(qrT, slice(None), k, slice(c * 512, c * 512 + 512)), k == 0, k == KQ - 1)
                        last.then_inc(sh_full.sem, sh_full.step)
                    for u in range(2):
                        hh = pp * 2 + u
                        g0 = NPE + u * (NPR + NTP)
                        pe.wait_ge(wh_lo_ok.sem, wh_lo_ok.at(b * (H + 1) + hp * 2 + u))
                        for c in range(NPR):
                            out = turn(g0 + c)
                            tok = slice(c % 2 * 512, c % 2 * 512 + 512)
                            if c < 2:
                                for k in range(KQ):
                                    last = three(pe, out, cut(wh, slice(None), u, slice(k * P, k * P + P)), cut(qrT, slice(None), k, tok), k == 0, k == KQ - 1)
                            elif c < 4:
                                last = three(pe, out, cut(wh, slice(None), u, slice(384, 512)), cut(ckvT, slice(None), tok))
                            else:
                                for t in range(4):
                                    row = ((c - 4) * 4 + t) * P
                                    last = three(pe, out[:, t * P:t * P + P], cut(ckvT, slice(None), slice(row, row + P)),
                                                 cut(wh, slice(None), u, slice(512, 640)))
                            last.then_inc(sh_full.sem, sh_full.step)
                        pe.wait_ge(sh_read.sem, sh_read.at(pp * SHARED + g0 + 5))
                        pe.wait_ge(qplo_ok.sem, qplo_ok.at(pp * 2 + 1))

                        def scores(i):
                            pe.wait_ge(masked.sem, masked.at(hh * NT + i, 2))
                            rows_i = slice(i * P, i * P + P)
                            for lo in range(0, EXT[i], 512):
                                hi = min(EXT[i], lo + 512)
                                out = banks[:, 2 * (i % 2) + lo // 512, 0:hi - lo]
                                three(pe, out, cut(qn, slice(None), rows_i), cut(kT, slice(None), slice(lo, hi)), True, False)
                                last = three(pe, out, cut(qp, slice(None), rows_i), cut(kpT, slice(None), u, slice(lo, hi)), False, True)
                            last.then_inc(sc_full.sem, sc_full.step)

                        def turn_probs(s, kt):
                            jj = 4 * s + kt
                            out = turn(g0 + NPR + jj)
                            for i in range(max(4 * s, kt), 4 * s + 4):
                                if kt == 0:
                                    pe.wait_ge(p_norm.sem, p_norm.at(hh * NT + i))
                                last = pe.transpose(out[:, (i - 4 * s) * P:(i - 4 * s + 1) * P],
                                                    probs[:, OFF[i] + kt * P:OFF[i] + kt * P + P], ident[:])
                            last.then_inc(sh_full.sem, sh_full.step)

                        def values(s, kt):
                            jj, lo = 4 * s + kt, max(0, kt - 4 * s) * P
                            pe.wait_ge(sh_read.sem, sh_read.at(pp * SHARED + g0 + NPR + jj))
                            last = three(pe, banks[:, 6 + s, lo:512], cut(v_, slice(None), kt), cut(PT, slice(None), jj % 2, slice(lo, 512)),
                                         kt == 0, kt == 4 * s + 3)
                            last.then_inc(pv_done.sem, pv_done.step)

                        def outputs(s):
                            pe.wait_ge(oT_read.sem, oT_read.at(hh * 2 + s, 2))
                            turn_probs(s, 0)
                            for kt in range(1, 4 * s + 4):
                                turn_probs(s, kt)
                                values(s, kt - 1)
                            values(s, 4 * s + 3)

                        for i in range(6):
                            scores(i)
                        outputs(0)
                        scores(6)
                        scores(7)
                        outputs(1)
                barrier(pe, 2, b)

                def head_rows(h, j, first):
                    pe.wait_ge(olo_ok.sem, olo_ok.at(b * H + h))
                    pe.wait_ge(owlo_ok.sem, owlo_ok.at(b * H + h))
                    for t in range(NT):
                        last = three(pe, banks[:, t, :], cut(oTr, slice(None), j, slice(t * P, t * P + P)), cut(ow, slice(None), j), first, False)
                    last.then_inc(o_mm.sem, o_mm.step)

                head_rows(0, 0, True)
                head_rows(1, 1, False)
                with pe.Fori(1, H // 2) as hp:
                    for j in range(2):
                        head_rows(hp * 2 + j, j, False)
                barrier(pe, 3, b)

            pe.wait_ge(rt.sem, rt.at(RT_MARKED))
            marks = r_mk[:].rearrange("p n e -> p (n e)")
            pe.matmul(banks[:, 0, 0:B * NT * NE], upper[:], marks, start=True, stop=True)
            pe.matmul(banks[:, 1, 0:B * NT * NE], ones[:], marks, start=True, stop=True).then_inc(rt_pe.sem, rt_pe.step)
            barrier(pe, 0)

            with pe.Fori(0, NBLK) as k:
                pe.wait_ge(xe_in.sem, xe_in.at(k))
                for a in range(2):
                    pe.wait_ge(xelo_ok.sem, xelo_ok.at(k * 2 + a, 2))
                    for c in range(KD):
                        last = pe.transpose(banks[:, a, c * P:c * P + P], xe[:, a, c * P:c * P + P], ident[:])
                    last.then_inc(xeT_full.sem, xeT_full.step)
                pe.wait_ge(xelo_ok.sem, xelo_ok.at(k * 2 + 1))

                def up(m):
                    q = m % 2
                    pe.wait_ge(wgulo_ok.sem, wgulo_ok.at(k * KM + m))
                    pe.wait_ge(h_ok.sem, h_ok.at(k * KM + m, 2))
                    for w in range(2):
                        for c in range(KD):
                            last = three(pe, banks[:, 2 + q, w * BLK:w * BLK + BLK], cut(wgu, slice(None), q, slice(w * D + c * P, w * D + c * P + P)),
                                         cut(xeT, slice(None), c), c == 0, c == KD - 1)
                    last.then_inc(gu_full.sem, gu_full.step)

                def down_rows(m):
                    q = m % 2
                    pe.wait_ge(hlo_ok.sem, hlo_ok.at(k * KM + m))
                    pe.wait_ge(wdnlo_ok.sem, wdnlo_ok.at(k * KM + m))
                    if m == 0:
                        pe.wait_ge(ye_ok.sem, ye_ok.at(k, 1))
                    for a in range(2):
                        last = three(pe, banks[:, 6 + a, :], cut(hT, slice(None), q, slice(a * P, a * P + P)), cut(wdn, slice(None), q), m == 0, m == KM - 1)
                    last.then_inc(down.sem, down.step)

                up(0)
                for m in range(1, KM):
                    up(m)
                    down_rows(m - 1)
                down_rows(KM - 1)
            barrier(pe, 1)


def tables():
    f32 = np.float32
    inv = 1.0 / 10000.0 ** (np.arange(0, ROPE, 2, dtype=f32) / ROPE)
    ang = np.outer(np.arange(S, dtype=f32), inv).astype(f32)
    cos, sin = np.cos(ang).astype(f32), np.sin(ang).astype(f32)
    c4, s4 = np.tile(cos.T, (4, 1)), np.tile(sin.T, (4, 1))
    sign = np.where(np.arange(P) < 64, 1.0, -1.0).astype(f32)[:, None]
    turns = ((np.arange(P) // HALF) % 2 == 0)[:, None]
    k, q = np.arange(P)[None, :], np.arange(P)[:, None]
    return {
        "ident": np.eye(P, dtype=f32),
        "causal": np.where(k <= q, 0.0, MASKED).astype(f32),
        "upper": (q < k).astype(f32),
        "ones": np.ones((P, P), f32),
        "rope_c": np.ascontiguousarray(c4),
        "rope_s": np.ascontiguousarray(s4 * sign),
        "idx_c": np.where(turns, c4, 1.0).astype(f32),
        "nat_c": np.ascontiguousarray(cos.reshape(NT, P, HALF).transpose(1, 0, 2)),
        "nat_s": np.ascontiguousarray(sin.reshape(NT, P, HALF).transpose(1, 0, 2)),
    }


def kernel(**inputs):
    import concourse.bacc as bacc
    from concourse.bass_utils import run_bass_kernel_spmd

    g = {k.replace("L0_attn_", "").replace("L0_ffn_", ""): np.asarray(v) for k, v in inputs.items()}
    cc = np.ascontiguousarray

    def by_chunks(w, k):
        return cc(w.reshape(k, P, -1).transpose(1, 0, 2))

    wa = np.concatenate([g["q_a_w"].T, g["kv_a_w"].T, g["idx_wk_w"].T, g["idx_wproj_w"].T, g["gate_w"]], axis=1)
    qb = g["q_b_w"].reshape(H, NOPE + ROPE, QR)
    qn = qb[:, :NOPE, :].transpose(0, 2, 1).reshape(H, KQ, P, NOPE).transpose(0, 2, 1, 3).reshape(H, P, KQ * NOPE)
    qp = qb[:, NOPE:, :].reshape(PAIRS, 2, 2, HALF, QR).transpose(0, 2, 1, 3, 4).reshape(PAIRS, P, QR)
    qp = qp.transpose(0, 2, 1).reshape(PAIRS, KQ, P, P).transpose(0, 2, 1, 3)
    kvb = g["kv_b_w"].reshape(H, NOPE + VD, KVR).transpose(0, 2, 1)
    wh = np.concatenate([qn, kvb], axis=2)
    iq = g["idx_wq_b_w"].reshape(H, 4, HALF, QR)[:, [0, 2, 1, 3]].reshape(H, P, QR)
    wi = iq.transpose(0, 2, 1).reshape(H, KQ, P, P).transpose(0, 2, 1, 3)
    up = [g[w].reshape(NE, KD, P, KM, P).transpose(0, 3, 2, 1, 4).reshape(NE * KM, P, D) for w in ("w1", "w3")]
    arrays = {
        "x": g["hidden_states"],
        "wa": by_chunks(wa, KD),
        "wi": cc(wi),
        "wh": cc(np.concatenate([wh, wh[:1]])),
        "wp": cc(np.concatenate([qp, qp[:1]])),
        "ow": cc(g["o_w"].T.reshape(H, VD, D)),
        "we": cc(np.concatenate(up + [g["w2"].reshape(NE * KM, P, D)], axis=2)),
        "kn_w": cc(np.broadcast_to(g["idx_kn_w"], (P, ID))),
        "kn_b": cc(np.broadcast_to(g["idx_kn_b"], (P, ID))),
        "q_ln": cc(g["q_a_ln_w"].reshape(KQ, P).T),
        "kv_ln": cc(g["kv_a_ln_w"].reshape(P, 1)),
        **tables(),
    }
    nc = bacc.Bacc("TRN2", target_bir_lowering=False, num_devices=1)
    io = {n: nc.dram_tensor(f"in_{n}", a.shape, F32, kind="ExternalInput").ap() for n, a in arrays.items()}
    io["out"] = nc.dram_tensor("out_0", (B, S, D), F32, kind="ExternalOutput").ap()
    build(nc, io)
    r = run_bass_kernel_spmd(nc, [{f"in_{n}": a for n, a in arrays.items()}], core_ids=[0])
    return r.results[0]["out_0"]
```

```python
import numpy as np
import concourse.bass as bass
from concourse import mybir
from contextlib import ExitStack

F32 = mybir.dt.float32
F32R = mybir.dt.float32r
I32 = mybir.dt.int32
U32 = mybir.dt.uint32
ALU = mybir.AluOpType
ACT = mybir.ActivationFunctionType
AX = mybir.AxisListType

P = 128
B, S, D = 2, 1024, 512
T = B * S
NT = S // P
KD = D // P
H, NOPE, ROPE, VD = 16, 128, 64, 128
QR, KVR = 384, 128
KQ = QR // P
ID = 128
TOPK = 128
HALF = ROPE // 2
SCALE = float(NOPE + ROPE) ** -0.5
EPS_LN, EPS_RMS = 1e-5, 1e-6
NE, MF = 8, 1792
KM = MF // P
CQ, CKV, CKP, CIK, CIW, CLG = 0, 384, 512, 576, 704, 720
NA = 728
NB = NA - QR
BLK = 256
NBLK = (2 * T - NE) // BLK + NE
ROWS = NBLK * BLK
MASKED = -1.0e30
TAKEN = -3.0e38
EXT = [(i + 1) * P for i in range(NT)]
OFF = [sum(EXT[:i]) for i in range(NT + 1)]
PAIRS = H // 2
NWR = 7
SLAB = 206 * 1024
RT_SHIFTED, RT_MARKED = 1, 14
ROUNDS = TOPK // 8
NPE, NPR, NT0, NT1 = 2, 6, 4, 8
START = NPE + NPR
PER_PAIR = NPE + 2 * (NPR + NT0 + NT1)
FIRST_TILES, LAST_TILES = (1, 2, 3, 4, 5), (6, 7)


def first_group(b, hp, u):
    return b * PAIRS * PER_PAIR + START + hp * PER_PAIR + u * (NT0 + NPR + NT1)


def split_group(b, hp, u, o):
    each = PER_PAIR - NPE
    behind_rotary = u and o >= NT0 + NPE and not (isinstance(hp, int) and hp == PAIRS - 1)
    return b * PAIRS * each + NPR + hp * each + (u * (NT0 + NPR + NT1) + o - (NPE if behind_rotary else 0))


class Ev:

    def __init__(self, sem, credit=0, step=1):
        self.sem, self.credit, self.step = sem, credit, step

    def at(self, n, back=0):
        return (n - (back - 1 - self.credit)) * self.step


def build(nc, io):
    ctx = ExitStack()
    with ctx:
        evs = {"act": [], "dve": [], "pool": [], "pe": [], "sp": []}

        def ev(name, owner, credit=0, step=1):
            e = Ev(ctx.enter_context(nc.semaphore(name)), credit, step)
            evs[owner].append(e)
            return e

        def dma_ev(name, owner, credit=0):
            return ev(name, owner, credit, 16)

        cursor = [(nc.sbuf_base + 31) // 32 * 32]
        ctx.enter_context(nc.sbuf_tensor("slab", [P, SLAB // 4], F32))

        def place(name, shape, dt=F32):
            t = nc.alloc_sbuf_tensor_at(name, shape, dt, offset=cursor[0])
            cursor[0] += (int(np.prod(shape[1:])) * 4 + 31) // 32 * 32
            return t

        def pair(name, shape):
            return place(name + "_hi", shape, F32R), place(name + "_lo", shape, F32R)

        ident = place("ident", [P, P])
        causal = place("causal", [P, P])
        upper = place("upper", [P, P])
        ones = place("ones", [P, P])
        rope_c = place("rope_c", [P, S])
        rope_s = place("rope_s", [P, S])
        idx_c = place("idx_c", [P, S])
        nat_c = place("nat_c", [P, NT, HALF])
        nat_s = place("nat_s", [P, NT, HALF])
        kn_w = place("kn_w", [P, ID])
        kn_b = place("kn_b", [P, ID])
        q_ln = place("q_ln", [P, KQ])
        kv_ln = place("kv_ln", [P, 1])
        eps_ln = place("eps_ln", [P, 1])
        eps_rms = place("eps_rms", [P, 1])
        logits = place("logits", [P, B * NT, NE])
        iw = place("iw", [P, NT, H])
        m8 = place("m8", [P, NT, 8])
        slots = place("slots", [P, 2, B * NT], I32)
        gates = place("gates", [P, 2, B * NT])
        slot_now = place("slot_now", [P, 2, 2], I32)
        owner = place("owner", [1, NBLK], I32)
        iota8 = place("iota8", [P, NE])
        lim8 = place("lim8", [P, NE])
        iotab = place("iotab", [P, NBLK])
        BATCH = cursor[0]
        qrT = pair("qrT", [P, KQ, S])
        ckvT = pair("ckvT", [P, S])
        kpT = pair("kpT", [P, 2, S])
        ikT = pair("ikT", [P, S])
        scores_of = [place(f"acc{b}", [P, OFF[NT]]) for b in range(B)]
        REGION = cursor[0]
        const_tiles = [("ident", ident), ("causal", causal), ("upper", upper), ("ones", ones), ("rope_c", rope_c),
                       ("rope_s", rope_s), ("idx_c", idx_c), ("nat_c", nat_c), ("nat_s", nat_s),
                       ("kn_w", kn_w), ("kn_b", kn_b), ("q_ln", q_ln), ("kv_ln", kv_ln)]

        wa_raw = place("wa_raw", [P, KD, NA])
        wa = pair("wa", [P, KD, NA])
        x_sb = place("x_sb", [P, 2, D])
        xn = place("xn", [P, 2, D])
        xT = pair("xT", [P, 2, D])
        ln_st = place("ln_st", [P, 2, 6])
        ln_mv = place("ln_mv", [P, 2, 2])
        ln_sd = place("ln_sd", [P, 2, 1])
        ln_r = place("ln_r", [P, 2, 1])
        junk = place("junk", [P, 2, QR])
        junk2 = place("junk2", [P, 2, KVR])
        bs = place("bs", [P, 2, NB])
        ssq = place("ssq", [P, 2, 2])
        ik_st = place("ik_st", [P, 2, 6])
        ik_mv = place("ik_mv", [P, 2, 2])
        sd3 = place("sd3", [P, 2, 3])
        r3 = place("r3", [P, 2, 3])
        nat_q = place("nat_q", [P, 2, QR + KVR])
        nat_k = place("nat_k", [P, 2, 3, P])
        ikn = place("ikn", [P, ID])
        rk1 = place("rk1", [P, 2, HALF])
        rk2 = place("rk2", [P, 2, HALF])
        ri1 = place("ri1", [P, 2, HALF])
        ri2 = place("ri2", [P, 2, HALF])
        zero = place("zero", [P, 2, D])

        cursor[0] = REGION
        wi_raw = place("wi_raw", [P, 2, KQ, P])
        wi = pair("wi", [P, 2, KQ, P])
        iy = place("iy", [P, 2, 512])
        scaled = place("scaled", [P, 512])
        turned = place("turned", [P, 512])
        iqT = pair("iqT", [P, 2, S])
        relu = place("relu", [P, 2, S])
        r_e = place("r_e", [P, B * NT, NE])
        r_t = place("r_t", [P, B * NT])
        r_m = place("r_m", [P, B * NT, 8])
        r_i = place("r_i", [P, B * NT, 8], U32)
        r_if = place("r_if", [P, B * NT, 8])
        r_oh = place("r_oh", [P, 2, B * NT, NE])
        r_mk = place("r_mk", [P, B * NT, NE])
        r_a = place("r_a", [P, B * NT, NE])
        r_b = place("r_b", [P, B * NT, NE])
        r_cnt = place("r_cnt", [P, NE, NE])
        r_n = place("r_n", [P, 3, NE])
        r_sl = place("r_sl", [P, 2, B * NT])
        r_ow = place("r_ow", [P, NBLK, NE])
        r_of = place("r_of", [P, NBLK])

        cursor[0] = REGION
        wh_raw = place("wh_raw", [P, 640])
        wp_raw = place("wp_raw", [P, KQ, P])
        wh = pair("wh", [P, 640])
        wp = pair("wp", [P, KQ, P])
        qn = pair("qn", [P, S])
        qp = pair("qp", [P, S])
        kT = pair("kT", [P, S])
        v_ = pair("v", [P, 2, NT, VD])
        py = place("py", [P, 2, 512])
        p_scaled = place("p_scaled", [P, 512])
        p_turned = place("p_turned", [P, 512])
        probs = place("probs", [P, OFF[NT]])
        nmax = place("nmax", [P, NT])
        row_sum = place("row_sum", [P, NT])
        rinv = place("rinv", [P, NT])
        PT = pair("PT", [P, 2, 512])
        oT = place("oT", [P, 2, 512])
        rows = place("rows", [P, 2, D])

        cursor[0] = REGION
        oT_raw = place("oT_raw", [P, 2, S])
        ow_raw = place("ow_raw", [P, 2, D])
        oTr = pair("oTr", [P, 2, S])
        ow = pair("ow", [P, 2, D])
        xo = place("xo", [P, 2, D])
        po = place("po", [P, 2, D])

        cursor[0] = BATCH
        xe = place("xe", [P, 2, D])
        xeT = pair("xeT", [P, KD, BLK])
        we = place("we", [P, NWR, 3 * D])
        wgu = pair("wgu", [P, 2, 2 * D])
        wdn = pair("wdn", [P, 2, D])
        sg = place("sg", [P, 2, BLK])
        hf = place("hf", [P, 2, BLK])
        hT = pair("hT", [P, 2, BLK])
        ye = place("ye", [P, 2, D])
        g_a = place("g_a", [P, 2, D])
        g_b = place("g_b", [P, 2, D])
        part_sb = place("part_sb", [P, 2, D])
        mix = place("mix", [P, 2, D])
        fin = place("fin", [P, 2, D])
    
        def projection(c, u, part):
            if c < 4:
                return (qn if c < 2 else kT)[part][:, c % 2 * 512:c % 2 * 512 + 512]
            return v_[part][:, u, (c - 4) * 4:(c - 4) * 4 + 4, :]

        banks = ctx.enter_context(nc.psum_tensor("banks", [P, 8, 512]))

        xn_d = nc.dram_tensor("xn_d", (B * NT, P, D), F32, kind="Internal").ap()
        oT_d = nc.dram_tensor("oT_d", (B, H, P, S), F32, kind="Internal").ap()
        part_d = nc.dram_tensor("part_d", (B * NT, P, D), F32, kind="Internal").ap()
        kept_d = [nc.dram_tensor(f"kept_d{i}", (B, P, n), F32R, kind="Internal").ap() for i, n in enumerate((KQ * S, S, 2 * S) * 2)]
        xs_d = nc.dram_tensor("xs_d", (ROWS, D), F32, kind="Internal").ap()
        ys_d = nc.dram_tensor("ys_d", (ROWS, D), F32, kind="Internal").ap()
        xs_blk = xs_d.rearrange("(k a p) d -> k p a d", p=P, a=2)
        ys_blk = ys_d.rearrange("(k a p) d -> k p a d", p=P, a=2)
        x_t = io["x"].rearrange("b (t p) d -> (b t) p d", p=P)
        out_t = io["out"].rearrange("b (t p) d -> (b t) p d", p=P)

        kept = [t[0][:].rearrange("p a c -> p (a c)") if len(t[0].shape) == 3 else t[0][:] for t in (qrT, ckvT, kpT)]
        kept += [t[1][:].rearrange("p a c -> p (a c)") if len(t[1].shape) == 3 else t[1][:] for t in (qrT, ckvT, kpT)]

        phase_end = ctx.enter_context(nc.semaphore("phase_end"))
        consts = dma_ev("consts", "sp")
        wa_in = dma_ev("wa_in", "sp")
        x_in = [dma_ev(f"x_in{j}", "sp") for j in range(2)]
        wi_in = [dma_ev(f"wi_in{j}", "sp") for j in range(2)]
        wh_in = dma_ev("wh_in", "sp")
        kept_out = dma_ev("kept_out", "sp")
        wp_in = dma_ev("wp_in", "sp")
        oT_out = [dma_ev(f"oT_out{j}", "sp", 1) for j in range(2)]
        o_in = [dma_ev(f"o_in{j}", "sp") for j in range(2)]
        ow_in = [dma_ev(f"ow_in{j}", "sp") for j in range(2)]
        xo_in = [dma_ev(f"xo_in{j}", "sp") for j in range(2)]
        zero_out = dma_ev("zero_out", "sp")
        row_in = [dma_ev(f"row_in{j}", "sp") for j in range(2)]
        xe_in = dma_ev("xe_in", "sp")
        we_in = [dma_ev(f"we_in{j}", "sp") for j in range(NWR)]
        part_in = [dma_ev(f"part_in{j}", "sp") for j in range(2)]
        wa_hi_ok = ev("wa_hi_ok", "act")
        deviation = ev("deviation", "act")
        xn_out = [dma_ev(f"xn_out{j}", "act", 1) for j in range(2)]
        xhi_ok = ev("xhi_ok", "act")
        squares = ev("squares", "act")
        roots = ev("roots", "act")
        nhi_ok = ev("nhi_ok", "act")
        wi_hi_ok = ev("wi_hi_ok", "act")
        iqhi_ok = ev("iqhi_ok", "act")
        relu_ok = ev("relu_ok", "act", 2)
        wh_hi_ok = ev("wh_hi_ok", "act")
        wp_hi_ok = ev("wp_hi_ok", "act")
        qphi_ok = ev("qphi_ok", "act")
        sh_hi = ev("sh_hi", "act")
        exps = ev("exps", "act")
        oT_read = ev("oT_read", "act", 2)
        ohi_ok = ev("ohi_ok", "act")
        owhi_ok = ev("owhi_ok", "act")
        part_out = [dma_ev(f"part_out{j}", "act", 1) for j in range(2)]
        rt_exp = ev("rt_exp", "act")
        wguhi_ok = ev("wguhi_ok", "act")
        wdnhi_ok = ev("wdnhi_ok", "act")
        xehi_ok = ev("xehi_ok", "act")
        silu_ok = ev("silu_ok", "act")
        hhi_ok = ev("hhi_ok", "act")
        ye_ok = ev("ye_ok", "act", 1)
        ye_out = dma_ev("ye_out", "act", 1)
        fin_out = [dma_ev(f"fin_out{j}", "act", 1) for j in range(2)]
        eps_ok = ev("eps_ok", "dve")
        stats = ev("stats", "dve")
        moments = ev("moments", "dve")
        inverse = ev("inverse", "dve")
        normed = ev("normed", "dve", 2)
        xlo_ok = ev("xlo_ok", "dve", 2)
        copied = ev("copied", "dve")
        ik_stats = ev("ik_stats", "dve")
        ik_moments = ev("ik_moments", "dve")
        inverses = ev("inverses", "dve")
        natq_ok = ev("natq_ok", "dve", 2)
        nlo_ok = ev("nlo_ok", "dve", 2)
        acc_clear = ev("acc_clear", "dve")
        i_parts = ev("i_parts", "dve", 2)
        iy_ok = ev("iy_ok", "dve", 1)
        acc_ok = ev("acc_ok", "dve", 2)
        diag_ok = ev("diag_ok", "dve")
        top8_ok = ev("top8_ok", "dve")
        taken_ok = ev("taken_ok", "dve", NT - 1)
        mask_ok = ev("mask_ok", "dve")
        sh_read = ev("sh_read", "dve", 2)
        py_ok = ev("py_ok", "dve", 1)
        masked = ev("masked", "dve", 2)
        sums_inv = ev("sums_inv", "dve")
        olo_ok = ev("olo_ok", "dve", 2)
        po_ok = ev("po_ok", "dve", 2)
        rt = ev("rt", "dve")
        wgulo_ok = ev("wgulo_ok", "dve", NWR)
        xelo_ok = ev("xelo_ok", "dve", 2)
        h_ok = ev("h_ok", "dve", 2)
        mix_ok = ev("mix_ok", "dve")
        fin_ok = ev("fin_ok", "dve", 2)
        wa_lo_ok = ev("wa_lo_ok", "pool")
        nat_clear = ev("nat_clear", "pool")
        key_step = [ev(f"key_step{j}", "pool") for j in range(5)]
        natk_ok = ev("natk_ok", "pool", 2)
        wi_lo_ok = ev("wi_lo_ok", "pool", 2)
        iqlo_ok = ev("iqlo_ok", "pool", 2)
        wh_lo_ok = ev("wh_lo_ok", "pool", 1)
        wp_lo_ok = ev("wp_lo_ok", "pool", 1)
        qplo_ok = ev("qplo_ok", "dve", 2)
        p_norm = ev("p_norm", "pool")
        owlo_ok = ev("owlo_ok", "pool", 2)
        zero_ok = ev("zero_ok", "pool")
        rt_pool = ev("rt_pool", "pool")
        row_sc = [dma_ev(f"row_sc{j}", "pool") for j in range(2)]
        wdnlo_ok = ev("wdnlo_ok", "pool", NWR)
        kept_in = dma_ev("kept_in", "pool")
        slot_set = ev("slot_set", "pool")
        hlo_ok = ev("hlo_ok", "dve", 2)
        g_in = [dma_ev(f"g_in{j}", "pool") for j in range(2)]
        xt_full = ev("xt_full", "pe", 2)
        projected = ev("projected", "pe")
        nt_full = ev("nt_full", "pe", 2)
        iq_full = ev("iq_full", "pe", 4)
        is_full = ev("is_full", "pe", 1)
        sh_full = ev("sh_full", "pe")
        sc_full = ev("sc_full", "pe")
        pv_done = ev("pv_done", "pe", 2)
        o_mm = ev("o_mm", "pe", 2)
        rt_pe = ev("rt_pe", "pe")
        xeT_full = ev("xeT_full", "pe", 2)
        gu_full = ev("gu_full", "pe")
        down = ev("down", "pe", 2)

        spare = {}

        def in_register(eng, value):
            if eng not in spare:
                spare[eng] = eng.alloc_register(name="behind")
            eng.reg_mov(spare[eng], value)
            return spare[eng]

        block = ctx.enter_context(nc.Block())

        def barrier(eng, k):
            eng.drain().then_inc(phase_end, 1)
            eng.wait_ge(phase_end, 5 * (k + 1))

        def three(pe, out, left, right, start=True, stop=True):
            pe.matmul(out, left[0], right[0], start=start, stop=False, skip_group_check=True)
            pe.matmul(out, left[0], right[1], start=False, stop=False, skip_group_check=True)
            return pe.matmul(out, left[1], right[0], start=False, stop=stop, skip_group_check=True)

        def cut(parts, *at):
            return parts[0][at], parts[1][at]

        def scores_psum(r, width):
            return banks[:, 2 * r:2 * r + 2, :].rearrange("p a c -> p (a c)")[:, 0:width]

        def plain(part):
            return part.bitcast(F32)

        @block.sync
        def _(sp):
            for e in evs["sp"]:
                if e.credit:
                    sp.sem_inc(e.sem, e.credit * e.step)
            for name, tile in const_tiles:
                sp.dma_start(tile[:], io[name]).then_inc(consts.sem, consts.step)
            for b in range(B):
                sp.dma_start(wa_raw[:], io["wa"]).then_inc(wa_in.sem, wa_in.step)
                with sp.Fori(0, NT // 2) as it:
                    for j in range(2):
                        n = b * NT + it * 2 + j
                        sp.wait_ge(normed.sem, normed.at(n, 2))
                        sp.dma_start(x_sb[:, j, :], x_t[n]).then_inc(x_in[j].sem, x_in[j].step)
                if b == 0:
                    sp.wait_ge(zero_ok.sem, zero_ok.at(0))
                    with sp.Fori(0, NBLK) as k:
                        sp.dma_start(xs_blk[k], zero[:]).then_inc(zero_out.sem, zero_out.step)
                    sp.wait_ge(zero_out.sem, zero_out.at(NBLK - 1))
                barrier(sp, 2 * b)
                for u in range(2):
                    sp.dma_start(wi_raw[:, u], io["wi"][u]).then_inc(wi_in[u].sem, wi_in[u].step)
                for part, there in zip(kept, kept_d):
                    sp.dma_start(plain(there[b]), plain(part)).then_inc(kept_out.sem, kept_out.step)
                with sp.Fori(0, PAIRS - 1) as hp:
                    for u in range(2):
                        sp.wait_ge(wi_lo_ok.sem, wi_lo_ok.at(b * H + hp * 2 + u))
                        sp.dma_start(wi_raw[:, u], io["wi"][hp * 2 + u + 2]).then_inc(wi_in[u].sem, wi_in[u].step)
                sp.wait_ge(kept_out.sem, kept_out.at((b + 1) * len(kept) - 1))
                barrier(sp, 2 * b + 1)
            for b in range(B):
                sp.dma_start(wp_raw[:], io["wp"][0]).then_inc(wp_in.sem, wp_in.step)
                sp.dma_start(wh_raw[:], io["wh"][0]).then_inc(wh_in.sem, wh_in.step)
                sp.wait_ge(wh_lo_ok.sem, wh_lo_ok.at(b * H))
                sp.dma_start(wh_raw[:], io["wh"][1]).then_inc(wh_in.sem, wh_in.step)
                if b == 0:
                    for u in range(2):
                        sp.dma_start(rows[:, u, :], xn_d[u]).then_inc(row_in[u].sem, row_in[u].step)

                def head_step(hp, u, last):
                    h = hp * 2 + u
                    if u == 0 and not last:
                        sp.wait_ge(wp_lo_ok.sem, wp_lo_ok.at(b * PAIRS + hp))
                        sp.dma_start(wp_raw[:], io["wp"][hp + 1]).then_inc(wp_in.sem, wp_in.step)
                    if not last:
                        sp.wait_ge(wh_lo_ok.sem, wh_lo_ok.at(b * H + h + 1))
                        sp.dma_start(wh_raw[:], io["wh"][h + 2]).then_inc(wh_in.sem, wh_in.step)
                    for s in range(2):
                        sp.wait_ge(oT_read.sem, oT_read.at((b * H + h) * 2 + s))
                        sp.dma_start(oT_d[b, h, :, s * 512:s * 512 + 512], oT[:, s, :]).then_inc(oT_out[s].sem, oT_out[s].step)
                    if b == 0 and not last:
                        sp.wait_ge(row_sc[u].sem, row_sc[u].at(hp * 2 + 1))
                        sp.dma_start(rows[:, u, :], xn_d[h + 2]).then_inc(row_in[u].sem, row_in[u].step)

                with sp.Fori(0, PAIRS - 1) as hp:
                    for u in range(2):
                        head_step(hp, u, False)
                for u in range(2):
                    head_step(PAIRS - 1, u, True)
                for s in range(2):
                    sp.wait_ge(oT_out[s].sem, oT_out[s].at(b * H + H - 1))
                barrier(sp, 4 + 2 * b)

                def head_loads(hp):
                    for j in range(2):
                        h = hp * 2 + j
                        sp.wait_ge(olo_ok.sem, olo_ok.at(b * H + h, 2))
                        sp.wait_ge(owlo_ok.sem, owlo_ok.at(b * H + h, 2))
                        sp.dma_start(oT_raw[:, j, :], oT_d[b, h]).then_inc(o_in[j].sem, o_in[j].step)
                        sp.dma_start(ow_raw[:, j, :], io["ow"][h]).then_inc(ow_in[j].sem, ow_in[j].step)

                with sp.Fori(0, H // 2) as hp:
                    head_loads(hp)
                with sp.Fori(0, NT // 2) as it:
                    for j in range(2):
                        n = b * NT + it * 2 + j
                        sp.wait_ge(po_ok.sem, po_ok.at(n, 2))
                        sp.dma_start(xo[:, j, :], x_t[n]).then_inc(xo_in[j].sem, xo_in[j].step)
                barrier(sp, 5 + 2 * b)
            with sp.Fori(0, NBLK) as k:
                e = sp.value_load(owner[0:1, bass.ds(k, 1)], min_val=0, max_val=NE - 1)
                sp.wait_ge(xeT_full.sem, xeT_full.at(k * 2 + 1, 2))
                sp.dma_start(xe[:], xs_blk[k]).then_inc(xe_in.sem, xe_in.step)
                for m in range(KM):
                    r = m % NWR
                    sp.wait_ge(wgulo_ok.sem, wgulo_ok.at(k * KM + m, NWR))
                    sp.wait_ge(wdnlo_ok.sem, wdnlo_ok.at(k * KM + m, NWR))
                    sp.dma_start(we[:, r, :], io["we"][e * KM + m]).then_inc(we_in[r].sem, we_in[r].step)
            for m in range(2):
                sp.wait_ge(wgulo_ok.sem, wgulo_ok.at(NBLK * KM + m, NWR))
                sp.wait_ge(wdnlo_ok.sem, wdnlo_ok.at(NBLK * KM + m, NWR))
                sp.dma_start(we[:, m, :], io["we"][m]).then_inc(we_in[m].sem, we_in[m].step)
            barrier(sp, 8)
            with sp.Fori(0, B * NT // 2) as it:
                for j in range(2):
                    n = it * 2 + j
                    sp.wait_ge(fin_ok.sem, fin_ok.at(n, 2))
                    sp.dma_start(part_sb[:, j, :], part_d[n]).then_inc(part_in[j].sem, part_in[j].step)

        @block.scalar
        def _(act):
            for e in evs["act"]:
                if e.credit:
                    act.sem_inc(e.sem, e.credit * e.step)
            act.wait_ge(eps_ok.sem, eps_ok.at(0))
            act.wait_ge(consts.sem, consts.at(len(const_tiles) - 1))
            for b in range(B):
                act.wait_ge(wa_in.sem, wa_in.at(b))
                act.activation(wa[0][:], wa_raw[:], ACT.Copy).then_inc(wa_hi_ok.sem, wa_hi_ok.step)
                with act.Fori(0, NT // 2) as it:
                    for j in range(2):
                        n = b * NT + it * 2 + j
                        act.wait_ge(moments.sem, moments.at(n))
                        act.activation(ln_sd[:, j, :], ln_mv[:, j, 1:2], ACT.Sqrt, bias=eps_ln[:, 0:1]).then_inc(deviation.sem, deviation.step)
                        act.wait_ge(normed.sem, normed.at(n))
                        act.dma_start(xn_d[n], xn[:, j, :]).then_inc(xn_out[j].sem, xn_out[j].step)
                    for j in range(2):
                        n = b * NT + it * 2 + j
                        act.wait_ge(xt_full.sem, xt_full.at(n))
                        act.activation(xT[0][:, j, :], banks[:, j, :], ACT.Copy).then_inc(xhi_ok.sem, xhi_ok.step)
                    for j in range(2):
                        n = b * NT + it * 2 + j
                        act.wait_ge(projected.sem, projected.at(n))
                        act.activation(junk[:, j, :], banks[:, 2 + 2 * j, 0:QR], ACT.Square, accum_out=ssq[:, j, 0:1])
                        act.wait_ge(copied.sem, copied.at(n))
                        act.activation(junk2[:, j, :], bs[:, j, 0:KVR], ACT.Square, accum_out=ssq[:, j, 1:2]).then_inc(squares.sem, squares.step)
                        act.wait_ge(ik_moments.sem, ik_moments.at(n))
                        act.wait_ge(squares.sem, squares.at(n))
                        act.activation(sd3[:, j, 0:1], ssq[:, j, 0:1], ACT.Sqrt, bias=eps_rms[:, 0:1], scale=1.0 / QR)
                        act.activation(sd3[:, j, 1:2], ssq[:, j, 1:2], ACT.Sqrt, bias=eps_rms[:, 0:1], scale=1.0 / KVR)
                        act.activation(sd3[:, j, 2:3], ik_mv[:, j, 1:2], ACT.Sqrt, bias=eps_rms[:, 0:1]).then_inc(roots.sem, roots.step)
                    for j in range(2):
                        n = b * NT + it * 2 + j
                        cols = bass.ds((it * 2 + j) * P, P)
                        act.wait_ge(nt_full.sem, nt_full.at(n))
                        for c in range(KQ):
                            act.activation(qrT[0][:, c, cols], banks[:, 6, c * P:c * P + P], ACT.Identity, scale=q_ln[:, c:c + 1])
                        act.activation(ckvT[0][:, cols], banks[:, 6, QR:QR + KVR], ACT.Identity, scale=kv_ln[:, 0:1])
                        act.activation(kpT[0][:, :, cols], banks[:, 7, 0:2 * P].rearrange("p (a c) -> p a c", a=2), ACT.Copy)
                        act.activation(ikT[0][:, cols], banks[:, 7, 2 * P:3 * P], ACT.Copy).then_inc(nhi_ok.sem, nhi_ok.step)
                for j in range(2):
                    act.wait_ge(xn_out[j].sem, xn_out[j].at(b * (NT // 2) + NT // 2 - 1))
                barrier(act, 2 * b)

                def queries_hi(q, u, c):
                    act.wait_ge(iy_ok.sem, iy_ok.at(q * 2 + c))
                    act.activation(iqT[0][:, u, c * 512:c * 512 + 512], iy[:, c, :], ACT.Copy).then_inc(iqhi_ok.sem, iqhi_ok.step)

                def index_step(hp, u, last):
                    q = b * H + hp * 2 + u
                    for i in range(1, NT):
                        n = q * (NT - 1) + i - 1
                        r = (u * (NT - 1) + i - 1) % 2
                        act.wait_ge(is_full.sem, is_full.at(n))
                        act.wait_ge(acc_ok.sem, acc_ok.at(n, 2))
                        act.activation(relu[:, r, 0:EXT[i]], scores_psum(r, EXT[i]), ACT.Relu).then_inc(relu_ok.sem, relu_ok.step)
                        if i in (2, 4) and not (last and u == 1):
                            queries_hi(q + 1, 1 - u, i // 4)
                    if not last:
                        act.wait_ge(wi_in[u].sem, wi_in[u].at(b * PAIRS + hp + 1))
                        act.activation(wi[0][:, u], wi_raw[:, u], ACT.Copy).then_inc(wi_hi_ok.sem, wi_hi_ok.step)

                for u in range(2):
                    act.wait_ge(wi_in[u].sem, wi_in[u].at(b * PAIRS))
                    act.activation(wi[0][:, u], wi_raw[:, u], ACT.Copy).then_inc(wi_hi_ok.sem, wi_hi_ok.step)
                if b == B - 1:
                    act.wait_ge(rt.sem, rt.at(RT_SHIFTED))
                    act.activation(r_e[:], r_e[:], ACT.Exp).then_inc(rt_exp.sem, rt_exp.step)
                for c in range(2):
                    queries_hi(b * H, 0, c)
                with act.Fori(0, PAIRS - 1) as hp:
                    for u in range(2):
                        index_step(hp, u, False)
                for u in range(2):
                    index_step(PAIRS - 1, u, True)
                barrier(act, 2 * b + 1)

            for b in range(B):
                def pair_weights_hi(p):
                    act.wait_ge(wp_in.sem, wp_in.at(b * PAIRS + p))
                    act.activation(wp[0][:], wp_raw[:], ACT.Copy).then_inc(wp_hi_ok.sem, wp_hi_ok.step)

                def head_weights_hi(h):
                    act.wait_ge(wh_in.sem, wh_in.at(b * H + h))
                    act.activation(wh[0][:], wh_raw[:], ACT.Copy).then_inc(wh_hi_ok.sem, wh_hi_ok.step)

                def rotary_hi(p):
                    for c in range(NPE):
                        act.wait_ge(py_ok.sem, py_ok.at((b * PAIRS + p) * 2 + c))
                        act.activation(qp[0][:, c * 512:c * 512 + 512], py[:, c, :], ACT.Copy).then_inc(qphi_ok.sem, qphi_ok.step)

                def projections_hi(g, o, u):
                    for c in range(NPR):
                        dst, src = projection(c, u, 0), banks[:, 4 + (o + c) % 2, :]
                        if c >= 4:
                            src = src.rearrange("p (t d) -> p t d", t=4)
                        act.wait_ge(sh_full.sem, sh_full.at(g + o + c))
                        act.activation(dst, src, ACT.Copy).then_inc(sh_hi.sem, sh_hi.step)

                def exponentials(h, i):
                    act.wait_ge(masked.sem, masked.at((b * H + h) * NT + i))
                    a = probs[:, OFF[i]:OFF[i + 1]]
                    act.activation(a, a, ACT.Exp, bias=nmax[:, i:i + 1], scale=-1.0,
                                            accum_out=row_sum[:, i:i + 1]).then_inc(exps.sem, exps.step)

                def head_step(hp, u, last):
                    h, g, tail = hp * 2 + u, first_group(b, hp, u), last and u == 1

                    def block_hi(s, kt):
                        jj = 4 * s + kt
                        o = kt if s == 0 else NT0 + (0 if tail else NPR + NPE * u) + kt
                        lo = max(0, kt - 4 * s) * P
                        act.wait_ge(sh_full.sem, sh_full.at(g + o))
                        act.wait_ge(pv_done.sem, pv_done.at((b * H + h) * (NT0 + NT1) + jj, 2))
                        act.activation(PT[0][:, jj % 2, lo:512], banks[:, 4 + o % 2, lo:512], ACT.Copy).then_inc(sh_hi.sem, sh_hi.step)

                    def out_rows(s):
                        act.wait_ge(pv_done.sem, pv_done.at((b * H + h) * (NT0 + NT1) + NT0 + NT1 * s - 1))
                        act.wait_ge(oT_out[s].sem, oT_out[s].at(b * H + h, 1))
                        act.activation(oT[:, s, :], banks[:, 6 + s, :], ACT.Copy).then_inc(oT_read.sem, oT_read.step)

                    if not tail:
                        if u == 1:
                            pair_weights_hi(hp + 1)
                        head_weights_hi(h + 1)
                    block_hi(0, 0)
                    exponentials(h, 4)
                    block_hi(0, 1)
                    exponentials(h, 5)
                    block_hi(0, 2)
                    exponentials(h, 6)
                    block_hi(0, 3)
                    out_rows(0)
                    exponentials(h, 7)
                    if not tail:
                        if u == 1:
                            rotary_hi(hp + 1)
                        projections_hi(g, NT0 + NPE * u, 1 - u)
                    for kt in range(NT1):
                        block_hi(1, kt)
                        if 1 <= kt <= 4 and not tail:
                            exponentials(h + 1, kt - 1)
                    out_rows(1)

                pair_weights_hi(0)
                head_weights_hi(0)
                rotary_hi(0)
                projections_hi(b * PAIRS * PER_PAIR, NPE, 0)
                for i in range(4):
                    exponentials(0, i)
                with act.Fori(0, PAIRS - 1) as hp:
                    for u in range(2):
                        head_step(hp, u, False)
                for u in range(2):
                    head_step(PAIRS - 1, u, True)
                barrier(act, 4 + 2 * b)

                with act.Fori(0, H // 2) as hp:
                    for j in range(2):
                        n = b * H + hp * 2 + j
                        act.wait_ge(o_in[j].sem, o_in[j].at(b * (H // 2) + hp))
                        act.wait_ge(o_mm.sem, o_mm.at(n, 2))
                        act.activation(oTr[0][:, j, :], oT_raw[:, j, :], ACT.Copy).then_inc(ohi_ok.sem, ohi_ok.step)
                        act.wait_ge(ow_in[j].sem, ow_in[j].at(b * (H // 2) + hp))
                        act.activation(ow[0][:, j, :], ow_raw[:, j, :], ACT.Copy).then_inc(owhi_ok.sem, owhi_ok.step)
                with act.Fori(0, NT // 2) as it:
                    for j in range(2):
                        n = b * NT + it * 2 + j
                        act.wait_ge(po_ok.sem, po_ok.at(n))
                        act.dma_start(part_d[n], po[:, j, :]).then_inc(part_out[j].sem, part_out[j].step)
                for j in range(2):
                    act.wait_ge(part_out[j].sem, part_out[j].at(b * (NT // 2) + NT // 2 - 1))
                barrier(act, 5 + 2 * b)

            def up_hi(c, r, q, k_in):
                act.wait_ge(we_in[r].sem, we_in[r].at(k_in))
                act.activation(wgu[0][:, q, :], we[:, r, 0:2 * D], ACT.Copy).then_inc(wguhi_ok.sem, wguhi_ok.step)

            up_hi(0, 0, 0, 0)
            up_hi(1, 1, 1, 0)
            act.activation(wdn[0][:, 0, :], we[:, 0, 2 * D:], ACT.Copy).then_inc(wdnhi_ok.sem, wdnhi_ok.step)
            with act.Fori(0, NBLK) as k:
                for a in range(2):
                    act.wait_ge(xeT_full.sem, xeT_full.at(k * 2 + a))
                    act.activation(xeT[0][:, :, a * P:a * P + P],
                                               banks[:, a, :].rearrange("p (k t) -> p k t", k=KD), ACT.Copy).then_inc(xehi_ok.sem, xehi_ok.step)
                for m in range(KM):
                    c, q = k * KM + m, m % 2
                    act.wait_ge(gu_full.sem, gu_full.at(c))
                    act.activation(sg[:, q, :], banks[:, 2 + q, 0:BLK], ACT.Silu).then_inc(silu_ok.sem, silu_ok.step)
                    act.wait_ge(h_ok.sem, h_ok.at(c))
                    act.activation(hT[0][:, q, :], hf[:, q, :], ACT.Copy).then_inc(hhi_ok.sem, hhi_ok.step)
                    r = (m + 2) % NWR
                    act.wait_ge(we_in[r].sem, we_in[r].at(k * (KM // NWR) + (m + 2) // NWR))
                    act.activation(wgu[0][:, q, :], we[:, r, 0:2 * D], ACT.Copy).then_inc(wguhi_ok.sem, wguhi_ok.step)
                    act.wait_ge(down.sem, down.at(c, 1))
                    act.activation(wdn[0][:, 1 - q, :], we[:, (m + 1) % NWR, 2 * D:], ACT.Copy).then_inc(wdnhi_ok.sem, wdnhi_ok.step)
                act.wait_ge(down.sem, down.at(k * KM + KM - 1))
                act.wait_ge(ye_out.sem, ye_out.at(k, 1))
                act.activation(ye[:], banks[:, 6:8, :], ACT.Copy).then_inc(ye_ok.sem, ye_ok.step)
                act.wait_ge(ye_ok.sem, ye_ok.at(k))
                act.dma_start(ys_blk[k], ye[:]).then_inc(ye_out.sem, ye_out.step)
            act.wait_ge(ye_out.sem, ye_out.at(NBLK - 1))
            barrier(act, 8)
            with act.Fori(0, B * NT // 2) as it:
                for j in range(2):
                    act.wait_ge(fin_ok.sem, fin_ok.at(it * 2 + j))
                    act.dma_start(out_t[it * 2 + j], fin[:, j, :]).then_inc(fin_out[j].sem, fin_out[j].step)
            for j in range(2):
                act.wait_ge(fin_out[j].sem, fin_out[j].at(B * NT // 2 - 1))

        @block.vector
        def _(dve):
            for e in evs["dve"]:
                if e.credit:
                    dve.sem_inc(e.sem, e.credit * e.step)
            dve.memset(eps_ln[:], EPS_LN)
            dve.memset(eps_rms[:], EPS_RMS).then_inc(eps_ok.sem, eps_ok.step)
            dve.wait_ge(consts.sem, consts.at(len(const_tiles) - 1))
            step = [0]

            def link(ins):
                step[0] += 1
                ins.then_inc(rt.sem, 1)
                dve.wait_ge(rt.sem, step[0])

            def over(ap, shape):
                return ap.broadcast_to(shape)

            NTT = B * NT
            full = [P, NTT, NE]
            def route_start():
                link(dve.tensor_reduce(r_t[:], logits[:], AX.X, ALU.max))
                link(dve.tensor_tensor(r_e[:], logits[:], over(r_t[:].unsqueeze(2), full), ALU.subtract))
                assert step[0] == RT_SHIFTED + 1
                dve.wait_ge(rt_exp.sem, rt_exp.at(0))
                link(dve.tensor_reduce(r_t[:], r_e[:], AX.X, ALU.add))
                link(dve.reciprocal(r_t[:], r_t[:]))
                link(dve.tensor_tensor(r_e[:], r_e[:], over(r_t[:].unsqueeze(2), full), ALU.mult))
                for n in range(NTT):
                    last = dve.max(r_m[:, n, :], r_e[:, n, :])
                link(last)
                for n in range(NTT):
                    last = dve.max_index(r_i[:, n, :], r_m[:, n, :], r_e[:, n, :])
                link(last)
                link(dve.tensor_tensor(r_t[:], r_m[:, :, 0], r_m[:, :, 1], ALU.add))
                link(dve.reciprocal(r_t[:], r_t[:]))
                for k in range(2):
                    link(dve.tensor_tensor(gates[:, k, :], r_m[:, :, k], r_t[:], ALU.mult))
                link(dve.tensor_copy(r_if[:], r_i[:]))
                dve.wait_ge(rt_pool.sem, rt_pool.at(0))
                for k in range(2):
                    link(dve.tensor_tensor(r_oh[:, k], over(iota8[:].unsqueeze(1), full), over(r_if[:, :, k:k + 1], full), ALU.is_equal))
                link(dve.tensor_tensor(r_mk[:], r_oh[:, 0], r_oh[:, 1], ALU.add))
                assert step[0] == RT_MARKED + 1

            def route_end():
                dve.wait_ge(rt_pe.sem, rt_pe.at(0))
                link(dve.tensor_copy(r_a[:], banks[:, 7, 0:NTT * NE].rearrange("p (n e) -> p n e", e=NE)))
                src, dst, w = r_a, r_b, 1
                while w < NTT:
                    link(dve.tensor_copy(dst[:, 0:w, :], src[:, 0:w, :]))
                    link(dve.tensor_tensor(dst[:, w:, :], src[:, w:, :], src[:, 0:NTT - w, :], ALU.add))
                    src, dst, w = dst, src, 2 * w
                link(dve.tensor_tensor(r_cnt[:], over(src[:, NTT - 1, :].unsqueeze(2), [P, NE, NE]), over(lim8[:].unsqueeze(1), [P, NE, NE]), ALU.is_gt))
                link(dve.tensor_reduce(r_n[:, 0, :], r_cnt[:], AX.X, ALU.add))
                link(dve.tensor_copy(r_n[:, 1, :], r_n[:, 0, :]))
                at, to, w = 1, 2, 1
                while w < NE:
                    link(dve.tensor_copy(r_n[:, to, 0:w], r_n[:, at, 0:w]))
                    link(dve.tensor_tensor(r_n[:, to, w:], r_n[:, at, w:], r_n[:, at, 0:NE - w], ALU.add))
                    at, to, w = to, at, 2 * w
                link(dve.tensor_tensor(r_ow[:], over(iotab[:].unsqueeze(2), [P, NBLK, NE]), over(r_n[:, at, :].unsqueeze(1), [P, NBLK, NE]), ALU.is_ge))
                link(dve.tensor_reduce(r_of[:], r_ow[:], AX.X, ALU.add))
                link(dve.tensor_scalar(r_of[:], r_of[:], float(NE - 1), None, ALU.min))
                link(dve.tensor_copy(owner[:], r_of[0:1, :]))
                link(dve.tensor_tensor(r_n[:, to, :], r_n[:, at, :], r_n[:, 0, :], ALU.subtract))
                link(dve.tensor_scalar(r_n[:, to, :], r_n[:, to, :], float(BLK), None, ALU.mult))
                link(dve.tensor_tensor(dst[:], banks[:, 6, 0:NTT * NE].rearrange("p (n e) -> p n e", e=NE), over(r_n[:, to, :].unsqueeze(1), full), ALU.add))
                link(dve.tensor_tensor(dst[:, 1:, :], dst[:, 1:, :], src[:, 0:NTT - 1, :], ALU.add))
                for k in range(2):
                    link(dve.tensor_tensor(r_mk[:], r_oh[:, k], dst[:], ALU.mult))
                    link(dve.tensor_reduce(r_sl[:, k, :], r_mk[:], AX.X, ALU.add))
                link(dve.tensor_copy(slots[:], r_sl[:]))

            def begin_best(bt):
                acc = scores_of[bt]
                for i in range(1, NT):
                    diag = acc[:, OFF[i + 1] - P:OFF[i + 1]]
                    last = dve.tensor_tensor(diag, diag, causal[:], ALU.add)
                last.then_inc(diag_ok.sem, diag_ok.step)
                dve.wait_ge(diag_ok.sem, diag_ok.at(bt))

            def find(bt, k, i):
                n = (bt * ROUNDS + k) * (NT - 1) + i - 1
                behind = in_register(dve, taken_ok.at(n, NT - 1))
                dve.wait_ge(taken_ok.sem, taken_ok.step)
                dve.wait_ge(taken_ok.sem, behind)
                dve.max(m8[:, i, :], scores_of[bt][:, OFF[i]:OFF[i + 1]]).then_inc(top8_ok.sem, top8_ok.step)

            def take(bt, k, i):
                a = scores_of[bt][:, OFF[i]:OFF[i + 1]]
                behind = in_register(dve, top8_ok.at((bt * ROUNDS + k) * (NT - 1) + i - 1))
                dve.wait_ge(top8_ok.sem, top8_ok.step)
                dve.wait_ge(top8_ok.sem, behind)
                dve.match_replace(a, m8[:, i, :], a, TAKEN).then_inc(taken_ok.sem, taken_ok.step)

            def find_and_take(bt, k, tiles):
                find(bt, k, tiles[0])
                for i, after in zip(tiles, tiles[1:]):
                    find(bt, k, after)
                    take(bt, k, i)
                take(bt, k, tiles[-1])

            def end_best(bt):
                acc = scores_of[bt]
                dve.wait_ge(taken_ok.sem, taken_ok.at((bt + 1) * ROUNDS * (NT - 1) - 1))
                for i in range(1, NT):
                    a = acc[:, OFF[i]:OFF[i + 1]]
                    dve.tensor_scalar(a, a, TAKEN, MASKED, ALU.not_equal, ALU.mult)
                dve.tensor_copy(acc[:, 0:P], causal[:]).then_inc(mask_ok.sem, mask_ok.step)
                dve.wait_ge(mask_ok.sem, mask_ok.at(bt))

            for b in range(B):
                if b == 1:
                    begin_best(0)
                with dve.Fori(0, NT // 2) as it:
                    for j in range(2):
                        n = b * NT + it * 2 + j
                        dve.wait_ge(x_in[j].sem, x_in[j].at(b * (NT // 2) + it))
                        dve.bn_stats(ln_st[:, j, :], x_sb[:, j, :]).then_inc(stats.sem, stats.step)
                        behind = in_register(dve, stats.at(n))
                        dve.wait_ge(stats.sem, stats.step)
                        dve.wait_ge(stats.sem, behind)
                        dve.bn_aggr(ln_mv[:, j, :], ln_st[:, j, :]).then_inc(moments.sem, moments.step)
                        dve.wait_ge(deviation.sem, deviation.at(n))
                        dve.reciprocal(ln_r[:, j, :], ln_sd[:, j, :]).then_inc(inverse.sem, inverse.step)
                        dve.wait_ge(inverse.sem, inverse.at(n))
                        dve.wait_ge(xt_full.sem, xt_full.at(n, 2))
                        dve.wait_ge(xn_out[j].sem, xn_out[j].at(b * (NT // 2) + it, 1))
                        dve.tensor_scalar(xn[:, j, :], x_sb[:, j, :], ln_mv[:, j, 0:1], ln_r[:, j, 0:1],
                                                     ALU.subtract, ALU.mult).then_inc(normed.sem, normed.step)
                    for j in range(2):
                        n = b * NT + it * 2 + j
                        if b == 1:
                            find_and_take(0, it * 2, LAST_TILES if j else FIRST_TILES)
                        dve.wait_ge(xhi_ok.sem, xhi_ok.at(n))
                        dve.tensor_tensor(xT[1][:, j, :], banks[:, j, :], plain(xT[0][:, j, :]), ALU.subtract).then_inc(xlo_ok.sem, xlo_ok.step)
                    for j in range(2):
                        n = b * NT + it * 2 + j
                        dve.wait_ge(projected.sem, projected.at(n))
                        dve.wait_ge(natk_ok.sem, natk_ok.at(n, 2))
                        if b == 1:
                            find_and_take(0, it * 2 + 1, LAST_TILES if j else FIRST_TILES)
                        dve.tensor_copy(bs[:, j, :], banks[:, 3 + 2 * j, 0:NB]).then_inc(copied.sem, copied.step)
                        dve.wait_ge(copied.sem, copied.at(n))
                        dve.bn_stats(ik_st[:, j, :], bs[:, j, CIK - QR:CIW - QR]).then_inc(ik_stats.sem, ik_stats.step)
                        behind = in_register(dve, ik_stats.at(n))
                        dve.wait_ge(ik_stats.sem, ik_stats.step)
                        dve.wait_ge(ik_stats.sem, behind)
                        dve.bn_aggr(ik_mv[:, j, :], ik_st[:, j, :]).then_inc(ik_moments.sem, ik_moments.step)
                        dve.tensor_scalar(iw[:, bass.ds(it * 2 + j, 1), :], bs[:, j:j + 1, CIW - QR:CLG - QR], float(H) ** -0.5, None, ALU.mult)
                        dve.tensor_copy(logits[:, bass.ds(n, 1), :], bs[:, j:j + 1, CLG - QR:NB])
                        dve.wait_ge(roots.sem, roots.at(n))
                        dve.reciprocal(r3[:, j, :], sd3[:, j, :]).then_inc(inverses.sem, inverses.step)
                        dve.wait_ge(inverses.sem, inverses.at(n))
                        dve.wait_ge(nt_full.sem, nt_full.at(n, 2))
                        dve.tensor_scalar(nat_q[:, j, 0:QR], banks[:, 2 + 2 * j, 0:QR], r3[:, j, 0:1], None, ALU.mult)
                        dve.tensor_scalar(nat_q[:, j, QR:], bs[:, j, 0:KVR], r3[:, j, 1:2], None, ALU.mult).then_inc(natq_ok.sem, natq_ok.step)
                    for j in range(2):
                        n = b * NT + it * 2 + j
                        cols = bass.ds((it * 2 + j) * P, P)
                        dve.wait_ge(nhi_ok.sem, nhi_ok.at(n))
                        for c in range(KQ):
                            dve.scalar_tensor_tensor(qrT[1][:, c, cols], banks[:, 6, c * P:c * P + P], q_ln[:, c:c + 1],
                                                     plain(qrT[0][:, c, cols]), ALU.mult, ALU.subtract)
                        dve.scalar_tensor_tensor(ckvT[1][:, cols], banks[:, 6, QR:QR + KVR], kv_ln[:, 0:1],
                                                 plain(ckvT[0][:, cols]), ALU.mult, ALU.subtract)
                        dve.tensor_tensor(kpT[1][:, :, cols], banks[:, 7, 0:2 * P].rearrange("p (a c) -> p a c", a=2),
                                          plain(kpT[0][:, :, cols]), ALU.subtract)
                        dve.tensor_tensor(ikT[1][:, cols], banks[:, 7, 2 * P:3 * P], plain(ikT[0][:, cols]), ALU.subtract).then_inc(nlo_ok.sem, nlo_ok.step)
                barrier(dve, 2 * b)

                acc = scores_of[b]
                dve.memset(turned[:], 0.0)
                dve.memset(acc[:], 0.0).then_inc(acc_clear.sem, acc_clear.step)
                dve.wait_ge(acc_clear.sem, acc_clear.at(b))

                def queries(q, c):
                    g, tok = q * 2 + c, slice(c * 512, c * 512 + 512)
                    dve.wait_ge(iq_full.sem, iq_full.at(g))
                    dve.wait_ge(iy_ok.sem, iy_ok.at(g, 1))
                    dve.tensor_tensor(scaled[:], banks[:, 4 + c, :], idx_c[:, tok], ALU.mult)
                    dve.tensor_tensor(turned[0:32, :], banks[64:96, 4 + c, :], rope_s[64:96, tok], ALU.mult)
                    dve.tensor_tensor(turned[64:96, :], banks[0:32, 4 + c, :], rope_s[0:32, tok], ALU.mult).then_inc(i_parts.sem, i_parts.step)
                    dve.wait_ge(i_parts.sem, i_parts.at(g))
                    dve.wait_ge(iqlo_ok.sem, iqlo_ok.at(g, 2))
                    dve.tensor_tensor(iy[:, c, :], scaled[:], turned[:], ALU.add).then_inc(iy_ok.sem, iy_ok.step)

                def index_step(hp, u, last):
                    h = hp * 2 + u
                    q = b * H + h
                    for i in range(1, NT):
                        if i in (1, 4) and not (last and u == 1):
                            queries(q + 1, i // 4)
                        n = q * (NT - 1) + i - 1
                        r = (u * (NT - 1) + i - 1) % 2
                        a = acc[:, OFF[i]:OFF[i + 1]]
                        dve.wait_ge(relu_ok.sem, relu_ok.at(n))
                        dve.scalar_tensor_tensor(a, relu[:, r, 0:EXT[i]], iw[:, i, bass.ds(h, 1)], a, ALU.mult, ALU.add).then_inc(acc_ok.sem, acc_ok.step)
                    if b == 1:
                        find_and_take(0, hp + ROUNDS // 2, LAST_TILES if u else FIRST_TILES)

                if b == B - 1:
                    route_start()
                for c in range(2):
                    queries(b * H, c)
                with dve.Fori(0, PAIRS - 1) as hp:
                    for u in range(2):
                        index_step(hp, u, False)
                for u in range(2):
                    index_step(PAIRS - 1, u, True)
                if b == B - 1:
                    end_best(0)
                    route_end()
                dve.wait_ge(acc_ok.sem, acc_ok.at((b + 1) * H * (NT - 1) - 1))
                barrier(dve, 2 * b + 1)

            for b in range(B):
                acc = scores_of[b]
                if b == 0:
                    begin_best(1)

                def rotary(g, o, p, c):
                    n, tok = (b * PAIRS + p) * 2 + c, slice(c * 512, c * 512 + 512)
                    bank = 4 + (o + c) % 2
                    dve.wait_ge(sh_full.sem, sh_full.at(g + o + c))
                    dve.wait_ge(py_ok.sem, py_ok.at(n, 1))
                    dve.tensor_tensor(p_scaled[:], banks[:, bank, :], rope_c[:, tok], ALU.mult)
                    dve.tensor_tensor(p_turned[0:64, :], banks[64:128, bank, :], rope_s[64:128, tok], ALU.mult)
                    dve.tensor_tensor(p_turned[64:128, :], banks[0:64, bank, :], rope_s[0:64, tok], ALU.mult).then_inc(sh_read.sem, sh_read.step)
                    dve.wait_ge(sh_read.sem, sh_read.at(g + o + c))
                    dve.wait_ge(qplo_ok.sem, qplo_ok.at(n, 2))
                    dve.tensor_tensor(py[:, c, :], p_scaled[:], p_turned[:], ALU.add).then_inc(py_ok.sem, py_ok.step)

                def rotary_lo(p, c):
                    tok = slice(c * 512, c * 512 + 512)
                    dve.wait_ge(qphi_ok.sem, qphi_ok.at((b * PAIRS + p) * 2 + c))
                    dve.tensor_tensor(qp[1][:, tok], py[:, c, :], plain(qp[0][:, tok]), ALU.subtract).then_inc(qplo_ok.sem, qplo_ok.step)

                def projections_lo(k, o, u, c):
                    dst, src, hi = projection(c, u, 1), banks[:, 4 + (o + c) % 2, :], projection(c, u, 0)
                    if c >= 4:
                        src = src.rearrange("p (t d) -> p t d", t=4)
                    dve.wait_ge(sh_hi.sem, sh_hi.at(k))
                    dve.tensor_tensor(dst, src, plain(hi), ALU.subtract).then_inc(sh_read.sem, sh_read.step)

                def mask_and_max(h, i):
                    behind = in_register(dve, sc_full.at((b * H + h) * NT + i))
                    dve.wait_ge(sc_full.sem, sc_full.step)
                    dve.wait_ge(sc_full.sem, behind)
                    dve.tensor_tensor_reduce(probs[:, OFF[i]:OFF[i + 1]], scores_psum(i % 2, EXT[i]),
                                                        acc[:, OFF[i]:OFF[i + 1]], -SCALE, 3.0e38, ALU.add, ALU.min,
                                                        nmax[:, i:i + 1]).then_inc(masked.sem, masked.step)

                def invert(h, i):
                    dve.wait_ge(exps.sem, exps.at((b * H + h) * NT + i))
                    dve.reciprocal(rinv[:, i:i + 1], row_sum[:, i:i + 1]).then_inc(sums_inv.sem, sums_inv.step)

                def head_step(hp, u, last):
                    h, g, tail = hp * 2 + u, first_group(b, hp, u), last and u == 1

                    def block_lo(s, kt):
                        jj = 4 * s + kt
                        o = kt if s == 0 else NT0 + (0 if tail else NPR + NPE * u) + kt
                        lo = max(0, kt - 4 * s) * P
                        dve.wait_ge(sh_hi.sem, sh_hi.at(split_group(b, hp, u, o)))
                        dve.tensor_tensor(PT[1][:, jj % 2, lo:512], banks[:, 4 + o % 2, lo:512],
                                                      plain(PT[0][:, jj % 2, lo:512]), ALU.subtract).then_inc(sh_read.sem, sh_read.step)

                    def best(*pieces):
                        if b == 0:
                            for what, i in pieces:
                                what(1, h, i)

                    mask_and_max(h, 4)
                    block_lo(0, 0)
                    best((find, 1), (find, 2), (take, 1))
                    mask_and_max(h, 5)
                    invert(h, 4)
                    block_lo(0, 1)
                    best((find, 3), (take, 2))
                    mask_and_max(h, 6)
                    invert(h, 5)
                    block_lo(0, 2)
                    best((find, 4), (take, 3))
                    block_lo(0, 3)
                    invert(h, 6)
                    mask_and_max(h, 7)
                    best((find, 5), (take, 4))
                    if u == 1 and not tail:
                        rotary(g, NT0, hp + 1, 0)
                    invert(h, 7)
                    if not tail:
                        o = NT0 + NPE * u
                        if u == 1:
                            rotary(g, NT0, hp + 1, 1)
                        for c in range(NPR):
                            projections_lo(split_group(b, hp, u, o + c), o, 1 - u, c)
                            if u == 1 and c < NPE:
                                rotary_lo(hp + 1, c)
                    best((find, 6))
                    for kt in range(NT1):
                        block_lo(1, kt)
                        if kt < 4 and not tail:
                            mask_and_max(h + 1, kt)
                        if 1 <= kt <= 4 and not tail:
                            invert(h + 1, kt - 1)
                        if kt == 1:
                            best((take, 5))
                        if kt == 3:
                            best((find, 7))
                        if kt == 5:
                            best((take, 6))
                    best((take, 7))

                for c in range(NPE):
                    rotary(b * PAIRS * PER_PAIR, 0, 0, c)
                for c in range(NPR):
                    projections_lo(b * PAIRS * (PER_PAIR - NPE) + c, NPE, 0, c)
                    if c < NPE:
                        rotary_lo(0, c)
                for i in range(4):
                    mask_and_max(0, i)
                    if i:
                        invert(0, i - 1)
                invert(0, 3)
                with dve.Fori(0, PAIRS - 1) as hp:
                    for u in range(2):
                        head_step(hp, u, False)
                for u in range(2):
                    head_step(PAIRS - 1, u, True)
                if b == 0:
                    end_best(1)
                barrier(dve, 4 + 2 * b)

                with dve.Fori(0, H // 2) as hp:
                    for j in range(2):
                        n = b * H + hp * 2 + j
                        dve.wait_ge(ohi_ok.sem, ohi_ok.at(n))
                        dve.tensor_tensor(oTr[1][:, j, :], oT_raw[:, j, :], plain(oTr[0][:, j, :]), ALU.subtract).then_inc(olo_ok.sem, olo_ok.step)
                dve.wait_ge(o_mm.sem, o_mm.at(b * H + H - 1))
                with dve.Fori(0, NT // 2) as it:
                    for j in range(2):
                        dve.wait_ge(xo_in[j].sem, xo_in[j].at(b * (NT // 2) + it))
                        dve.wait_ge(part_out[j].sem, part_out[j].at(b * (NT // 2) + it, 1))
                        dve.tensor_tensor(po[:, j, :], banks[:, bass.ds(it * 2 + j, 1), :].rearrange("p a c -> p (a c)"), xo[:, j, :], ALU.add).then_inc(po_ok.sem, po_ok.step)
                barrier(dve, 5 + 2 * b)

            def up_lo(c, r, q):
                dve.wait_ge(wguhi_ok.sem, wguhi_ok.at(c))
                dve.tensor_tensor(wgu[1][:, q, :], we[:, r, 0:2 * D], plain(wgu[0][:, q, :]), ALU.subtract).then_inc(wgulo_ok.sem, wgulo_ok.step)

            up_lo(0, 0, 0)
            up_lo(1, 1, 1)
            with dve.Fori(0, NBLK) as k:
                for a in range(2):
                    dve.wait_ge(xehi_ok.sem, xehi_ok.at(k * 2 + a))
                    dve.tensor_tensor(xeT[1][:, :, a * P:a * P + P], banks[:, a, :].rearrange("p (k t) -> p k t", k=KD),
                                                  plain(xeT[0][:, :, a * P:a * P + P]), ALU.subtract).then_inc(xelo_ok.sem, xelo_ok.step)
                for m in range(KM):
                    c, q = k * KM + m, m % 2
                    dve.wait_ge(silu_ok.sem, silu_ok.at(c))
                    dve.wait_ge(hlo_ok.sem, hlo_ok.at(c, 2))
                    dve.tensor_tensor(hf[:, q, :], banks[:, 2 + q, BLK:2 * BLK], sg[:, q, :], ALU.mult).then_inc(h_ok.sem, h_ok.step)
                    dve.wait_ge(hhi_ok.sem, hhi_ok.at(c))
                    dve.tensor_tensor(hT[1][:, q, :], hf[:, q, :], plain(hT[0][:, q, :]), ALU.subtract).then_inc(hlo_ok.sem, hlo_ok.step)
                    up_lo(c + 2, (m + 2) % NWR, q)
            barrier(dve, 8)

            with dve.Fori(0, B * NT // 2) as it:
                for j in range(2):
                    n = it * 2 + j
                    dve.wait_ge(part_in[j].sem, part_in[j].at(it))
                    dve.wait_ge(g_in[j].sem, g_in[j].at(it * 2 + 1))
                    dve.scalar_tensor_tensor(mix[:, j, :], g_a[:, j, :], gates[:, 0, bass.ds(n, 1)], part_sb[:, j, :], ALU.mult, ALU.add).then_inc(mix_ok.sem, mix_ok.step)
                    dve.wait_ge(mix_ok.sem, mix_ok.at(n))
                    dve.wait_ge(fin_out[j].sem, fin_out[j].at(it, 1))
                    dve.scalar_tensor_tensor(fin[:, j, :], g_b[:, j, :], gates[:, 1, bass.ds(n, 1)], mix[:, j, :], ALU.mult, ALU.add).then_inc(fin_ok.sem, fin_ok.step)

        @block.gpsimd
        def _(pool):
            for e in evs["pool"]:
                if e.credit:
                    pool.sem_inc(e.sem, e.credit * e.step)
            pool.wait_ge(consts.sem, consts.at(len(const_tiles) - 1))
            pool.memset(zero[:], 0.0).then_inc(zero_ok.sem, zero_ok.step)
            pool.iota(iota8[:], [[1, NE]], base=0, channel_multiplier=0, allow_small_or_imprecise_dtypes=True)
            pool.iota(lim8[:], [[BLK, NE]], base=0, channel_multiplier=0, allow_small_or_imprecise_dtypes=True)
            pool.iota(iotab[:], [[1, NBLK]], base=0, channel_multiplier=0, allow_small_or_imprecise_dtypes=True).then_inc(rt_pool.sem, rt_pool.step)
            for b in range(B):
                pool.memset(nat_k[:], 0.0).then_inc(nat_clear.sem, nat_clear.step)
                pool.wait_ge(nat_clear.sem, nat_clear.at(b))
                pool.wait_ge(wa_hi_ok.sem, wa_hi_ok.at(b))
                pool.tensor_tensor(wa[1][:], wa_raw[:], plain(wa[0][:]), ALU.subtract).then_inc(wa_lo_ok.sem, wa_lo_ok.step)
                with pool.Fori(0, NT // 2) as it:
                    for j in range(2):
                        n = b * NT + it * 2 + j
                        both = [P, 2, HALF]
                        cos = nat_c[:, bass.ds(it * 2 + j, 1), :].broadcast_to(both)
                        sin = nat_s[:, bass.ds(it * 2 + j, 1), :].broadcast_to(both)
                        kp = bs[:, j, CKP - QR:CIK - QR].rearrange("p (a c) -> p a c", a=2)
                        behind = in_register(pool, inverses.at(n))
                        pool.wait_ge(inverses.sem, inverses.step)
                        pool.wait_ge(inverses.sem, behind)
                        behind = in_register(pool, natk_ok.at(n, 1))
                        pool.wait_ge(natk_ok.sem, natk_ok.step)
                        pool.wait_ge(natk_ok.sem, behind)
                        behind = in_register(pool, nt_full.at(n, 2))
                        pool.wait_ge(nt_full.sem, nt_full.step)
                        pool.wait_ge(nt_full.sem, behind)
                        pool.tensor_scalar(ikn[:], bs[:, j, CIK - QR:CIW - QR], ik_mv[:, j, 0:1], r3[:, j, 2:3],
                                                           ALU.subtract, ALU.mult).then_inc(key_step[0].sem, key_step[0].step)
                        pool.tensor_tensor(rk1[:], kp, cos, ALU.mult)
                        pool.tensor_tensor(rk2[:], kp, sin, ALU.mult).then_inc(key_step[1].sem, key_step[1].step)
                        pool.wait_ge(key_step[0].sem, key_step[0].at(n))
                        pool.tensor_tensor(ikn[:], ikn[:], kn_w[:], ALU.mult).then_inc(key_step[2].sem, key_step[2].step)
                        pool.wait_ge(key_step[1].sem, key_step[1].at(n))
                        for odd in range(2):
                            o = HALF * odd
                            pool.tensor_tensor(nat_k[:, j, odd, o:o + HALF], rk1[:, 0, :], rk2[:, 1, :], ALU.subtract)
                            pool.tensor_tensor(nat_k[:, j, odd, 64 + o:64 + o + HALF], rk1[:, 1, :], rk2[:, 0, :], ALU.add)
                        pool.wait_ge(key_step[2].sem, key_step[2].at(n))
                        pool.tensor_tensor(ikn[:], ikn[:], kn_b[:], ALU.add).then_inc(key_step[3].sem, key_step[3].step)
                        behind = in_register(pool, key_step[3].at(n))
                        pool.wait_ge(key_step[3].sem, key_step[3].step)
                        pool.wait_ge(key_step[3].sem, behind)
                        rot = ikn[:, 0:ROPE].rearrange("p (a c) -> p a c", a=2)
                        pool.tensor_tensor(ri1[:], rot, cos, ALU.mult)
                        pool.tensor_tensor(ri2[:], rot, sin, ALU.mult).then_inc(key_step[4].sem, key_step[4].step)
                        pool.tensor_copy(nat_k[:, j, 2, HALF:2 * HALF], ikn[:, ROPE:ROPE + HALF])
                        pool.tensor_copy(nat_k[:, j, 2, 3 * HALF:], ikn[:, ROPE + HALF:])
                        pool.wait_ge(key_step[4].sem, key_step[4].at(n))
                        pool.tensor_tensor(nat_k[:, j, 2, 0:HALF], ri1[:, 0, :], ri2[:, 1, :], ALU.subtract)
                        pool.tensor_tensor(nat_k[:, j, 2, 2 * HALF:3 * HALF], ri1[:, 1, :], ri2[:, 0, :], ALU.add).then_inc(natk_ok.sem, natk_ok.step)
                barrier(pool, 2 * b)

                def weights_lo(q, u):
                    pool.wait_ge(wi_hi_ok.sem, wi_hi_ok.at(q))
                    pool.tensor_tensor(wi[1][:, u], wi_raw[:, u], plain(wi[0][:, u]), ALU.subtract).then_inc(wi_lo_ok.sem, wi_lo_ok.step)

                def queries_lo(q, u):
                    for c in range(2):
                        tok = slice(c * 512, c * 512 + 512)
                        pool.wait_ge(iqhi_ok.sem, iqhi_ok.at(q * 2 + c))
                        pool.tensor_tensor(iqT[1][:, u, tok], iy[:, c, :], plain(iqT[0][:, u, tok]), ALU.subtract).then_inc(iqlo_ok.sem, iqlo_ok.step)

                for u in range(2):
                    weights_lo(b * H + u, u)
                queries_lo(b * H, 0)
                with pool.Fori(0, PAIRS - 1) as hp:
                    for u in range(2):
                        queries_lo(b * H + hp * 2 + u + 1, 1 - u)
                        weights_lo(b * H + hp * 2 + u + 2, u)
                queries_lo(b * H + H - 1, 1)
                if b == B - 1:
                    pool.wait_ge(kept_out.sem, kept_out.at(B * len(kept) - 1))
                    for part in (1, 2, 4, 5):
                        pool.dma_start(kept[part], kept_d[part][0]).then_inc(kept_in.sem, kept_in.step)
                    pool.wait_ge(iq_full.sem, iq_full.at((b * H + H) * 2 - 1))
                    for part in (0, 3):
                        pool.dma_start(kept[part], kept_d[part][0]).then_inc(kept_in.sem, kept_in.step)
                    pool.wait_ge(kept_in.sem, kept_in.at(len(kept) - 1))
                barrier(pool, 2 * b + 1)

            for b in range(B):
                def pair_weights_lo(p):
                    pool.wait_ge(wp_hi_ok.sem, wp_hi_ok.at(b * PAIRS + p))
                    pool.tensor_tensor(wp[1][:], wp_raw[:], plain(wp[0][:]), ALU.subtract).then_inc(wp_lo_ok.sem, wp_lo_ok.step)

                def head_weights_lo(h):
                    pool.wait_ge(wh_hi_ok.sem, wh_hi_ok.at(b * H + h))
                    pool.tensor_tensor(wh[1][:], wh_raw[:], plain(wh[0][:]), ALU.subtract).then_inc(wh_lo_ok.sem, wh_lo_ok.step)

                def normalise(h, i):
                    a = probs[:, OFF[i]:OFF[i + 1]]
                    behind = in_register(pool, sums_inv.at((b * H + h) * NT + i))
                    pool.wait_ge(sums_inv.sem, sums_inv.step)
                    pool.wait_ge(sums_inv.sem, behind)
                    pool.tensor_scalar(a, a, rinv[:, i:i + 1], None, ALU.mult).then_inc(p_norm.sem, p_norm.step)

                def head_step(hp, u, last):
                    h, tail = hp * 2 + u, last and u == 1
                    if not tail:
                        if u == 1:
                            pair_weights_lo(hp + 1)
                        head_weights_lo(h + 1)
                    for i in range(4, NT):
                        normalise(h, i)
                    if b == 0:
                        behind = in_register(pool, row_in[u].at(hp))
                        pool.wait_ge(row_in[u].sem, row_in[u].step)
                        pool.wait_ge(row_in[u].sem, behind)
                        pool.tensor_copy(slot_now[:, u, :], slots[:, :, bass.ds(h, 1)].rearrange("p k n -> p (k n)")).then_inc(slot_set.sem, slot_set.step)
                        behind = in_register(pool, slot_set.at(h))
                        pool.wait_ge(slot_set.sem, slot_set.step)
                        pool.wait_ge(slot_set.sem, behind)
                        for k in range(2):
                            pool.indirect_dma_start(xs_d, bass.IndirectOffsetOnAxis(ap=slot_now[:, u, k:k + 1], axis=0),
                                                                  rows[:, u, :], None).then_inc(row_sc[u].sem, row_sc[u].step)
                    if not tail:
                        for i in range(4):
                            normalise(h + 1, i)

                pair_weights_lo(0)
                head_weights_lo(0)
                for i in range(4):
                    normalise(0, i)
                with pool.Fori(0, PAIRS - 1) as hp:
                    for u in range(2):
                        head_step(hp, u, False)
                for u in range(2):
                    head_step(PAIRS - 1, u, True)
                if b == 0:
                    for j in range(2):
                        pool.wait_ge(row_sc[j].sem, row_sc[j].at(B * NT - 1))
                barrier(pool, 4 + 2 * b)

                if b + 1 < B:
                    for part, there in zip(kept, kept_d):
                        pool.dma_start(part, there[b + 1]).then_inc(kept_in.sem, kept_in.step)
                with pool.Fori(0, H // 2) as hp:
                    for j in range(2):
                        n = b * H + hp * 2 + j
                        pool.wait_ge(owhi_ok.sem, owhi_ok.at(n))
                        pool.tensor_tensor(ow[1][:, j, :], ow_raw[:, j, :], plain(ow[0][:, j, :]), ALU.subtract).then_inc(owlo_ok.sem, owlo_ok.step)
                pool.wait_ge(kept_in.sem, kept_in.at(B * len(kept) - 1))
                barrier(pool, 5 + 2 * b)

            pool.wait_ge(wdnhi_ok.sem, wdnhi_ok.at(0))
            pool.tensor_tensor(wdn[1][:, 0, :], we[:, 0, 2 * D:], plain(wdn[0][:, 0, :]), ALU.subtract).then_inc(wdnlo_ok.sem, wdnlo_ok.step)
            with pool.Fori(0, NBLK) as k:
                for m in range(KM):
                    c, q = k * KM + m, m % 2
                    pool.wait_ge(wdnhi_ok.sem, wdnhi_ok.at(c + 1))
                    pool.tensor_tensor(wdn[1][:, 1 - q, :], we[:, (m + 1) % NWR, 2 * D:], plain(wdn[0][:, 1 - q, :]), ALU.subtract).then_inc(wdnlo_ok.sem, wdnlo_ok.step)
            barrier(pool, 8)
            for n in range(B * NT):
                j = n % 2
                if n >= 2:
                    pool.wait_ge(fin_ok.sem, fin_ok.at(n - 2))
                for k, g in enumerate((g_a, g_b)):
                    pool.indirect_dma_start(g[:, j, :], None, ys_d,
                                                        bass.IndirectOffsetOnAxis(ap=slots[:, k, n:n + 1], axis=0)).then_inc(g_in[j].sem, g_in[j].step)

        @block.tensor
        def _(pe):
            for e in evs["pe"]:
                if e.credit:
                    pe.sem_inc(e.sem, e.credit * e.step)
            pe.wait_ge(consts.sem, consts.at(len(const_tiles) - 1))
            for b in range(B):
                pe.wait_ge(wa_lo_ok.sem, wa_lo_ok.at(b))
                with pe.Fori(0, NT // 2) as it:
                    for j in range(2):
                        n = b * NT + it * 2 + j
                        pe.wait_ge(normed.sem, normed.at(n))
                        pe.wait_ge(xlo_ok.sem, xlo_ok.at(n, 2))
                        for c in range(KD):
                            last = pe.transpose(banks[:, j, c * P:c * P + P], xn[:, j, c * P:c * P + P], ident[:])
                        last.then_inc(xt_full.sem, xt_full.step)
                    for j in range(2):
                        n = b * NT + it * 2 + j
                        pe.wait_ge(xlo_ok.sem, xlo_ok.at(n))
                        pe.wait_ge(natq_ok.sem, natq_ok.at(n, 2))
                        for bank, lo, hi in ((2 + 2 * j, 0, QR), (3 + 2 * j, QR, NA)):
                            for c in range(KD):
                                last = three(pe, banks[:, bank, 0:hi - lo], cut(xT, slice(None), j, slice(c * P, c * P + P)),
                                             cut(wa, slice(None), c, slice(lo, hi)), c == 0, c == KD - 1)
                        last.then_inc(projected.sem, projected.step)
                    for j in range(2):
                        n = b * NT + it * 2 + j
                        pe.wait_ge(natq_ok.sem, natq_ok.at(n))
                        pe.wait_ge(natk_ok.sem, natk_ok.at(n))
                        pe.wait_ge(nlo_ok.sem, nlo_ok.at(n, 1))
                        for c in range(4):
                            pe.transpose(banks[:, 6, c * P:c * P + P], nat_q[:, j, c * P:c * P + P], ident[:])
                        for c in range(3):
                            last = pe.transpose(banks[:, 7, c * P:c * P + P], nat_k[:, j, c, :], ident[:])
                        last.then_inc(nt_full.sem, nt_full.step)
                barrier(pe, 2 * b)

                def queries(q, u, c):
                    if c == 0:
                        pe.wait_ge(wi_lo_ok.sem, wi_lo_ok.at(q))
                    pe.wait_ge(i_parts.sem, i_parts.at(q * 2 + c, 2))
                    tok = slice(c * 512, c * 512 + 512)
                    for k in range(KQ):
                        last = three(pe, banks[:, 4 + c, :], cut(wi, slice(None), u, k), cut(qrT, slice(None), k, tok), k == 0, k == KQ - 1)
                    last.then_inc(iq_full.sem, iq_full.step)

                def index_step(hp, u, last_pair):
                    q = b * H + hp * 2 + u
                    for i in range(1, NT):
                        if i in (1, 4):
                            if not (last_pair and u == 1):
                                queries(q + 1, 1 - u, i // 4)
                            pe.wait_ge(iqlo_ok.sem, iqlo_ok.at(q * 2 + i // 4))
                        n = q * (NT - 1) + i - 1
                        r = (u * (NT - 1) + i - 1) % 2
                        pe.wait_ge(relu_ok.sem, relu_ok.at(n, 2))
                        for lo in range(0, EXT[i], 512):
                            hi = min(EXT[i], lo + 512)
                            last = three(pe, banks[:, 2 * r + lo // 512, 0:hi - lo], cut(iqT, slice(None), u, slice(i * P, i * P + P)),
                                         cut(ikT, slice(None), slice(lo, hi)))
                        last.then_inc(is_full.sem, is_full.step)

                for c in range(2):
                    queries(b * H, 0, c)
                if b == B - 1:
                    pe.wait_ge(rt.sem, rt.at(RT_MARKED))
                    marks = r_mk[:].rearrange("p n e -> p (n e)")
                    pe.matmul(banks[:, 6, 0:B * NT * NE], upper[:], marks, start=True, stop=True)
                    pe.matmul(banks[:, 7, 0:B * NT * NE], ones[:], marks, start=True, stop=True).then_inc(rt_pe.sem, rt_pe.step)
                with pe.Fori(0, PAIRS - 1) as hp:
                    for u in range(2):
                        index_step(hp, u, False)
                for u in range(2):
                    index_step(PAIRS - 1, u, True)
                barrier(pe, 2 * b + 1)

            for b in range(B):
                def turn(g, o):
                    pe.wait_ge(sh_read.sem, sh_read.at(g + o, 2))
                    return banks[:, 4 + o % 2, :]

                def rotary(g, o, p):
                    pe.wait_ge(wp_lo_ok.sem, wp_lo_ok.at(b * PAIRS + p))
                    for c in range(NPE):
                        out = turn(g, o + c)
                        for k in range(KQ):
                            last = three(pe, out, cut(wp, slice(None), k), cut(qrT, slice(None), k, slice(c * 512, c * 512 + 512)), k == 0, k == KQ - 1)
                        last.then_inc(sh_full.sem, sh_full.step)

                def project(g, o, h):
                    pe.wait_ge(wh_lo_ok.sem, wh_lo_ok.at(b * H + h))
                    for c in range(NPR):
                        out = turn(g, o + c)
                        tok = slice(c % 2 * 512, c % 2 * 512 + 512)
                        if c < 2:
                            for k in range(KQ):
                                last = three(pe, out, cut(wh, slice(None), slice(k * P, k * P + P)), cut(qrT, slice(None), k, tok), k == 0, k == KQ - 1)
                        elif c < 4:
                            last = three(pe, out, cut(wh, slice(None), slice(384, 512)), cut(ckvT, slice(None), tok))
                        else:
                            for t in range(4):
                                row = ((c - 4) * 4 + t) * P
                                last = three(pe, out[:, t * P:t * P + P], cut(ckvT, slice(None), slice(row, row + P)),
                                             cut(wh, slice(None), slice(512, 640)))
                        last.then_inc(sh_full.sem, sh_full.step)

                def scores(h, u, i):
                    pe.wait_ge(masked.sem, masked.at((b * H + h) * NT + i, 2))
                    rows_i = slice(i * P, i * P + P)
                    for lo in range(0, EXT[i], 512):
                        hi = min(EXT[i], lo + 512)
                        out = banks[:, 2 * (i % 2) + lo // 512, 0:hi - lo]
                        three(pe, out, cut(qn, slice(None), rows_i), cut(kT, slice(None), slice(lo, hi)), True, False)
                        last = three(pe, out, cut(qp, slice(None), rows_i), cut(kpT, slice(None), u, slice(lo, hi)), False, True)
                    last.then_inc(sc_full.sem, sc_full.step)

                def head_step(hp, u, last):
                    h, g, tail = hp * 2 + u, first_group(b, hp, u), last and u == 1
                    second = NT0 + (0 if tail else NPR + NPE * u)

                    def turn_probs(s, kt):
                        out = turn(g, second * s + kt)
                        for i in range(max(4 * s, kt), 4 * s + 4):
                            if kt == 0:
                                pe.wait_ge(p_norm.sem, p_norm.at((b * H + h) * NT + i))
                            last = pe.transpose(out[:, (i - 4 * s) * P:(i - 4 * s + 1) * P],
                                                probs[:, OFF[i] + kt * P:OFF[i] + kt * P + P], ident[:])
                        last.then_inc(sh_full.sem, sh_full.step)

                    def values(s, kt):
                        jj, lo = 4 * s + kt, max(0, kt - 4 * s) * P
                        if kt == 0:
                            pe.wait_ge(oT_read.sem, oT_read.at((b * H + h) * 2 + s, 2))
                        pe.wait_ge(sh_read.sem, sh_read.at(g + second * s + kt))
                        last = three(pe, banks[:, 6 + s, lo:512], cut(v_, slice(None), u, kt), cut(PT, slice(None), jj % 2, slice(lo, 512)),
                                     kt == 0, kt == 4 * s + 3)
                        last.then_inc(pv_done.sem, pv_done.step)

                    scores(h, u, 4)
                    turn_probs(0, 0)
                    scores(h, u, 5)
                    turn_probs(0, 1)
                    values(0, 0)
                    scores(h, u, 6)
                    turn_probs(0, 2)
                    values(0, 1)
                    turn_probs(0, 3)
                    values(0, 2)
                    scores(h, u, 7)
                    values(0, 3)
                    if not tail:
                        if u == 1:
                            rotary(g, NT0, hp + 1)
                        project(g, NT0 + NPE * u, h + 1)
                    for kt in range(NT1):
                        turn_probs(1, kt)
                        if kt < 4 and not tail:
                            if kt == 0:
                                pe.wait_ge(sh_read.sem, sh_read.at(g + second - 1))
                                if u == 1:
                                    pe.wait_ge(qplo_ok.sem, qplo_ok.at((b * PAIRS + hp + 1) * 2 + 1))
                            scores(h + 1, 1 - u, kt)
                        if kt:
                            values(1, kt - 1)
                    values(1, NT1 - 1)

                rotary(b * PAIRS * PER_PAIR, 0, 0)
                project(b * PAIRS * PER_PAIR, NPE, 0)
                pe.wait_ge(sh_read.sem, sh_read.at(b * PAIRS * PER_PAIR + START - 1))
                pe.wait_ge(qplo_ok.sem, qplo_ok.at(b * PAIRS * 2 + 1))
                for i in range(4):
                    scores(0, 0, i)
                with pe.Fori(0, PAIRS - 1) as hp:
                    for u in range(2):
                        head_step(hp, u, False)
                for u in range(2):
                    head_step(PAIRS - 1, u, True)
                barrier(pe, 4 + 2 * b)

                def head_rows(h, j, first):
                    pe.wait_ge(olo_ok.sem, olo_ok.at(b * H + h))
                    pe.wait_ge(owlo_ok.sem, owlo_ok.at(b * H + h))
                    for t in range(NT):
                        last = three(pe, banks[:, t, :], cut(oTr, slice(None), j, slice(t * P, t * P + P)), cut(ow, slice(None), j), first, False)
                    last.then_inc(o_mm.sem, o_mm.step)

                head_rows(0, 0, True)
                head_rows(1, 1, False)
                with pe.Fori(1, H // 2) as hp:
                    for j in range(2):
                        head_rows(hp * 2 + j, j, False)
                barrier(pe, 5 + 2 * b)

            with pe.Fori(0, NBLK) as k:
                pe.wait_ge(xe_in.sem, xe_in.at(k))
                for a in range(2):
                    pe.wait_ge(xelo_ok.sem, xelo_ok.at(k * 2 + a, 2))
                    for c in range(KD):
                        last = pe.transpose(banks[:, a, c * P:c * P + P], xe[:, a, c * P:c * P + P], ident[:])
                    last.then_inc(xeT_full.sem, xeT_full.step)
                pe.wait_ge(xelo_ok.sem, xelo_ok.at(k * 2 + 1))

                def up(m):
                    q = m % 2
                    pe.wait_ge(wgulo_ok.sem, wgulo_ok.at(k * KM + m))
                    pe.wait_ge(h_ok.sem, h_ok.at(k * KM + m, 2))
                    for w in range(2):
                        for c in range(KD):
                            last = three(pe, banks[:, 2 + q, w * BLK:w * BLK + BLK], cut(wgu, slice(None), q, slice(w * D + c * P, w * D + c * P + P)),
                                         cut(xeT, slice(None), c), c == 0, c == KD - 1)
                    last.then_inc(gu_full.sem, gu_full.step)

                def down_rows(m):
                    q = m % 2
                    pe.wait_ge(hlo_ok.sem, hlo_ok.at(k * KM + m))
                    pe.wait_ge(wdnlo_ok.sem, wdnlo_ok.at(k * KM + m))
                    if m == 0:
                        pe.wait_ge(ye_ok.sem, ye_ok.at(k, 1))
                    for a in range(2):
                        last = three(pe, banks[:, 6 + a, :], cut(hT, slice(None), q, slice(a * P, a * P + P)), cut(wdn, slice(None), q), m == 0, m == KM - 1)
                    last.then_inc(down.sem, down.step)

                up(0)
                for m in range(1, KM):
                    up(m)
                    down_rows(m - 1)
                down_rows(KM - 1)
            barrier(pe, 8)


def tables():
    f32 = np.float32
    inv = 1.0 / 10000.0 ** (np.arange(0, ROPE, 2, dtype=f32) / ROPE)
    ang = np.outer(np.arange(S, dtype=f32), inv).astype(f32)
    cos, sin = np.cos(ang).astype(f32), np.sin(ang).astype(f32)
    c4, s4 = np.tile(cos.T, (4, 1)), np.tile(sin.T, (4, 1))
    sign = np.where(np.arange(P) < 64, 1.0, -1.0).astype(f32)[:, None]
    turns = ((np.arange(P) // HALF) % 2 == 0)[:, None]
    k, q = np.arange(P)[None, :], np.arange(P)[:, None]
    return {
        "ident": np.eye(P, dtype=f32),
        "causal": np.where(k <= q, 0.0, MASKED).astype(f32),
        "upper": (q < k).astype(f32),
        "ones": np.ones((P, P), f32),
        "rope_c": np.ascontiguousarray(c4),
        "rope_s": np.ascontiguousarray(s4 * sign),
        "idx_c": np.where(turns, c4, 1.0).astype(f32),
        "nat_c": np.ascontiguousarray(cos.reshape(NT, P, HALF).transpose(1, 0, 2)),
        "nat_s": np.ascontiguousarray(sin.reshape(NT, P, HALF).transpose(1, 0, 2)),
    }


def kernel(**inputs):
    import concourse.bacc as bacc
    from concourse.bass_utils import run_bass_kernel_spmd

    g = {k.replace("L0_attn_", "").replace("L0_ffn_", ""): np.asarray(v) for k, v in inputs.items()}
    cc = np.ascontiguousarray

    def by_chunks(w, k):
        return cc(w.reshape(k, P, -1).transpose(1, 0, 2))

    wa = np.concatenate([g["q_a_w"].T, g["kv_a_w"].T, g["idx_wk_w"].T, g["idx_wproj_w"].T, g["gate_w"]], axis=1)
    qb = g["q_b_w"].reshape(H, NOPE + ROPE, QR)
    qn = qb[:, :NOPE, :].transpose(0, 2, 1).reshape(H, KQ, P, NOPE).transpose(0, 2, 1, 3).reshape(H, P, KQ * NOPE)
    qp = qb[:, NOPE:, :].reshape(PAIRS, 2, 2, HALF, QR).transpose(0, 2, 1, 3, 4).reshape(PAIRS, P, QR)
    qp = qp.transpose(0, 2, 1).reshape(PAIRS, KQ, P, P).transpose(0, 2, 1, 3)
    kvb = g["kv_b_w"].reshape(H, NOPE + VD, KVR).transpose(0, 2, 1)
    wh = np.concatenate([qn, kvb], axis=2)
    iq = g["idx_wq_b_w"].reshape(H, 4, HALF, QR)[:, [0, 2, 1, 3]].reshape(H, P, QR)
    wi = iq.transpose(0, 2, 1).reshape(H, KQ, P, P).transpose(0, 2, 1, 3)
    up = [g[w].reshape(NE, KD, P, KM, P).transpose(0, 3, 2, 1, 4).reshape(NE * KM, P, D) for w in ("w1", "w3")]
    arrays = {
        "x": g["hidden_states"],
        "wa": by_chunks(wa, KD),
        "wi": cc(wi),
        "wh": cc(wh),
        "wp": cc(qp),
        "ow": cc(g["o_w"].T.reshape(H, VD, D)),
        "we": cc(np.concatenate(up + [g["w2"].reshape(NE * KM, P, D)], axis=2)),
        "kn_w": cc(np.broadcast_to(g["idx_kn_w"], (P, ID))),
        "kn_b": cc(np.broadcast_to(g["idx_kn_b"], (P, ID))),
        "q_ln": cc(g["q_a_ln_w"].reshape(KQ, P).T),
        "kv_ln": cc(g["kv_a_ln_w"].reshape(P, 1)),
        **tables(),
    }
    nc = bacc.Bacc("TRN2", target_bir_lowering=False, num_devices=1)
    io = {n: nc.dram_tensor(f"in_{n}", a.shape, F32, kind="ExternalInput").ap() for n, a in arrays.items()}
    io["out"] = nc.dram_tensor("out_0", (B, S, D), F32, kind="ExternalOutput").ap()
    build(nc, io)
    r = run_bass_kernel_spmd(nc, [{f"in_{n}": a for n, a in arrays.items()}], core_ids=[0])
    return r.results[0]["out_0"]
```

```python
import numpy as np
import concourse.bass as bass
from concourse import mybir
from contextlib import ExitStack

F32 = mybir.dt.float32
F32R = mybir.dt.float32r
I32 = mybir.dt.int32
U32 = mybir.dt.uint32
ALU = mybir.AluOpType
ACT = mybir.ActivationFunctionType
AX = mybir.AxisListType

P = 128
B, S, D = 2, 1024, 512
T = B * S
NT = S // P
KD = D // P
H, NOPE, ROPE, VD = 16, 128, 64, 128
QR, KVR = 384, 128
KQ = QR // P
ID = 128
TOPK = 128
HALF = ROPE // 2
SCALE = float(NOPE + ROPE) ** -0.5
EPS_LN, EPS_RMS = 1e-5, 1e-6
NE, MF = 8, 1792
KM = MF // P
CQ, CKV, CKP, CIK, CIW, CLG = 0, 384, 512, 576, 704, 720
NA = 728
NB = NA - QR
BLK = 256
NBLK = (2 * T - NE) // BLK + NE
ROWS = NBLK * BLK
MASKED = -1.0e30
TAKEN = -3.0e38
EXT = [(i + 1) * P for i in range(NT)]
OFF = [sum(EXT[:i]) for i in range(NT + 1)]
PAIRS = H // 2
NEXT_ROWS = 8
NMIX = 4
NWR = 7
SLAB = 206 * 1024
RT_SHIFTED, RT_MARKED = 1, 14
SCORE_BANKS = (0, 2, 6)
ROUNDS = TOPK // 8
NPE, NPR, NT0, NT1 = 2, 6, 4, 8
START = NPE + NPR
PER_PAIR = NPE + 2 * (NPR + NT0 + NT1)
FIRST_TILES, LAST_TILES = (1, 2, 3, 4, 5), (6, 7)


PROJECTIONS = (2, 6, 0, 7, 3, 1, 4, 5), (2, 0, 3, 1, 4, 5)
ROTARY = 6
SCORES_AT = (5, 6, 8, 9), (3, 5, 6, 7)
EXPS_AT = (6, 7, 9, 10), (4, 6, 7, 8)
INVERSES_AT = (7, 8, 10, 11), (5, 7, 8, 9)


def index_slot(u, i):
    at = u * (NT - 1) + i - 1
    return at % 3, 2 if at < 2 else 3


def shared_bank(u, o):
    return 4 + (u * (NT0 + NPR + NT1) + o) % 3


def bank_use(u, o):
    return 2 if u == 0 and o < 2 else 3


def first_group(b, hp, u):
    return b * PAIRS * PER_PAIR + START + hp * PER_PAIR + u * (NT0 + NPR + NT1)


def split_group(b, hp, u):
    each = PER_PAIR - NPE
    return b * PAIRS * each + NPR + hp * each + u * (NT0 + NPR + NT1)


class Ev:

    def __init__(self, sem, credit=0, step=1):
        self.sem, self.credit, self.step = sem, credit, step

    def at(self, n, back=0):
        return (n - (back - 1 - self.credit)) * self.step


def build(nc, io):
    ctx = ExitStack()
    with ctx:
        evs = {"act": [], "dve": [], "pool": [], "pe": [], "sp": []}

        def ev(name, owner, credit=0, step=1):
            e = Ev(ctx.enter_context(nc.semaphore(name)), credit, step)
            evs[owner].append(e)
            return e

        def dma_ev(name, owner, credit=0):
            return ev(name, owner, credit, 16)

        cursor = [(nc.sbuf_base + 31) // 32 * 32]
        ctx.enter_context(nc.sbuf_tensor("slab", [P, SLAB // 4], F32))

        def place(name, shape, dt=F32):
            t = nc.alloc_sbuf_tensor_at(name, shape, dt, offset=cursor[0])
            cursor[0] += (int(np.prod(shape[1:])) * 4 + 31) // 32 * 32
            return t

        def pair(name, shape):
            return place(name + "_hi", shape, F32R), place(name + "_lo", shape, F32R)

        ident = place("ident", [P, P])
        causal = place("causal", [P, P])
        upper = place("upper", [P, P])
        ones = place("ones", [P, P])
        rope_c = place("rope_c", [P, S])
        rope_s = place("rope_s", [P, S])
        nat_c = place("nat_c", [P, NT, HALF])
        nat_s = place("nat_s", [P, NT, HALF])
        kn_w = place("kn_w", [P, ID])
        kn_b = place("kn_b", [P, ID])
        q_ln = place("q_ln", [P, KQ])
        kv_ln = place("kv_ln", [P, 1])
        eps_ln = place("eps_ln", [P, 1])
        eps_rms = place("eps_rms", [P, 1])
        logits = place("logits", [P, B * NT, NE])
        iw = place("iw", [P, NT, H])
        m8 = place("m8", [P, NT, 8])
        slots = place("slots", [P, 2, B * NT], I32)
        gates = place("gates", [P, 2, B * NT])
        slot_now = place("slot_now", [P, 2, 2], I32)
        owner = place("owner", [1, NBLK], I32)
        iota8 = place("iota8", [P, NE])
        lim8 = place("lim8", [P, NE])
        iotab = place("iotab", [P, NBLK])
        BATCH = cursor[0]
        qrT = pair("qrT", [P, KQ, S])
        ckvT = pair("ckvT", [P, S])
        kpT = pair("kpT", [P, 2, S])
        ikT = pair("ikT", [P, S])
        scores_of = [place(f"acc{b}", [P, OFF[NT]]) for b in range(B)]

        wh_raw = place("wh_raw", [P, 640])
        wp_raw = place("wp_raw", [P, KQ, P])
        wh = pair("wh", [P, 640])
        wp = pair("wp", [P, KQ, P])
        REGION = cursor[0]
        const_tiles = [("ident", ident), ("q_ln", q_ln), ("kv_ln", kv_ln), ("nat_c", nat_c), ("nat_s", nat_s), ("kn_w", kn_w),
                       ("kn_b", kn_b), ("rope_c", rope_c), ("rope_s", rope_s), ("causal", causal), ("upper", upper), ("ones", ones)]
        EARLY = 7

        x_sb = place("x_sb", [P, 2, D])
        xn = place("xn", [P, 2, D])
        xT = pair("xT", [P, 2, D])
        ln_st = place("ln_st", [P, 2, 6])
        ln_mv = place("ln_mv", [P, 2, 2])
        ln_sd = place("ln_sd", [P, 2, 1])
        ln_r = place("ln_r", [P, 2, 1])
        junk = place("junk", [P, 2, QR])
        junk2 = place("junk2", [P, 2, KVR])
        bs = place("bs", [P, 2, NB])
        ssq = place("ssq", [P, 2, 2])
        ik_st = place("ik_st", [P, 2, 6])
        ik_mv = place("ik_mv", [P, 2, 2])
        sd3 = place("sd3", [P, 2, 3])
        r3 = place("r3", [P, 2, 3])
        nat_q = place("nat_q", [P, 4, QR + KVR])
        nat_k = place("nat_k", [P, 4, 3, P])
        ikn = place("ikn", [P, ID])
        rk1 = place("rk1", [P, 2, HALF])
        rk2 = place("rk2", [P, 2, HALF])
        ri1 = place("ri1", [P, 2, HALF])
        ri2 = place("ri2", [P, 2, HALF])
        zero = place("zero", [P, 2, D])
        wa_raw = place("wa_raw", [P, KD, NA])
        WA = cursor[0]
        wa = pair("wa", [P, KD, NA])
        wi_raw = place("wi_raw", [P, 2, KQ, P])
        wi = pair("wi", [P, 2, KQ, P])

        cursor[0] = REGION
        iy = place("iy", [P, 2, 512])
        scaled = place("scaled", [P, 512])
        idx_c = place("idx_c", [P, S])
        turned = place("turned", [P, 512])
        iqT = pair("iqT", [P, 2, S])
        relu = place("relu", [P, 3, S])
        r_e = place("r_e", [P, B * NT, NE])
        r_t = place("r_t", [P, B * NT])
        r_m = place("r_m", [P, B * NT, 8])
        r_i = place("r_i", [P, B * NT, 8], U32)
        r_if = place("r_if", [P, B * NT, 8])
        r_oh = place("r_oh", [P, 2, B * NT, NE])
        r_mk = place("r_mk", [P, B * NT, NE])
        r_rank = place("r_rank", [P, B * NT, NE])
        r_a = place("r_a", [P, B * NT, NE])
        r_b = place("r_b", [P, B * NT, NE])
        r_cnt = place("r_cnt", [P, NE, NE])
        r_n = place("r_n", [P, 3, NE])
        r_sl = place("r_sl", [P, 2, B * NT])
        r_ow = place("r_ow", [P, NBLK, NE])
        r_of = place("r_of", [P, NBLK])

        assert cursor[0] <= WA

        cursor[0] = REGION
        qn = pair("qn", [P, S])
        qp = pair("qp", [P, S])
        kT = pair("kT", [P, S])
        v_ = pair("v", [P, 2, NT, VD])
        py = place("py", [P, 2, 512])
        p_scaled = place("p_scaled", [P, 512])
        p_turned = place("p_turned", [P, 512])
        probs = place("probs", [P, OFF[NT]])
        nmax = place("nmax", [P, NT])
        row_sum = place("row_sum", [P, NT])
        rinv = place("rinv", [P, NT])
        PT = pair("PT", [P, 3, 512])
        oT = place("oT", [P, 2, 512])
        rows = place("rows", [P, 2, D])

        cursor[0] = REGION
        oT_raw = place("oT_raw", [P, 2, S])
        ow_raw = place("ow_raw", [P, 2, D])
        oTr = pair("oTr", [P, 2, S])
        ow = pair("ow", [P, 2, D])
        xo = place("xo", [P, NT, D])
        po = place("po", [P, NT, D])

        cursor[0] = BATCH
        xe = place("xe", [P, 2, D])
        xeT = pair("xeT", [P, 2 * KD, BLK])
        we = place("we", [P, NWR, 3 * D])
        wgu = pair("wgu", [P, 2, 2 * D])
        wdn = pair("wdn", [P, 2, D])
        assert cursor[0] <= REGION
        sg = place("sg", [P, 2, BLK])
        hf = place("hf", [P, 2, BLK])
        hT = pair("hT", [P, 2, BLK])
        ye = place("ye", [P, 2, D])
        g_a = place("g_a", [P, NMIX, D])
        g_b = place("g_b", [P, NMIX, D])
        part_sb = place("part_sb", [P, NMIX, D])
        mix = place("mix", [P, NMIX, D])
        fin = place("fin", [P, NMIX, D])
    
        def projection(c, u, part):
            if c < 4:
                return (qn if c < 2 else kT)[part][:, c % 2 * 512:c % 2 * 512 + 512]
            return v_[part][:, u, (c - 4) * 4:(c - 4) * 4 + 4, :]

        banks = ctx.enter_context(nc.psum_tensor("banks", [P, 8, 512]))

        xn_d = nc.dram_tensor("xn_d", (B * NT, P, D), F32, kind="Internal").ap()
        oT_d = nc.dram_tensor("oT_d", (B, H, P, S), F32, kind="Internal").ap()
        part_d = nc.dram_tensor("part_d", (B * NT, P, D), F32, kind="Internal").ap()
        kept_d = [nc.dram_tensor(f"kept_d{i}", (B, P, n), F32R, kind="Internal").ap() for i, n in enumerate((KQ * S, S, 2 * S) * 2)]
        xs_d = nc.dram_tensor("xs_d", (ROWS, D), F32, kind="Internal").ap()
        ys_d = nc.dram_tensor("ys_d", (ROWS, D), F32, kind="Internal").ap()
        xs_blk = xs_d.rearrange("(k a p) d -> k p a d", p=P, a=2)
        ys_blk = ys_d.rearrange("(k a p) d -> k p a d", p=P, a=2)
        x_t = io["x"].rearrange("b (t p) d -> (b t) p d", p=P)
        out_t = io["out"].rearrange("b (t p) d -> (b t) p d", p=P)

        kept = [t[0][:].rearrange("p a c -> p (a c)") if len(t[0].shape) == 3 else t[0][:] for t in (qrT, ckvT, kpT)]
        kept += [t[1][:].rearrange("p a c -> p (a c)") if len(t[1].shape) == 3 else t[1][:] for t in (qrT, ckvT, kpT)]

        phase_end = ctx.enter_context(nc.semaphore("phase_end"))
        consts = dma_ev("consts", "sp")
        late_consts = dma_ev("late_consts", "sp")
        wa_in = dma_ev("wa_in", "sp")
        x_in = [dma_ev(f"x_in{j}", "sp") for j in range(2)]
        idx_c_in = dma_ev("idx_c_in", "sp")
        wi_in = [dma_ev(f"wi_in{j}", "sp") for j in range(2)]
        wh_in = dma_ev("wh_in", "sp")
        kept_out = dma_ev("kept_out", "sp")
        wp_in = dma_ev("wp_in", "sp")
        oT_out = [dma_ev(f"oT_out{j}", "sp", 1) for j in range(2)]
        o_in = [dma_ev(f"o_in{j}", "sp") for j in range(2)]
        ow_in = [dma_ev(f"ow_in{j}", "sp") for j in range(2)]
        xo_in = dma_ev("xo_in", "sp")
        zero_out = dma_ev("zero_out", "sp")
        row_in = [dma_ev(f"row_in{j}", "sp") for j in range(2)]
        xe_in = dma_ev("xe_in", "sp")
        we_in = [dma_ev(f"we_in{j}", "sp") for j in range(NWR)]
        part_in = [dma_ev(f"part_in{j}", "sp") for j in range(NMIX)]
        wa_hi_ok = ev("wa_hi_ok", "act")
        deviation = ev("deviation", "act")
        xn_out = [dma_ev(f"xn_out{j}", "act", 1) for j in range(2)]
        xhi_ok = ev("xhi_ok", "act")
        squares = ev("squares", "act")
        roots = ev("roots", "act")
        nhi_ok = ev("nhi_ok", "act")
        wi_hi_ok = ev("wi_hi_ok", "act")
        iqhi_ok = ev("iqhi_ok", "act")
        relu_ok = ev("relu_ok", "act", 3)
        wh_hi_ok = ev("wh_hi_ok", "act")
        wp_hi_ok = ev("wp_hi_ok", "act")
        qphi_ok = ev("qphi_ok", "act")
        sh_hi = ev("sh_hi", "act")
        exps = ev("exps", "act")
        last_norm = ev("last_norm", "act")
        oT_read = ev("oT_read", "act", 2)
        ohi_ok = ev("ohi_ok", "act")
        owhi_ok = ev("owhi_ok", "act")
        part_out = dma_ev("part_out", "act")
        rt_exp = ev("rt_exp", "act")
        wguhi_ok = ev("wguhi_ok", "act")
        wdnhi_ok = ev("wdnhi_ok", "act")
        xehi_ok = ev("xehi_ok", "act")
        silu_ok = ev("silu_ok", "act")
        hhi_ok = ev("hhi_ok", "act")
        ye_ok = ev("ye_ok", "act", 1)
        ye_out = dma_ev("ye_out", "act", 1)
        fin_out = [dma_ev(f"fin_out{j}", "act", 1) for j in range(NMIX)]
        eps_ok = ev("eps_ok", "dve")
        stats = ev("stats", "dve")
        moments = ev("moments", "dve")
        inverse = ev("inverse", "dve")
        normed = ev("normed", "dve", 2)
        xlo_ok = ev("xlo_ok", "dve", 2)
        copied = ev("copied", "dve")
        ik_stats = ev("ik_stats", "dve")
        ik_moments = ev("ik_moments", "dve")
        inverses = ev("inverses", "dve")
        natq_ok = ev("natq_ok", "dve", 2)
        nlo_ok = ev("nlo_ok", "dve", 2)
        acc_clear = ev("acc_clear", "dve")
        i_parts = ev("i_parts", "dve", 2)
        acc_ok = ev("acc_ok", "dve", 3)
        ranks_read = ev("ranks_read", "dve")
        diag_ok = ev("diag_ok", "dve")
        top8_ok = ev("top8_ok", "dve")
        taken_ok = ev("taken_ok", "dve", NT - 1)
        mask_ok = ev("mask_ok", "dve")
        sh_read = ev("sh_read", "dve", 3)
        py_ok = ev("py_ok", "dve", 1)
        masked = ev("masked", "dve", 2)
        sums_inv = ev("sums_inv", "dve")
        olo_ok = ev("olo_ok", "dve", 2)
        po_ok = ev("po_ok", "dve")
        rt = ev("rt", "dve")
        wgulo_ok = ev("wgulo_ok", "dve", NWR)
        xelo_ok = ev("xelo_ok", "dve", 2)
        h_ok = ev("h_ok", "dve", 2)
        mix_ok = ev("mix_ok", "dve")
        fin_ok = ev("fin_ok", "dve", NMIX)
        wa_lo_ok = ev("wa_lo_ok", "pool")
        nat_clear = ev("nat_clear", "pool")
        key_step = [ev(f"key_step{j}", "pool") for j in range(5)]
        natk_ok = ev("natk_ok", "pool", 2)
        wi_lo_ok = ev("wi_lo_ok", "pool", 2)
        iqlo_ok = ev("iqlo_ok", "pool", 2)
        iy_ok = ev("iy_ok", "pool", 1)
        wh_lo_ok = ev("wh_lo_ok", "pool", 1)
        wp_lo_ok = ev("wp_lo_ok", "pool", 1)
        qplo_ok = ev("qplo_ok", "dve", 2)
        p_norm = ev("p_norm", "pool")
        owlo_ok = ev("owlo_ok", "pool", 2)
        zero_ok = ev("zero_ok", "pool")
        rt_pool = ev("rt_pool", "pool")
        row_sc = [dma_ev(f"row_sc{j}", "pool") for j in range(2)]
        wdnlo_ok = ev("wdnlo_ok", "pool", NWR)
        kept_in = dma_ev("kept_in", "pool")
        slot_set = ev("slot_set", "pool")
        hlo_ok = ev("hlo_ok", "dve", 2)
        g_in = [dma_ev(f"g_in{j}", "pool") for j in range(NMIX)]
        xt_full = ev("xt_full", "pe", 2)
        projected = ev("projected", "pe")
        nt_full = ev("nt_full", "pe", 4)
        iq_full = ev("iq_full", "pe", 4)
        is_full = ev("is_full", "pe", 1)
        sh_full = ev("sh_full", "pe")
        sc_full = ev("sc_full", "pe")
        pv_done = ev("pv_done", "pe", 3)
        o_mm = ev("o_mm", "pe", 2 * NT)
        rt_pe = ev("rt_pe", "pe")
        xeT_full = ev("xeT_full", "pe", 2)
        gu_full = ev("gu_full", "pe")
        down = ev("down", "pe", 2)

        spare = {}

        def in_register(eng, value):
            if eng not in spare:
                spare[eng] = eng.alloc_register(name="behind")
            eng.reg_mov(spare[eng], value)
            return spare[eng]

        block = ctx.enter_context(nc.Block())

        def barrier(eng, k):
            eng.drain().then_inc(phase_end, 1)
            eng.wait_ge(phase_end, 5 * (k + 1))

        def three(pe, out, left, right, start=True, stop=True):
            pe.matmul(out, left[0], right[0], start=start, stop=False, skip_group_check=True)
            pe.matmul(out, left[0], right[1], start=False, stop=False, skip_group_check=True)
            return pe.matmul(out, left[1], right[0], start=False, stop=stop, skip_group_check=True)

        def cut(parts, *where):
            return parts[0][where], parts[1][where]

        def parity(k):
            return slice(k % 2 * KD, k % 2 * KD + KD) if isinstance(k, int) else bass.ds(k % 2 * KD, KD)

        def at(x):
            return x if isinstance(x, int) else bass.ds(x, 1)

        def scores_psum(r, width):
            first = SCORE_BANKS[r]
            return banks[:, first:first + 2, :].rearrange("p a c -> p (a c)")[:, 0:width]

        def plain(part):
            return part.bitcast(F32)

        @block.sync
        def _(sp):
            for e in evs["sp"]:
                if e.credit:
                    sp.sem_inc(e.sem, e.credit * e.step)

            def first_weights():
                sp.dma_start(wp_raw[:], io["wp"][0]).then_inc(wp_in.sem, wp_in.step)
                sp.dma_start(wh_raw[:], io["wh"][0]).then_inc(wh_in.sem, wh_in.step)

            def block_loads(k, expert, chunks, last):
                for m in chunks:
                    r = m % NWR
                    sp.wait_ge(wgulo_ok.sem, wgulo_ok.at(k * KM + m, NWR))
                    sp.wait_ge(wdnlo_ok.sem, wdnlo_ok.at(k * KM + m, NWR))
                    sp.dma_start(we[:, r, :], io["we"][expert * KM + m]).then_inc(we_in[r].sem, we_in[r].step)
                    if m == NWR and not last:
                        sp.wait_ge(xeT_full.sem, xeT_full.at(k * 2 + 1))
                        sp.dma_start(xe[:], xs_blk[k + 1]).then_inc(xe_in.sem, xe_in.step)

            for name, tile in const_tiles[:EARLY]:
                sp.dma_start(tile[:], io[name]).then_inc(consts.sem, consts.step)
            for j in range(2):
                sp.dma_start(x_sb[:, j, :], x_t[j]).then_inc(x_in[j].sem, x_in[j].step)
            sp.dma_start(wa_raw[:], io["wa"]).then_inc(wa_in.sem, wa_in.step)
            for name, tile in const_tiles[EARLY:]:
                sp.dma_start(tile[:], io[name]).then_inc(late_consts.sem, late_consts.step)
            for b in range(B):
                with sp.Fori(1 if b == 0 else 0, NT // 2) as it:
                    for j in range(2):
                        n = b * NT + it * 2 + j
                        sp.wait_ge(normed.sem, normed.at(n, 2))
                        sp.dma_start(x_sb[:, j, :], x_t[n]).then_inc(x_in[j].sem, x_in[j].step)
                if b == 0:
                    sp.wait_ge(zero_ok.sem, zero_ok.at(0))
                    with sp.Fori(0, NBLK) as k:
                        sp.dma_start(xs_blk[k], zero[:]).then_inc(zero_out.sem, zero_out.step)
                    sp.wait_ge(zero_out.sem, zero_out.at(NBLK - 1))
                    sp.wait_ge(late_consts.sem, late_consts.at(len(const_tiles) - EARLY - 1))
                for u in range(2):
                    sp.dma_start(wi_raw[:, u], io["wi"][u]).then_inc(wi_in[u].sem, wi_in[u].step)
                barrier(sp, 2 * b)
                sp.dma_start(idx_c[:], io["idx_c"]).then_inc(idx_c_in.sem, idx_c_in.step)
                for part, there in zip(kept, kept_d):
                    sp.dma_start(plain(there[b]), plain(part)).then_inc(kept_out.sem, kept_out.step)
                with sp.Fori(0, PAIRS - 1) as hp:
                    for u in range(2):
                        sp.wait_ge(wi_lo_ok.sem, wi_lo_ok.at(b * H + hp * 2 + u))
                        sp.dma_start(wi_raw[:, u], io["wi"][hp * 2 + u + 2]).then_inc(wi_in[u].sem, wi_in[u].step)
                sp.wait_ge(kept_out.sem, kept_out.at((b + 1) * len(kept) - 1))
                if b == B - 1:
                    first_weights()
                barrier(sp, 2 * b + 1)
            for b in range(B):
                sp.wait_ge(wh_lo_ok.sem, wh_lo_ok.at(b * H))
                sp.dma_start(wh_raw[:], io["wh"][1]).then_inc(wh_in.sem, wh_in.step)
                if b == 0:
                    for u in range(2):
                        sp.dma_start(rows[:, u, :], xn_d[u]).then_inc(row_in[u].sem, row_in[u].step)

                def head_loads(hp):
                    for j in range(2):
                        h = hp * 2 + j
                        sp.wait_ge(olo_ok.sem, olo_ok.at(b * H + h, 2))
                        sp.wait_ge(owlo_ok.sem, owlo_ok.at(b * H + h, 2))
                        sp.dma_start(oT_raw[:, j, :], oT_d[b, h]).then_inc(o_in[j].sem, o_in[j].step)
                        sp.dma_start(ow_raw[:, j, :], io["ow"][h]).then_inc(ow_in[j].sem, ow_in[j].step)

                def head_step(hp, u, last):
                    h = hp * 2 + u
                    if u == 0 and not last:
                        sp.wait_ge(wp_lo_ok.sem, wp_lo_ok.at(b * PAIRS + hp))
                        sp.dma_start(wp_raw[:], io["wp"][hp + 1]).then_inc(wp_in.sem, wp_in.step)
                    if not last:
                        sp.wait_ge(wh_lo_ok.sem, wh_lo_ok.at(b * H + h + 1))
                        sp.dma_start(wh_raw[:], io["wh"][h + 2]).then_inc(wh_in.sem, wh_in.step)
                    for s in range(2):
                        if last and u == 1 and s == 1:
                            sp.wait_ge(sc_full.sem, sc_full.at((b * H + H) * NT - 1))
                            for half in range(2):
                                sp.wait_ge(oT_out[half].sem, oT_out[half].at(b * H + 1))
                            head_loads(0)
                        sp.wait_ge(oT_read.sem, oT_read.at((b * H + h) * 2 + s))
                        sp.dma_start(oT_d[b, h, :, s * 512:s * 512 + 512], oT[:, s, :]).then_inc(oT_out[s].sem, oT_out[s].step)
                    if b == 0 and not last:
                        sp.wait_ge(row_sc[u].sem, row_sc[u].at(hp * 2 + 1))
                        sp.dma_start(rows[:, u, :], xn_d[h + 2]).then_inc(row_in[u].sem, row_in[u].step)

                with sp.Fori(0, PAIRS - 1) as hp:
                    for u in range(2):
                        head_step(hp, u, False)
                for u in range(2):
                    head_step(PAIRS - 1, u, True)
                for s in range(2):
                    sp.wait_ge(oT_out[s].sem, oT_out[s].at(b * H + H - 1))
                barrier(sp, 4 + 2 * b)

                with sp.Fori(1, H // 2) as hp:
                    head_loads(hp)
                sp.dma_start(xo[:], io["x"][b].rearrange("(t p) d -> p t d", p=P)).then_inc(xo_in.sem, xo_in.step)
                if b == B - 1:
                    expert = sp.value_load(owner[0:1, 0:1], min_val=0, max_val=NE - 1)
                    sp.dma_start(xe[:], xs_blk[0]).then_inc(xe_in.sem, xe_in.step)
                    block_loads(0, expert, range(NWR), False)
                if b < B - 1:
                    first_weights()
                barrier(sp, 5 + 2 * b)
            block_loads(0, expert, range(NWR, KM), False)
            with sp.Fori(1, NBLK - 1) as k:
                expert = sp.value_load(owner[0:1, bass.ds(k, 1)], min_val=0, max_val=NE - 1)
                block_loads(k, expert, range(KM), False)
            expert = sp.value_load(owner[0:1, NBLK - 1:NBLK], min_val=0, max_val=NE - 1)
            block_loads(NBLK - 1, expert, range(KM), True)
            for m in range(2):
                sp.wait_ge(wgulo_ok.sem, wgulo_ok.at(NBLK * KM + m, NWR))
                sp.wait_ge(wdnlo_ok.sem, wdnlo_ok.at(NBLK * KM + m, NWR))
                sp.dma_start(we[:, m, :], io["we"][m]).then_inc(we_in[m].sem, we_in[m].step)
            barrier(sp, 8)
            with sp.Fori(0, B * NT // NMIX) as it:
                for j in range(NMIX):
                    n = it * NMIX + j
                    sp.wait_ge(fin_ok.sem, fin_ok.at(n, NMIX))
                    sp.dma_start(part_sb[:, j, :], part_d[n]).then_inc(part_in[j].sem, part_in[j].step)

        @block.scalar
        def _(act):
            for e in evs["act"]:
                if e.credit:
                    act.sem_inc(e.sem, e.credit * e.step)
            act.wait_ge(eps_ok.sem, eps_ok.at(0))
            act.wait_ge(consts.sem, consts.at(EARLY - 1))
            def pair_weights_hi(n):
                act.wait_ge(wp_in.sem, wp_in.at(n))
                act.activation(wp[0][:], wp_raw[:], ACT.Copy).then_inc(wp_hi_ok.sem, wp_hi_ok.step)

            def head_weights_hi(n):
                act.wait_ge(wh_in.sem, wh_in.at(n))
                act.activation(wh[0][:], wh_raw[:], ACT.Copy).then_inc(wh_hi_ok.sem, wh_hi_ok.step)

            for b in range(B):
                if b == 0:
                    act.wait_ge(wa_in.sem, wa_in.at(0))
                    act.activation(wa[0][:], wa_raw[:], ACT.Copy).then_inc(wa_hi_ok.sem, wa_hi_ok.step)
                def normalise(it):
                    for j in range(2):
                        n = b * NT + it * 2 + j
                        act.wait_ge(moments.sem, moments.at(n))
                        act.activation(ln_sd[:, j, :], ln_mv[:, j, 1:2], ACT.Sqrt, bias=eps_ln[:, 0:1]).then_inc(deviation.sem, deviation.step)
                        act.wait_ge(normed.sem, normed.at(n))
                        act.dma_start(xn_d[n], xn[:, j, :]).then_inc(xn_out[j].sem, xn_out[j].step)

                def turn(it):
                    for j in range(2):
                        n = b * NT + it * 2 + j
                        act.wait_ge(xt_full.sem, xt_full.at(n))
                        act.activation(xT[0][:, j, :], banks[:, j, :], ACT.Copy).then_inc(xhi_ok.sem, xhi_ok.step)

                def norms(it, tiles=(0, 1)):
                    for j in tiles:
                        n = b * NT + it * 2 + j
                        act.wait_ge(projected.sem, projected.at(n))
                        act.activation(junk[:, j, :], banks[:, 2 + 2 * j, 0:QR], ACT.Square, accum_out=ssq[:, j, 0:1])
                        act.wait_ge(copied.sem, copied.at(n))
                        act.activation(junk2[:, j, :], bs[:, j, 0:KVR], ACT.Square, accum_out=ssq[:, j, 1:2]).then_inc(squares.sem, squares.step)
                        act.wait_ge(ik_moments.sem, ik_moments.at(n))
                        act.wait_ge(squares.sem, squares.at(n))
                        act.activation(sd3[:, j, 0:1], ssq[:, j, 0:1], ACT.Sqrt, bias=eps_rms[:, 0:1], scale=1.0 / QR)
                        act.activation(sd3[:, j, 1:2], ssq[:, j, 1:2], ACT.Sqrt, bias=eps_rms[:, 0:1], scale=1.0 / KVR)
                        act.activation(sd3[:, j, 2:3], ik_mv[:, j, 1:2], ACT.Sqrt, bias=eps_rms[:, 0:1]).then_inc(roots.sem, roots.step)

                def turn_normed(it, tiles=(0, 1)):
                    for j in tiles:
                        n = b * NT + it * 2 + j
                        cols = bass.ds((it * 2 + j) * P, P)
                        act.wait_ge(nt_full.sem, nt_full.at(n))
                        for c in range(KQ):
                            act.activation(qrT[0][:, c, cols], banks[:, 6, c * P:c * P + P], ACT.Identity, scale=q_ln[:, c:c + 1])
                        act.activation(ckvT[0][:, cols], banks[:, 6, QR:QR + KVR], ACT.Identity, scale=kv_ln[:, 0:1])
                        act.activation(kpT[0][:, :, cols], banks[:, 7, 0:2 * P].rearrange("p (a c) -> p a c", a=2), ACT.Copy)
                        act.activation(ikT[0][:, cols], banks[:, 7, 2 * P:3 * P], ACT.Copy).then_inc(nhi_ok.sem, nhi_ok.step)

                normalise(0)
                for it in range(NT // 2):
                    turn(it)
                    if it + 1 < NT // 2:
                        normalise(it + 1)
                    if b == 0:
                        norms(it)
                        if it:
                            turn_normed(it - 1)
                    else:
                        for j in range(2):
                            if it:
                                turn_normed(it - 1, (j,))
                            norms(it, (j,))
                turn_normed(NT // 2 - 1)
                for j in range(2):
                    act.wait_ge(xn_out[j].sem, xn_out[j].at(b * (NT // 2) + NT // 2 - 1))
                for u in range(2):
                    act.wait_ge(wi_in[u].sem, wi_in[u].at(b * PAIRS))
                    act.activation(wi[0][:, u], wi_raw[:, u], ACT.Copy).then_inc(wi_hi_ok.sem, wi_hi_ok.step)
                barrier(act, 2 * b)

                def queries_hi(q, u, c):
                    act.wait_ge(iy_ok.sem, iy_ok.at(q * 2 + c))
                    act.activation(iqT[0][:, u, c * 512:c * 512 + 512], iy[:, c, :], ACT.Copy).then_inc(iqhi_ok.sem, iqhi_ok.step)

                def index_step(hp, u, last):
                    q = b * H + hp * 2 + u
                    for i in range(1, NT):
                        n = q * (NT - 1) + i - 1
                        r, ago = index_slot(u, i)
                        act.wait_ge(is_full.sem, is_full.at(n))
                        act.wait_ge(acc_ok.sem, acc_ok.at(n, ago))
                        act.activation(relu[:, r, 0:EXT[i]], scores_psum(r, EXT[i]), ACT.Relu).then_inc(relu_ok.sem, relu_ok.step)
                        if i == 1 and not last:
                            act.wait_ge(wi_in[u].sem, wi_in[u].at(b * PAIRS + hp + 1))
                            act.activation(wi[0][:, u], wi_raw[:, u], ACT.Copy).then_inc(wi_hi_ok.sem, wi_hi_ok.step)
                        if i in (3, 6) and not (last and u == 1):
                            queries_hi(q + 1, 1 - u, i // 4)

                if b == B - 1:
                    act.wait_ge(rt.sem, rt.at(RT_SHIFTED))
                    act.activation(r_e[:], r_e[:], ACT.Exp).then_inc(rt_exp.sem, rt_exp.step)
                for c in range(2):
                    queries_hi(b * H, 0, c)
                with act.Fori(0, PAIRS - 1) as hp:
                    for u in range(2):
                        index_step(hp, u, False)
                for u in range(2):
                    index_step(PAIRS - 1, u, True)
                if b == B - 1:
                    pair_weights_hi(0)
                    head_weights_hi(0)
                barrier(act, 2 * b + 1)

            for b in range(B):
                def exponentials(h, i):
                    act.wait_ge(masked.sem, masked.at((b * H + h) * NT + i))
                    a = probs[:, OFF[i]:OFF[i + 1]]
                    act.activation(a, a, ACT.Exp, bias=nmax[:, i:i + 1], scale=-1.0,
                                            accum_out=row_sum[:, i:i + 1]).then_inc(exps.sem, exps.step)

                def exponentials_behind(h, u, at):
                    for i in range(4):
                        if EXPS_AT[u][i] == at:
                            exponentials(h, i)

                def normalise_last(h):
                    a = probs[:, OFF[NT - 1]:OFF[NT]]
                    act.wait_ge(sums_inv.sem, sums_inv.at((b * H + h) * NT + NT - 1))
                    act.activation(a, a, ACT.Identity, scale=rinv[:, NT - 1:NT]).then_inc(last_norm.sem, last_norm.step)

                def projections_hi(g, start, h, u, p, before=None):
                    todo = PROJECTIONS[u]
                    for at, c in enumerate(todo):
                        if c < ROTARY:
                            dst, src = projection(c, u, 0), banks[:, shared_bank(start[0], start[1] + at), :]
                            if c >= 4:
                                src = src.rearrange("p (t d) -> p t d", t=4)
                            act.wait_ge(sh_full.sem, sh_full.at(g + start[1] + at))
                            act.activation(dst, src, ACT.Copy).then_inc(sh_hi.sem, sh_hi.step)
                        if u == 0 and at in (2, 4):
                            half = at // 2 - 1
                            act.wait_ge(py_ok.sem, py_ok.at((b * PAIRS + p) * 2 + half))
                            act.activation(qp[0][:, half * 512:half * 512 + 512], py[:, half, :], ACT.Copy).then_inc(qphi_ok.sem, qphi_ok.step)
                        if at == 1 + (u == 0) and before is not None:
                            normalise_last(before)
                        exponentials_behind(h, u, at)

                def head_step(hp, u, last):
                    h, g, tail = hp * 2 + u, first_group(b, hp, u), last and u == 1

                    def block_hi(s, kt):
                        jj = 4 * s + kt
                        o = kt if s == 0 else NT0 + (0 if tail else NPR + NPE * u) + kt
                        lo = max(0, kt - 4 * s) * P
                        act.wait_ge(sh_full.sem, sh_full.at(g + o))
                        act.wait_ge(pv_done.sem, pv_done.at((b * H + h) * (NT0 + NT1) + jj, 3))
                        act.activation(PT[0][:, jj % 3, lo:512], banks[:, shared_bank(u, o), lo:512], ACT.Copy).then_inc(sh_hi.sem, sh_hi.step)

                    def out_rows(s):
                        act.wait_ge(pv_done.sem, pv_done.at((b * H + h) * (NT0 + NT1) + NT0 + NT1 * s - 1))
                        act.wait_ge(oT_out[s].sem, oT_out[s].at(b * H + h, 1))
                        act.activation(oT[:, s, :], banks[:, 7, :], ACT.Copy).then_inc(oT_read.sem, oT_read.step)

                    if not tail:
                        if u == 1:
                            pair_weights_hi(b * PAIRS + hp + 1)
                        head_weights_hi(b * H + h + 1)
                    block_hi(0, 0)
                    exponentials(h, 4)
                    block_hi(0, 1)
                    exponentials(h, 5)
                    block_hi(0, 2)
                    exponentials(h, 6)
                    block_hi(0, 3)
                    out_rows(0)
                    exponentials(h, 7)
                    if not tail:
                        projections_hi(g, (u, NT0), h + 1, 1 - u, hp + u, h)
                    else:
                        normalise_last(h)
                    for kt in range(NT1):
                        block_hi(1, kt)
                        if not tail:
                            exponentials_behind(h + 1, 1 - u, len(PROJECTIONS[1 - u]) + kt)
                    out_rows(1)

                projections_hi(first_group(b, 0, 0), (0, -START), 0, 0, 0)
                for kt in range(3):
                    exponentials_behind(0, 0, START + kt)
                with act.Fori(0, PAIRS - 1) as hp:
                    for u in range(2):
                        head_step(hp, u, False)
                for u in range(2):
                    head_step(PAIRS - 1, u, True)
                barrier(act, 4 + 2 * b)

                with act.Fori(0, H // 2) as hp:
                    for j in range(2):
                        n = b * H + hp * 2 + j
                        act.wait_ge(o_in[j].sem, o_in[j].at(b * (H // 2) + hp))
                        act.wait_ge(o_mm.sem, o_mm.at(n * NT + NT - 1, 2 * NT))
                        act.activation(oTr[0][:, j, :], oT_raw[:, j, :], ACT.Copy).then_inc(ohi_ok.sem, ohi_ok.step)
                        act.wait_ge(ow_in[j].sem, ow_in[j].at(b * (H // 2) + hp))
                        act.activation(ow[0][:, j, :], ow_raw[:, j, :], ACT.Copy).then_inc(owhi_ok.sem, owhi_ok.step)
                if b == B - 1:
                    for m in range(2):
                        act.wait_ge(we_in[m].sem, we_in[m].at(0))
                        act.activation(wgu[0][:, m, :], we[:, m, 0:2 * D], ACT.Copy).then_inc(wguhi_ok.sem, wguhi_ok.step)
                    act.activation(wdn[0][:, 0, :], we[:, 0, 2 * D:], ACT.Copy).then_inc(wdnhi_ok.sem, wdnhi_ok.step)
                for t in range(NT):
                    act.wait_ge(po_ok.sem, po_ok.at(b * NT + t))
                    act.dma_start(part_d[b * NT + t], po[:, t, :]).then_inc(part_out.sem, part_out.step)
                if b < B - 1:
                    pair_weights_hi((b + 1) * PAIRS)
                    head_weights_hi((b + 1) * H)
                act.wait_ge(part_out.sem, part_out.at((b + 1) * NT - 1))
                barrier(act, 5 + 2 * b)

            def rows_hi(k, halves=(0, 1)):
                for a in halves:
                    act.wait_ge(xeT_full.sem, xeT_full.at(k * 2 + a))
                    act.activation(xeT[0][:, parity(k), a * P:a * P + P],
                                               banks[:, a, :].rearrange("p (k t) -> p k t", k=KD), ACT.Copy).then_inc(xehi_ok.sem, xehi_ok.step)

            def inner(k, m):
                c, q = k * KM + m, m % 2
                act.wait_ge(gu_full.sem, gu_full.at(c))
                act.activation(sg[:, q, :], banks[:, 2 + q, 0:BLK], ACT.Silu).then_inc(silu_ok.sem, silu_ok.step)
                act.wait_ge(h_ok.sem, h_ok.at(c))
                act.activation(hT[0][:, q, :], hf[:, q, :], ACT.Copy).then_inc(hhi_ok.sem, hhi_ok.step)

            def up_hi(k, m):
                r = (m + 2) % NWR
                act.wait_ge(we_in[r].sem, we_in[r].at(k * (KM // NWR) + (m + 2) // NWR))
                act.activation(wgu[0][:, m % 2, :], we[:, r, 0:2 * D], ACT.Copy).then_inc(wguhi_ok.sem, wguhi_ok.step)

            def chunks(k, last):
                for m in range(KM):
                    c, q = k * KM + m, m % 2
                    if m:
                        inner(k, m)
                        up_hi(k, m)
                    act.wait_ge(down.sem, down.at(c, 1))
                    act.activation(wdn[0][:, 1 - q, :], we[:, (m + 1) % NWR, 2 * D:], ACT.Copy).then_inc(wdnhi_ok.sem, wdnhi_ok.step)
                    if m in (NEXT_ROWS + 1, NEXT_ROWS + 2) and not last:
                        rows_hi(k + 1, (m - NEXT_ROWS - 1,))
                if not last:
                    inner(k + 1, 0)
                    up_hi(k + 1, 0)
                act.wait_ge(down.sem, down.at(k * KM + KM - 1))
                act.wait_ge(ye_out.sem, ye_out.at(k, 1))
                act.activation(ye[:], banks[:, 6:8, :], ACT.Copy).then_inc(ye_ok.sem, ye_ok.step)
                act.wait_ge(ye_ok.sem, ye_ok.at(k))
                act.dma_start(ys_blk[k], ye[:]).then_inc(ye_out.sem, ye_out.step)

            rows_hi(0)
            inner(0, 0)
            up_hi(0, 0)
            with act.Fori(0, NBLK - 1) as k:
                chunks(k, False)
            chunks(NBLK - 1, True)
            act.wait_ge(ye_out.sem, ye_out.at(NBLK - 1))
            barrier(act, 8)
            with act.Fori(0, B * NT // NMIX) as it:
                for j in range(NMIX):
                    act.wait_ge(fin_ok.sem, fin_ok.at(it * NMIX + j))
                    act.dma_start(out_t[it * NMIX + j], fin[:, j, :]).then_inc(fin_out[j].sem, fin_out[j].step)
            for j in range(NMIX):
                act.wait_ge(fin_out[j].sem, fin_out[j].at(B * NT // NMIX - 1))

        @block.vector
        def _(dve):
            for e in evs["dve"]:
                if e.credit:
                    dve.sem_inc(e.sem, e.credit * e.step)
            dve.memset(eps_ln[:], EPS_LN)
            dve.memset(eps_rms[:], EPS_RMS).then_inc(eps_ok.sem, eps_ok.step)
            dve.wait_ge(consts.sem, consts.at(EARLY - 1))
            step = [0]

            def link(ins):
                step[0] += 1
                ins.then_inc(rt.sem, 1)
                dve.wait_ge(rt.sem, step[0])

            def over(ap, shape):
                return ap.broadcast_to(shape)

            NTT = B * NT
            full = [P, NTT, NE]
            def route_start():
                link(dve.tensor_reduce(r_t[:], logits[:], AX.X, ALU.max))
                link(dve.tensor_tensor(r_e[:], logits[:], over(r_t[:].unsqueeze(2), full), ALU.subtract))
                assert step[0] == RT_SHIFTED + 1
                dve.wait_ge(rt_exp.sem, rt_exp.at(0))
                link(dve.tensor_reduce(r_t[:], r_e[:], AX.X, ALU.add))
                link(dve.reciprocal(r_t[:], r_t[:]))
                link(dve.tensor_tensor(r_e[:], r_e[:], over(r_t[:].unsqueeze(2), full), ALU.mult))
                for n in range(NTT):
                    last = dve.max(r_m[:, n, :], r_e[:, n, :])
                link(last)
                for n in range(NTT):
                    last = dve.max_index(r_i[:, n, :], r_m[:, n, :], r_e[:, n, :])
                link(last)
                link(dve.tensor_tensor(r_t[:], r_m[:, :, 0], r_m[:, :, 1], ALU.add))
                link(dve.reciprocal(r_t[:], r_t[:]))
                for k in range(2):
                    link(dve.tensor_tensor(gates[:, k, :], r_m[:, :, k], r_t[:], ALU.mult))
                link(dve.tensor_copy(r_if[:], r_i[:]))
                dve.wait_ge(rt_pool.sem, rt_pool.at(0))
                for k in range(2):
                    link(dve.tensor_tensor(r_oh[:, k], over(iota8[:].unsqueeze(1), full), over(r_if[:, :, k:k + 1], full), ALU.is_equal))
                link(dve.tensor_tensor(r_mk[:], r_oh[:, 0], r_oh[:, 1], ALU.add))
                assert step[0] == RT_MARKED + 1

            def route_ranks():
                dve.wait_ge(rt_pe.sem, rt_pe.at(0))
                link(dve.tensor_copy(r_rank[:], banks[:, 6, 0:NTT * NE].rearrange("p (n e) -> p n e", e=NE)))
                link(dve.tensor_copy(r_a[:], banks[:, 7, 0:NTT * NE].rearrange("p (n e) -> p n e", e=NE)))
                dve.tensor_copy(r_t[:], r_m[:, :, 0]).then_inc(ranks_read.sem, ranks_read.step)

            def route_end():
                src, dst, w = r_a, r_b, 1
                while w < NTT:
                    link(dve.tensor_copy(dst[:, 0:w, :], src[:, 0:w, :]))
                    link(dve.tensor_tensor(dst[:, w:, :], src[:, w:, :], src[:, 0:NTT - w, :], ALU.add))
                    src, dst, w = dst, src, 2 * w
                link(dve.tensor_tensor(r_cnt[:], over(src[:, NTT - 1, :].unsqueeze(2), [P, NE, NE]), over(lim8[:].unsqueeze(1), [P, NE, NE]), ALU.is_gt))
                link(dve.tensor_reduce(r_n[:, 0, :], r_cnt[:], AX.X, ALU.add))
                link(dve.tensor_copy(r_n[:, 1, :], r_n[:, 0, :]))
                at, to, w = 1, 2, 1
                while w < NE:
                    link(dve.tensor_copy(r_n[:, to, 0:w], r_n[:, at, 0:w]))
                    link(dve.tensor_tensor(r_n[:, to, w:], r_n[:, at, w:], r_n[:, at, 0:NE - w], ALU.add))
                    at, to, w = to, at, 2 * w
                link(dve.tensor_tensor(r_ow[:], over(iotab[:].unsqueeze(2), [P, NBLK, NE]), over(r_n[:, at, :].unsqueeze(1), [P, NBLK, NE]), ALU.is_ge))
                link(dve.tensor_reduce(r_of[:], r_ow[:], AX.X, ALU.add))
                link(dve.tensor_scalar(r_of[:], r_of[:], float(NE - 1), None, ALU.min))
                link(dve.tensor_copy(owner[:], r_of[0:1, :]))
                link(dve.tensor_tensor(r_n[:, to, :], r_n[:, at, :], r_n[:, 0, :], ALU.subtract))
                link(dve.tensor_scalar(r_n[:, to, :], r_n[:, to, :], float(BLK), None, ALU.mult))
                link(dve.tensor_tensor(dst[:], r_rank[:], over(r_n[:, to, :].unsqueeze(1), full), ALU.add))
                link(dve.tensor_tensor(dst[:, 1:, :], dst[:, 1:, :], src[:, 0:NTT - 1, :], ALU.add))
                for k in range(2):
                    link(dve.tensor_tensor(r_mk[:], r_oh[:, k], dst[:], ALU.mult))
                    link(dve.tensor_reduce(r_sl[:, k, :], r_mk[:], AX.X, ALU.add))
                link(dve.tensor_copy(slots[:], r_sl[:]))

            def begin_best(bt):
                acc = scores_of[bt]
                for i in range(1, NT):
                    diag = acc[:, OFF[i + 1] - P:OFF[i + 1]]
                    last = dve.tensor_tensor(diag, diag, causal[:], ALU.add)
                last.then_inc(diag_ok.sem, diag_ok.step)
                dve.wait_ge(diag_ok.sem, diag_ok.at(bt))

            def find(bt, k, i):
                n = (bt * ROUNDS + k) * (NT - 1) + i - 1
                behind = in_register(dve, taken_ok.at(n, NT - 1))
                dve.wait_ge(taken_ok.sem, taken_ok.step)
                dve.wait_ge(taken_ok.sem, behind)
                dve.max(m8[:, i, :], scores_of[bt][:, OFF[i]:OFF[i + 1]]).then_inc(top8_ok.sem, top8_ok.step)

            def take(bt, k, i):
                a = scores_of[bt][:, OFF[i]:OFF[i + 1]]
                behind = in_register(dve, top8_ok.at((bt * ROUNDS + k) * (NT - 1) + i - 1))
                dve.wait_ge(top8_ok.sem, top8_ok.step)
                dve.wait_ge(top8_ok.sem, behind)
                dve.match_replace(a, m8[:, i, :], a, TAKEN).then_inc(taken_ok.sem, taken_ok.step)

            def find_and_take(bt, k, tiles):
                find(bt, k, tiles[0])
                for i, after in zip(tiles, tiles[1:]):
                    find(bt, k, after)
                    take(bt, k, i)
                take(bt, k, tiles[-1])

            def end_best(bt):
                acc = scores_of[bt]
                dve.wait_ge(taken_ok.sem, taken_ok.at((bt + 1) * ROUNDS * (NT - 1) - 1))
                for i in range(1, NT):
                    a = acc[:, OFF[i]:OFF[i + 1]]
                    dve.tensor_scalar(a, a, TAKEN, MASKED, ALU.not_equal, ALU.mult)
                dve.tensor_copy(acc[:, 0:P], causal[:]).then_inc(mask_ok.sem, mask_ok.step)
                dve.wait_ge(mask_ok.sem, mask_ok.at(bt))

            def up_lo(c, r, q):
                dve.wait_ge(wguhi_ok.sem, wguhi_ok.at(c))
                dve.tensor_tensor(wgu[1][:, q, :], we[:, r, 0:2 * D], plain(wgu[0][:, q, :]), ALU.subtract).then_inc(wgulo_ok.sem, wgulo_ok.step)

            for b in range(B):
                if b == 1:
                    begin_best(0)
                def normalise(it):
                    for j in range(2):
                        n = b * NT + it * 2 + j
                        dve.wait_ge(x_in[j].sem, x_in[j].at(b * (NT // 2) + it))
                        dve.bn_stats(ln_st[:, j, :], x_sb[:, j, :]).then_inc(stats.sem, stats.step)
                        dve.wait_ge(stats.sem, stats.at(n))
                        dve.bn_aggr(ln_mv[:, j, :], ln_st[:, j, :]).then_inc(moments.sem, moments.step)
                        dve.wait_ge(deviation.sem, deviation.at(n))
                        dve.reciprocal(ln_r[:, j, :], ln_sd[:, j, :]).then_inc(inverse.sem, inverse.step)
                        dve.wait_ge(inverse.sem, inverse.at(n))
                        dve.wait_ge(xt_full.sem, xt_full.at(n, 2))
                        dve.wait_ge(xn_out[j].sem, xn_out[j].at(b * (NT // 2) + it, 1))
                        dve.tensor_scalar(xn[:, j, :], x_sb[:, j, :], ln_mv[:, j, 0:1], ln_r[:, j, 0:1],
                                                     ALU.subtract, ALU.mult).then_inc(normed.sem, normed.step)

                def turn(it):
                    for j in range(2):
                        n = b * NT + it * 2 + j
                        dve.wait_ge(xhi_ok.sem, xhi_ok.at(n))
                        dve.tensor_tensor(xT[1][:, j, :], banks[:, j, :], plain(xT[0][:, j, :]), ALU.subtract).then_inc(xlo_ok.sem, xlo_ok.step)
                    if b == 1:
                        find_and_take(0, it * 2, FIRST_TILES)

                def norms(it, tiles=(0, 1)):
                    for j in tiles:
                        n = b * NT + it * 2 + j
                        dve.wait_ge(projected.sem, projected.at(n))
                        dve.wait_ge(natk_ok.sem, natk_ok.at(n, 2))
                        dve.tensor_copy(bs[:, j, :], banks[:, 3 + 2 * j, 0:NB]).then_inc(copied.sem, copied.step)
                        dve.wait_ge(copied.sem, copied.at(n))
                        dve.bn_stats(ik_st[:, j, :], bs[:, j, CIK - QR:CIW - QR]).then_inc(ik_stats.sem, ik_stats.step)
                        dve.wait_ge(ik_stats.sem, ik_stats.at(n))
                        dve.bn_aggr(ik_mv[:, j, :], ik_st[:, j, :]).then_inc(ik_moments.sem, ik_moments.step)
                        dve.tensor_scalar(iw[:, bass.ds(it * 2 + j, 1), :], bs[:, j:j + 1, CIW - QR:CLG - QR], float(H) ** -0.5, None, ALU.mult)
                        dve.tensor_copy(logits[:, bass.ds(n, 1), :], bs[:, j:j + 1, CLG - QR:NB])
                        dve.wait_ge(roots.sem, roots.at(n))
                        dve.reciprocal(r3[:, j, :], sd3[:, j, :]).then_inc(inverses.sem, inverses.step)
                        dve.wait_ge(inverses.sem, inverses.at(n))
                        dve.wait_ge(nt_full.sem, nt_full.at(n, 4))
                        dve.tensor_scalar(nat_q[:, n % 4, 0:QR], banks[:, 2 + 2 * j, 0:QR], r3[:, j, 0:1], None, ALU.mult)
                        dve.tensor_scalar(nat_q[:, n % 4, QR:], bs[:, j, 0:KVR], r3[:, j, 1:2], None, ALU.mult).then_inc(natq_ok.sem, natq_ok.step)
                def turn_normed(it, tiles=(0, 1)):
                    for j in tiles:
                        n = b * NT + it * 2 + j
                        cols = bass.ds((it * 2 + j) * P, P)
                        dve.wait_ge(nhi_ok.sem, nhi_ok.at(n))
                        for c in range(KQ):
                            dve.scalar_tensor_tensor(qrT[1][:, c, cols], banks[:, 6, c * P:c * P + P], q_ln[:, c:c + 1],
                                                     plain(qrT[0][:, c, cols]), ALU.mult, ALU.subtract)
                        dve.scalar_tensor_tensor(ckvT[1][:, cols], banks[:, 6, QR:QR + KVR], kv_ln[:, 0:1],
                                                 plain(ckvT[0][:, cols]), ALU.mult, ALU.subtract)
                        dve.tensor_tensor(kpT[1][:, :, cols], banks[:, 7, 0:2 * P].rearrange("p (a c) -> p a c", a=2),
                                          plain(kpT[0][:, :, cols]), ALU.subtract)
                        dve.tensor_tensor(ikT[1][:, cols], banks[:, 7, 2 * P:3 * P], plain(ikT[0][:, cols]), ALU.subtract).then_inc(nlo_ok.sem, nlo_ok.step)

                normalise(0)
                for it in range(NT // 2):
                    turn(it)
                    if it + 1 < NT // 2:
                        normalise(it + 1)
                    if b == 1:
                        find_and_take(0, it * 2, LAST_TILES)
                    if b == 0:
                        norms(it)
                        if it:
                            turn_normed(it - 1)
                    else:
                        for j in range(2):
                            if it:
                                turn_normed(it - 1, (j,))
                            norms(it, (j,))
                    if b == 1:
                        find_and_take(0, it * 2 + 1, FIRST_TILES)
                        find_and_take(0, it * 2 + 1, LAST_TILES)
                turn_normed(NT // 2 - 1)
                barrier(dve, 2 * b)

                acc = scores_of[b]
                dve.memset(turned[:], 0.0)
                dve.memset(acc[:], 0.0).then_inc(acc_clear.sem, acc_clear.step)
                dve.wait_ge(acc_clear.sem, acc_clear.at(b))

                def queries(q, c):
                    g, tok = q * 2 + c, slice(c * 512, c * 512 + 512)
                    dve.wait_ge(iq_full.sem, iq_full.at(g))
                    dve.wait_ge(iy_ok.sem, iy_ok.at(g, 1))
                    dve.tensor_tensor(scaled[:], banks[:, 4 + c, :], idx_c[:, tok], ALU.mult)
                    dve.tensor_tensor(turned[0:32, :], banks[64:96, 4 + c, :], rope_s[64:96, tok], ALU.mult)
                    dve.tensor_tensor(turned[64:96, :], banks[0:32, 4 + c, :], rope_s[0:32, tok], ALU.mult).then_inc(i_parts.sem, i_parts.step)

                def index_step(hp, u, last):
                    h = hp * 2 + u
                    q = b * H + h
                    for i in range(1, NT):
                        if i in (1, 4) and not (last and u == 1):
                            queries(q + 1, i // 4)
                        n = q * (NT - 1) + i - 1
                        r, _ = index_slot(u, i)
                        a = acc[:, OFF[i]:OFF[i + 1]]
                        dve.wait_ge(relu_ok.sem, relu_ok.at(n))
                        dve.scalar_tensor_tensor(a, relu[:, r, 0:EXT[i]], iw[:, i, bass.ds(h, 1)], a, ALU.mult, ALU.add).then_inc(acc_ok.sem, acc_ok.step)
                    if b == 1:
                        find_and_take(0, hp + ROUNDS // 2, LAST_TILES if u else FIRST_TILES)

                if b == B - 1:
                    route_start()
                dve.wait_ge(idx_c_in.sem, idx_c_in.at(b))
                for c in range(2):
                    queries(b * H, c)
                if b == B - 1:
                    route_ranks()
                with dve.Fori(0, PAIRS - 1) as hp:
                    for u in range(2):
                        index_step(hp, u, False)
                for u in range(2):
                    index_step(PAIRS - 1, u, True)
                if b == B - 1:
                    end_best(0)
                    route_end()
                dve.wait_ge(acc_ok.sem, acc_ok.at((b + 1) * H * (NT - 1) - 1))
                barrier(dve, 2 * b + 1)

            for b in range(B):
                acc = scores_of[b]
                if b == 0:
                    begin_best(1)

                def rotary(g, o, p, c):
                    n, tok = (b * PAIRS + p) * 2 + c, slice(c * 512, c * 512 + 512)
                    bank = shared_bank(*o)
                    dve.wait_ge(sh_full.sem, sh_full.at(g + o[1]))
                    dve.wait_ge(py_ok.sem, py_ok.at(n, 1))
                    dve.tensor_tensor(p_scaled[:], banks[:, bank, :], rope_c[:, tok], ALU.mult)
                    dve.tensor_tensor(p_turned[0:64, :], banks[64:128, bank, :], rope_s[64:128, tok], ALU.mult)
                    dve.tensor_tensor(p_turned[64:128, :], banks[0:64, bank, :], rope_s[0:64, tok], ALU.mult).then_inc(sh_read.sem, sh_read.step)
                    dve.wait_ge(sh_read.sem, sh_read.at(g + o[1]))
                    dve.wait_ge(qplo_ok.sem, qplo_ok.at(n, 2))
                    dve.tensor_tensor(py[:, c, :], p_scaled[:], p_turned[:], ALU.add).then_inc(py_ok.sem, py_ok.step)

                def rotary_lo(p, c):
                    tok = slice(c * 512, c * 512 + 512)
                    dve.wait_ge(qphi_ok.sem, qphi_ok.at((b * PAIRS + p) * 2 + c))
                    dve.tensor_tensor(qp[1][:, tok], py[:, c, :], plain(qp[0][:, tok]), ALU.subtract).then_inc(qplo_ok.sem, qplo_ok.step)

                def first_masks(h, u, at):
                    for i in range(4):
                        if SCORES_AT[u][i] == at:
                            mask_and_max(h, i)

                def inverses_behind(h, u, at):
                    for i in range(4):
                        if INVERSES_AT[u][i] == at:
                            invert(h, i)

                def projections_lo(g, k, start, h, u, p, between=None):
                    todo = PROJECTIONS[u]
                    for at, c in enumerate(todo):
                        here = (start[0], start[1] + at)
                        if c >= ROTARY:
                            rotary(g, here, p, c - ROTARY)
                        else:
                            dst, src, hi = projection(c, u, 1), banks[:, shared_bank(*here), :], projection(c, u, 0)
                            if c >= 4:
                                src = src.rearrange("p (t d) -> p t d", t=4)
                            dve.wait_ge(sh_hi.sem, sh_hi.at(k))
                            dve.tensor_tensor(dst, src, plain(hi), ALU.subtract).then_inc(sh_read.sem, sh_read.step)
                            k = k + 1
                        if at == 0 and between is not None:
                            invert(between, 7)
                        if u == 0 and at in (2, 4):
                            rotary_lo(p, at // 2 - 1)
                        inverses_behind(h, u, at)
                        first_masks(h, u, at)

                def mask_and_max(h, i):
                    behind = in_register(dve, sc_full.at((b * H + h) * NT + i))
                    dve.wait_ge(sc_full.sem, sc_full.step)
                    dve.wait_ge(sc_full.sem, behind)
                    dve.tensor_tensor_reduce(probs[:, OFF[i]:OFF[i + 1]], scores_psum(i % 2, EXT[i]),
                                                        acc[:, OFF[i]:OFF[i + 1]], -SCALE, 3.0e38, ALU.add, ALU.min,
                                                        nmax[:, i:i + 1]).then_inc(masked.sem, masked.step)

                def invert(h, i):
                    dve.wait_ge(exps.sem, exps.at((b * H + h) * NT + i))
                    dve.reciprocal(rinv[:, i:i + 1], row_sum[:, i:i + 1]).then_inc(sums_inv.sem, sums_inv.step)

                def head_step(hp, u, last):
                    h, g, tail = hp * 2 + u, first_group(b, hp, u), last and u == 1

                    def block_lo(s, kt):
                        jj = 4 * s + kt
                        o = kt if s == 0 else NT0 + (0 if tail else NPR + NPE * u) + kt
                        lo = max(0, kt - 4 * s) * P
                        rotary_before = NPE if s == 1 and u == 1 and not tail else 0
                        dve.wait_ge(sh_hi.sem, sh_hi.at(split_group(b, hp, u) + (o - rotary_before)))
                        dve.tensor_tensor(PT[1][:, jj % 3, lo:512], banks[:, shared_bank(u, o), lo:512],
                                                      plain(PT[0][:, jj % 3, lo:512]), ALU.subtract).then_inc(sh_read.sem, sh_read.step)

                    def best(*pieces):
                        if b == 0:
                            for what, i in pieces:
                                what(1, h, i)

                    mask_and_max(h, 4)
                    block_lo(0, 0)
                    best((find, 1), (find, 2), (take, 1))
                    mask_and_max(h, 5)
                    invert(h, 4)
                    block_lo(0, 1)
                    best((find, 3), (take, 2))
                    mask_and_max(h, 6)
                    invert(h, 5)
                    block_lo(0, 2)
                    best((find, 4), (take, 3))
                    block_lo(0, 3)
                    invert(h, 6)
                    mask_and_max(h, 7)
                    best((find, 5), (take, 4))
                    if tail:
                        invert(h, 7)
                    else:
                        projections_lo(g, split_group(b, hp, u) + NT0, (u, NT0), h + 1, 1 - u, hp + u, h)
                    best((find, 6))
                    for kt in range(NT1):
                        block_lo(1, kt)
                        if not tail:
                            inverses_behind(h + 1, 1 - u, len(PROJECTIONS[1 - u]) + kt)
                            first_masks(h + 1, 1 - u, len(PROJECTIONS[1 - u]) + kt)
                        if kt == 1:
                            best((take, 5))
                        if kt == 3:
                            best((find, 7))
                        if kt == 5:
                            best((take, 6))
                    best((take, 7))

                projections_lo(first_group(b, 0, 0), split_group(b, 0, 0) - NPR, (0, -START), 0, 0, 0)
                for kt in range(4):
                    inverses_behind(0, 0, START + kt)
                    first_masks(0, 0, START + kt)
                with dve.Fori(0, PAIRS - 1) as hp:
                    for u in range(2):
                        head_step(hp, u, False)
                for u in range(2):
                    head_step(PAIRS - 1, u, True)
                if b == 0:
                    end_best(1)
                barrier(dve, 4 + 2 * b)

                with dve.Fori(0, H // 2) as hp:
                    for j in range(2):
                        n = b * H + hp * 2 + j
                        dve.wait_ge(ohi_ok.sem, ohi_ok.at(n))
                        dve.tensor_tensor(oTr[1][:, j, :], oT_raw[:, j, :], plain(oTr[0][:, j, :]), ALU.subtract).then_inc(olo_ok.sem, olo_ok.step)
                if b == B - 1:
                    up_lo(0, 0, 0)
                    up_lo(1, 1, 1)
                dve.wait_ge(xo_in.sem, xo_in.at(b))
                for t in range(NT):
                    dve.wait_ge(o_mm.sem, o_mm.at((b * H + H - 1) * NT + t))
                    dve.tensor_tensor(po[:, t, :], banks[:, t, :], xo[:, t, :], ALU.add).then_inc(po_ok.sem, po_ok.step)
                barrier(dve, 5 + 2 * b)

            def rows_lo(k, halves=(0, 1)):
                for a in halves:
                    dve.wait_ge(xehi_ok.sem, xehi_ok.at(k * 2 + a))
                    dve.tensor_tensor(xeT[1][:, parity(k), a * P:a * P + P], banks[:, a, :].rearrange("p (k t) -> p k t", k=KD),
                                                  plain(xeT[0][:, parity(k), a * P:a * P + P]), ALU.subtract).then_inc(xelo_ok.sem, xelo_ok.step)

            def chunks(k, last):
                for m in range(KM):
                    c, q = k * KM + m, m % 2
                    dve.wait_ge(silu_ok.sem, silu_ok.at(c))
                    dve.wait_ge(hlo_ok.sem, hlo_ok.at(c, 2))
                    dve.tensor_tensor(hf[:, q, :], banks[:, 2 + q, BLK:2 * BLK], sg[:, q, :], ALU.mult).then_inc(h_ok.sem, h_ok.step)
                    dve.wait_ge(hhi_ok.sem, hhi_ok.at(c))
                    dve.tensor_tensor(hT[1][:, q, :], hf[:, q, :], plain(hT[0][:, q, :]), ALU.subtract).then_inc(hlo_ok.sem, hlo_ok.step)
                    up_lo(c + 2, (m + 2) % NWR, q)
                    if m in (NEXT_ROWS + 1, NEXT_ROWS + 2) and not last:
                        rows_lo(k + 1, (m - NEXT_ROWS - 1,))

            rows_lo(0)
            with dve.Fori(0, NBLK - 1) as k:
                chunks(k, False)
            chunks(NBLK - 1, True)
            barrier(dve, 8)

            with dve.Fori(0, B * NT // NMIX) as it:
                for j in range(NMIX):
                    n = it * NMIX + j
                    dve.wait_ge(part_in[j].sem, part_in[j].at(it))
                    dve.wait_ge(g_in[j].sem, g_in[j].at(it * 2 + 1))
                    dve.scalar_tensor_tensor(mix[:, j, :], g_a[:, j, :], gates[:, 0, bass.ds(n, 1)], part_sb[:, j, :], ALU.mult, ALU.add).then_inc(mix_ok.sem, mix_ok.step)
                    dve.wait_ge(mix_ok.sem, mix_ok.at(n))
                    dve.wait_ge(fin_out[j].sem, fin_out[j].at(it, 1))
                    dve.scalar_tensor_tensor(fin[:, j, :], g_b[:, j, :], gates[:, 1, bass.ds(n, 1)], mix[:, j, :], ALU.mult, ALU.add).then_inc(fin_ok.sem, fin_ok.step)

        @block.gpsimd
        def _(pool):
            for e in evs["pool"]:
                if e.credit:
                    pool.sem_inc(e.sem, e.credit * e.step)
            pool.wait_ge(consts.sem, consts.at(EARLY - 1))
            pool.memset(zero[:], 0.0).then_inc(zero_ok.sem, zero_ok.step)
            pool.iota(iota8[:], [[1, NE]], base=0, channel_multiplier=0, allow_small_or_imprecise_dtypes=True)
            pool.iota(lim8[:], [[BLK, NE]], base=0, channel_multiplier=0, allow_small_or_imprecise_dtypes=True)
            pool.iota(iotab[:], [[1, NBLK]], base=0, channel_multiplier=0, allow_small_or_imprecise_dtypes=True).then_inc(rt_pool.sem, rt_pool.step)
            def weights_lo(q, u):
                pool.wait_ge(wi_hi_ok.sem, wi_hi_ok.at(q))
                pool.tensor_tensor(wi[1][:, u], wi_raw[:, u], plain(wi[0][:, u]), ALU.subtract).then_inc(wi_lo_ok.sem, wi_lo_ok.step)

            def pair_weights_lo(n):
                pool.wait_ge(wp_hi_ok.sem, wp_hi_ok.at(n))
                pool.tensor_tensor(wp[1][:], wp_raw[:], plain(wp[0][:]), ALU.subtract).then_inc(wp_lo_ok.sem, wp_lo_ok.step)

            def head_weights_lo(n):
                pool.wait_ge(wh_hi_ok.sem, wh_hi_ok.at(n))
                pool.tensor_tensor(wh[1][:], wh_raw[:], plain(wh[0][:]), ALU.subtract).then_inc(wh_lo_ok.sem, wh_lo_ok.step)

            for b in range(B):
                pool.memset(nat_k[:], 0.0).then_inc(nat_clear.sem, nat_clear.step)
                pool.wait_ge(nat_clear.sem, nat_clear.at(b))
                if b == 0:
                    pool.wait_ge(wa_hi_ok.sem, wa_hi_ok.at(0))
                    pool.tensor_tensor(wa[1][:], wa_raw[:], plain(wa[0][:]), ALU.subtract).then_inc(wa_lo_ok.sem, wa_lo_ok.step)
                for it in range(NT // 2):
                    for j in range(2):
                        n = b * NT + it * 2 + j
                        both = [P, 2, HALF]
                        cos = nat_c[:, bass.ds(it * 2 + j, 1), :].broadcast_to(both)
                        sin = nat_s[:, bass.ds(it * 2 + j, 1), :].broadcast_to(both)
                        kp = bs[:, j, CKP - QR:CIK - QR].rearrange("p (a c) -> p a c", a=2)
                        pool.wait_ge(inverses.sem, inverses.at(n))
                        pool.wait_ge(natk_ok.sem, natk_ok.at(n, 1))
                        pool.wait_ge(nt_full.sem, nt_full.at(n, 4))
                        pool.tensor_scalar(ikn[:], bs[:, j, CIK - QR:CIW - QR], ik_mv[:, j, 0:1], r3[:, j, 2:3],
                                                           ALU.subtract, ALU.mult).then_inc(key_step[0].sem, key_step[0].step)
                        pool.tensor_tensor(rk1[:], kp, cos, ALU.mult)
                        pool.tensor_tensor(rk2[:], kp, sin, ALU.mult).then_inc(key_step[1].sem, key_step[1].step)
                        pool.wait_ge(key_step[0].sem, key_step[0].at(n))
                        pool.tensor_tensor(ikn[:], ikn[:], kn_w[:], ALU.mult).then_inc(key_step[2].sem, key_step[2].step)
                        pool.wait_ge(key_step[1].sem, key_step[1].at(n))
                        for odd in range(2):
                            o = HALF * odd
                            pool.tensor_tensor(nat_k[:, n % 4, odd, o:o + HALF], rk1[:, 0, :], rk2[:, 1, :], ALU.subtract)
                            pool.tensor_tensor(nat_k[:, n % 4, odd, 64 + o:64 + o + HALF], rk1[:, 1, :], rk2[:, 0, :], ALU.add)
                        pool.wait_ge(key_step[2].sem, key_step[2].at(n))
                        pool.tensor_tensor(ikn[:], ikn[:], kn_b[:], ALU.add).then_inc(key_step[3].sem, key_step[3].step)
                        pool.wait_ge(key_step[3].sem, key_step[3].at(n))
                        rot = ikn[:, 0:ROPE].rearrange("p (a c) -> p a c", a=2)
                        pool.tensor_tensor(ri1[:], rot, cos, ALU.mult)
                        pool.tensor_tensor(ri2[:], rot, sin, ALU.mult).then_inc(key_step[4].sem, key_step[4].step)
                        pool.tensor_copy(nat_k[:, n % 4, 2, HALF:2 * HALF], ikn[:, ROPE:ROPE + HALF])
                        pool.tensor_copy(nat_k[:, n % 4, 2, 3 * HALF:], ikn[:, ROPE + HALF:])
                        pool.wait_ge(key_step[4].sem, key_step[4].at(n))
                        pool.tensor_tensor(nat_k[:, n % 4, 2, 0:HALF], ri1[:, 0, :], ri2[:, 1, :], ALU.subtract)
                        pool.tensor_tensor(nat_k[:, n % 4, 2, 2 * HALF:3 * HALF], ri1[:, 1, :], ri2[:, 0, :], ALU.add).then_inc(natk_ok.sem, natk_ok.step)
                for u in range(2):
                    weights_lo(b * H + u, u)
                barrier(pool, 2 * b)

                def queries_sum(q, c):
                    pool.wait_ge(i_parts.sem, i_parts.at(q * 2 + c))
                    pool.wait_ge(iqlo_ok.sem, iqlo_ok.at(q * 2 + c, 2))
                    pool.tensor_tensor(iy[:, c, :], scaled[:], turned[:], ALU.add).then_inc(iy_ok.sem, iy_ok.step)

                def queries_lo(q, u, c):
                    tok = slice(c * 512, c * 512 + 512)
                    pool.wait_ge(iqhi_ok.sem, iqhi_ok.at(q * 2 + c))
                    pool.tensor_tensor(iqT[1][:, u, tok], iy[:, c, :], plain(iqT[0][:, u, tok]), ALU.subtract).then_inc(iqlo_ok.sem, iqlo_ok.step)

                for c in range(2):
                    queries_sum(b * H, c)
                    queries_lo(b * H, 0, c)
                with pool.Fori(0, PAIRS - 1) as hp:
                    for u in range(2):
                        q = b * H + hp * 2 + u + 1
                        queries_sum(q, 0)
                        weights_lo(q + 1, u)
                        queries_lo(q, 1 - u, 0)
                        queries_sum(q, 1)
                        queries_lo(q, 1 - u, 1)
                for c in range(2):
                    queries_sum(b * H + H - 1, c)
                    queries_lo(b * H + H - 1, 1, c)
                if b == B - 1:
                    pool.wait_ge(kept_out.sem, kept_out.at(B * len(kept) - 1))
                    for part in (1, 2, 4, 5):
                        pool.dma_start(kept[part], kept_d[part][0]).then_inc(kept_in.sem, kept_in.step)
                    pool.wait_ge(iq_full.sem, iq_full.at((b * H + H) * 2 - 1))
                    for part in (0, 3):
                        pool.dma_start(kept[part], kept_d[part][0]).then_inc(kept_in.sem, kept_in.step)
                    pool.wait_ge(kept_in.sem, kept_in.at(len(kept) - 1))
                if b == B - 1:
                    pair_weights_lo(0)
                    head_weights_lo(0)
                barrier(pool, 2 * b + 1)

            for b in range(B):
                def normalise(h, i):
                    a = probs[:, OFF[i]:OFF[i + 1]]
                    behind = in_register(pool, sums_inv.at((b * H + h) * NT + i))
                    pool.wait_ge(sums_inv.sem, sums_inv.step)
                    pool.wait_ge(sums_inv.sem, behind)
                    pool.tensor_scalar(a, a, rinv[:, i:i + 1], None, ALU.mult).then_inc(p_norm.sem, p_norm.step)

                def head_step(hp, u, last):
                    h, tail = hp * 2 + u, last and u == 1
                    normalise(h, 4)
                    if not tail:
                        if u == 1:
                            pair_weights_lo(b * PAIRS + hp + 1)
                        head_weights_lo(b * H + h + 1)
                    for i in range(5, NT - 1):
                        normalise(h, i)
                    if b == 0:
                        behind = in_register(pool, row_in[u].at(hp))
                        pool.wait_ge(row_in[u].sem, row_in[u].step)
                        pool.wait_ge(row_in[u].sem, behind)
                        pool.tensor_copy(slot_now[:, u, :], slots[:, :, bass.ds(h, 1)].rearrange("p k n -> p (k n)")).then_inc(slot_set.sem, slot_set.step)
                        behind = in_register(pool, slot_set.at(h))
                        pool.wait_ge(slot_set.sem, slot_set.step)
                        pool.wait_ge(slot_set.sem, behind)
                        for k in range(2):
                            pool.indirect_dma_start(xs_d, bass.IndirectOffsetOnAxis(ap=slot_now[:, u, k:k + 1], axis=0),
                                                                  rows[:, u, :], None).then_inc(row_sc[u].sem, row_sc[u].step)
                    if not tail:
                        for i in range(4):
                            normalise(h + 1, i)

                for i in range(4):
                    normalise(0, i)
                with pool.Fori(0, PAIRS - 1) as hp:
                    for u in range(2):
                        head_step(hp, u, False)
                for u in range(2):
                    head_step(PAIRS - 1, u, True)
                if b == 0:
                    for j in range(2):
                        pool.wait_ge(row_sc[j].sem, row_sc[j].at(B * NT - 1))
                barrier(pool, 4 + 2 * b)

                if b + 1 < B:
                    for part, there in zip(kept, kept_d):
                        pool.dma_start(part, there[b + 1]).then_inc(kept_in.sem, kept_in.step)
                with pool.Fori(0, H // 2) as hp:
                    for j in range(2):
                        n = b * H + hp * 2 + j
                        pool.wait_ge(owhi_ok.sem, owhi_ok.at(n))
                        pool.tensor_tensor(ow[1][:, j, :], ow_raw[:, j, :], plain(ow[0][:, j, :]), ALU.subtract).then_inc(owlo_ok.sem, owlo_ok.step)
                if b < B - 1:
                    pair_weights_lo((b + 1) * PAIRS)
                    head_weights_lo((b + 1) * H)
                else:
                    pool.wait_ge(wdnhi_ok.sem, wdnhi_ok.at(0))
                    pool.tensor_tensor(wdn[1][:, 0, :], we[:, 0, 2 * D:], plain(wdn[0][:, 0, :]), ALU.subtract).then_inc(wdnlo_ok.sem, wdnlo_ok.step)
                pool.wait_ge(kept_in.sem, kept_in.at(B * len(kept) - 1))
                barrier(pool, 5 + 2 * b)

            with pool.Fori(0, NBLK) as k:
                for m in range(KM):
                    c, q = k * KM + m, m % 2
                    pool.wait_ge(wdnhi_ok.sem, wdnhi_ok.at(c + 1))
                    pool.tensor_tensor(wdn[1][:, 1 - q, :], we[:, (m + 1) % NWR, 2 * D:], plain(wdn[0][:, 1 - q, :]), ALU.subtract).then_inc(wdnlo_ok.sem, wdnlo_ok.step)
            barrier(pool, 8)
            for n in range(B * NT):
                j = n % NMIX
                if n >= NMIX:
                    pool.wait_ge(fin_ok.sem, fin_ok.at(n - NMIX))
                for k, g in enumerate((g_a, g_b)):
                    pool.indirect_dma_start(g[:, j, :], None, ys_d,
                                                        bass.IndirectOffsetOnAxis(ap=slots[:, k, n:n + 1], axis=0)).then_inc(g_in[j].sem, g_in[j].step)

        @block.tensor
        def _(pe):
            for e in evs["pe"]:
                if e.credit:
                    pe.sem_inc(e.sem, e.credit * e.step)
            pe.wait_ge(consts.sem, consts.at(EARLY - 1))
            for b in range(B):
                pe.wait_ge(wa_lo_ok.sem, wa_lo_ok.at(0))
                def turn(it):
                    for j in range(2):
                        n = b * NT + it * 2 + j
                        pe.wait_ge(normed.sem, normed.at(n))
                        pe.wait_ge(xlo_ok.sem, xlo_ok.at(n, 2))
                        for c in range(KD):
                            last = pe.transpose(banks[:, j, c * P:c * P + P], xn[:, j, c * P:c * P + P], ident[:])
                        last.then_inc(xt_full.sem, xt_full.step)

                def project(it):
                    for j in range(2):
                        n = b * NT + it * 2 + j
                        pe.wait_ge(xlo_ok.sem, xlo_ok.at(n))
                        pe.wait_ge(natq_ok.sem, natq_ok.at(n, 2))
                        for bank, lo, hi in ((2 + 2 * j, 0, QR), (3 + 2 * j, QR, NA)):
                            for c in range(KD):
                                last = three(pe, banks[:, bank, 0:hi - lo], cut(xT, slice(None), j, slice(c * P, c * P + P)),
                                             cut(wa, slice(None), c, slice(lo, hi)), c == 0, c == KD - 1)
                        last.then_inc(projected.sem, projected.step)

                def turn_normed(it):
                    for j in range(2):
                        n = b * NT + it * 2 + j
                        pe.wait_ge(natq_ok.sem, natq_ok.at(n))
                        pe.wait_ge(natk_ok.sem, natk_ok.at(n))
                        pe.wait_ge(nlo_ok.sem, nlo_ok.at(n, 1))
                        for c in range(4):
                            pe.transpose(banks[:, 6, c * P:c * P + P], nat_q[:, n % 4, c * P:c * P + P], ident[:])
                        for c in range(3):
                            last = pe.transpose(banks[:, 7, c * P:c * P + P], nat_k[:, n % 4, c, :], ident[:])
                        last.then_inc(nt_full.sem, nt_full.step)

                for it in range(NT // 2):
                    turn(it)
                    project(it)
                    if it:
                        turn_normed(it - 1)
                turn_normed(NT // 2 - 1)
                barrier(pe, 2 * b)

                def queries(q, u, c):
                    if c == 0:
                        pe.wait_ge(wi_lo_ok.sem, wi_lo_ok.at(q))
                    pe.wait_ge(i_parts.sem, i_parts.at(q * 2 + c, 2))
                    tok = slice(c * 512, c * 512 + 512)
                    for k in range(KQ):
                        last = three(pe, banks[:, 4 + c, :], cut(wi, slice(None), u, k), cut(qrT, slice(None), k, tok), k == 0, k == KQ - 1)
                    last.then_inc(iq_full.sem, iq_full.step)

                def index_step(hp, u, last_pair):
                    q = b * H + hp * 2 + u
                    for i in range(1, NT):
                        if i in (1, 4):
                            if not (last_pair and u == 1):
                                queries(q + 1, 1 - u, i // 4)
                            pe.wait_ge(iqlo_ok.sem, iqlo_ok.at(q * 2 + i // 4))
                        n = q * (NT - 1) + i - 1
                        r, ago = index_slot(u, i)
                        pe.wait_ge(relu_ok.sem, relu_ok.at(n, ago))
                        for lo in range(0, EXT[i], 512):
                            hi = min(EXT[i], lo + 512)
                            last = three(pe, banks[:, SCORE_BANKS[r] + lo // 512, 0:hi - lo], cut(iqT, slice(None), u, slice(i * P, i * P + P)),
                                         cut(ikT, slice(None), slice(lo, hi)))
                        last.then_inc(is_full.sem, is_full.step)

                for c in range(2):
                    queries(b * H, 0, c)
                if b == B - 1:
                    pe.wait_ge(rt.sem, rt.at(RT_MARKED))
                    marks = r_mk[:].rearrange("p n e -> p (n e)")
                    pe.matmul(banks[:, 6, 0:B * NT * NE], upper[:], marks, start=True, stop=True)
                    pe.matmul(banks[:, 7, 0:B * NT * NE], ones[:], marks, start=True, stop=True).then_inc(rt_pe.sem, rt_pe.step)
                    pe.wait_ge(ranks_read.sem, ranks_read.at(0))
                with pe.Fori(0, PAIRS - 1) as hp:
                    for u in range(2):
                        index_step(hp, u, False)
                for u in range(2):
                    index_step(PAIRS - 1, u, True)
                barrier(pe, 2 * b + 1)

            for b in range(B):
                def turn(g, u, o):
                    pe.wait_ge(sh_read.sem, sh_read.at(g + o, bank_use(u, o)))
                    return banks[:, shared_bank(u, o), :]

                def scores_behind(h, u, at):
                    for i in range(4):
                        if SCORES_AT[u][i] == at:
                            scores(h, u, i)

                def project(g, start, h, u, p):
                    todo = PROJECTIONS[u]
                    pe.wait_ge(wh_lo_ok.sem, wh_lo_ok.at(b * H + h))
                    if u == 0:
                        pe.wait_ge(wp_lo_ok.sem, wp_lo_ok.at(b * PAIRS + p))
                    for at, c in enumerate(todo):
                        out = turn(g, start[0], start[1] + at)
                        tok = slice(c % 2 * 512, c % 2 * 512 + 512)
                        if c >= ROTARY:
                            for k in range(KQ):
                                last = three(pe, out, cut(wp, slice(None), k), cut(qrT, slice(None), k, tok), k == 0, k == KQ - 1)
                        elif c < 2:
                            for k in range(KQ):
                                last = three(pe, out, cut(wh, slice(None), slice(k * P, k * P + P)), cut(qrT, slice(None), k, tok), k == 0, k == KQ - 1)
                        elif c < 4:
                            last = three(pe, out, cut(wh, slice(None), slice(384, 512)), cut(ckvT, slice(None), tok))
                        else:
                            for t in range(4):
                                row = ((c - 4) * 4 + t) * P
                                last = three(pe, out[:, t * P:t * P + P], cut(ckvT, slice(None), slice(row, row + P)),
                                             cut(wh, slice(None), slice(512, 640)))
                        last.then_inc(sh_full.sem, sh_full.step)
                        if at == SCORES_AT[u][0]:
                            pe.wait_ge(sh_read.sem, sh_read.at(g + start[1] + todo.index(0)))
                            if u == 0:
                                pe.wait_ge(qplo_ok.sem, qplo_ok.at((b * PAIRS + p) * 2))
                        scores_behind(h, u, at)

                def scores(h, u, i):
                    pe.wait_ge(masked.sem, masked.at((b * H + h) * NT + i, 2))
                    rows_i = slice(i * P, i * P + P)
                    for lo in range(0, EXT[i], 512):
                        hi = min(EXT[i], lo + 512)
                        out = banks[:, 2 * (i % 2) + lo // 512, 0:hi - lo]
                        three(pe, out, cut(qn, slice(None), rows_i), cut(kT, slice(None), slice(lo, hi)), True, False)
                        last = three(pe, out, cut(qp, slice(None), rows_i), cut(kpT, slice(None), u, slice(lo, hi)), False, True)
                    last.then_inc(sc_full.sem, sc_full.step)

                def head_step(hp, u, last):
                    h, g, tail = hp * 2 + u, first_group(b, hp, u), last and u == 1
                    second = NT0 + (0 if tail else NPR + NPE * u)

                    def turn_probs(s, kt):
                        out = turn(g, u, second * s + kt)
                        for i in range(max(4 * s, kt), 4 * s + 4):
                            if kt == 0 and i < NT - 1:
                                pe.wait_ge(p_norm.sem, p_norm.at((b * H + h) * (NT - 1) + i))
                            if kt == 0 and i == NT - 1:
                                pe.wait_ge(last_norm.sem, last_norm.at(b * H + h))
                            last = pe.transpose(out[:, (i - 4 * s) * P:(i - 4 * s + 1) * P],
                                                probs[:, OFF[i] + kt * P:OFF[i] + kt * P + P], ident[:])
                        last.then_inc(sh_full.sem, sh_full.step)

                    def values(s, kt):
                        jj, lo = 4 * s + kt, max(0, kt - 4 * s) * P
                        if kt == 0:
                            pe.wait_ge(oT_read.sem, oT_read.at((b * H + h) * 2 + s, 1))
                        pe.wait_ge(sh_read.sem, sh_read.at(g + second * s + kt))
                        last = three(pe, banks[:, 7, lo:512], cut(v_, slice(None), u, kt), cut(PT, slice(None), jj % 3, slice(lo, 512)),
                                     kt == 0, kt == 4 * s + 3)
                        last.then_inc(pv_done.sem, pv_done.step)

                    if u == 0:
                        pe.wait_ge(qplo_ok.sem, qplo_ok.at((b * PAIRS + hp) * 2 + 1))
                    scores(h, u, 4)
                    turn_probs(0, 0)
                    scores(h, u, 5)
                    turn_probs(0, 1)
                    scores(h, u, 6)
                    turn_probs(0, 2)
                    values(0, 0)
                    turn_probs(0, 3)
                    values(0, 1)
                    values(0, 2)
                    scores(h, u, 7)
                    values(0, 3)
                    if not tail:
                        project(g, (u, NT0), h + 1, 1 - u, hp + u)
                    for kt in range(NT1):
                        turn_probs(1, kt)
                        if not tail:
                            scores_behind(h + 1, 1 - u, len(PROJECTIONS[1 - u]) + kt)
                        if kt >= 2:
                            values(1, kt - 2)
                    values(1, NT1 - 2)
                    values(1, NT1 - 1)

                project(first_group(b, 0, 0), (0, -START), 0, 0, 0)
                for kt in range(2):
                    scores_behind(0, 0, START + kt)
                pe.wait_ge(sh_read.sem, sh_read.at(first_group(b, 0, 0) - 1))
                with pe.Fori(0, PAIRS - 1) as hp:
                    for u in range(2):
                        head_step(hp, u, False)
                for u in range(2):
                    head_step(PAIRS - 1, u, True)
                barrier(pe, 4 + 2 * b)

                def head_rows(h, j, first):
                    pe.wait_ge(olo_ok.sem, olo_ok.at(b * H + h))
                    pe.wait_ge(owlo_ok.sem, owlo_ok.at(b * H + h))
                    for t in range(NT):
                        three(pe, banks[:, t, :], cut(oTr, slice(None), j, slice(t * P, t * P + P)), cut(ow, slice(None), j), first, False).then_inc(o_mm.sem, o_mm.step)

                head_rows(0, 0, True)
                head_rows(1, 1, False)
                with pe.Fori(1, H // 2) as hp:
                    for j in range(2):
                        head_rows(hp * 2 + j, j, False)
                barrier(pe, 5 + 2 * b)

            def turn_rows(k):
                pe.wait_ge(xe_in.sem, xe_in.at(k))
                for a in range(2):
                    pe.wait_ge(xelo_ok.sem, xelo_ok.at(k * 2 + a, 2))
                    for c in range(KD):
                        last = pe.transpose(banks[:, a, c * P:c * P + P], xe[:, a, c * P:c * P + P], ident[:])
                    last.then_inc(xeT_full.sem, xeT_full.step)

            def up(k, m):
                q, half = m % 2, k % 2 * KD
                pe.wait_ge(wgulo_ok.sem, wgulo_ok.at(k * KM + m))
                pe.wait_ge(h_ok.sem, h_ok.at(k * KM + m, 2))
                if m == 0:
                    pe.wait_ge(xelo_ok.sem, xelo_ok.at(k * 2 + 1))
                for w in range(2):
                    for c in range(KD):
                        last = three(pe, banks[:, 2 + q, w * BLK:w * BLK + BLK], cut(wgu, slice(None), q, slice(w * D + c * P, w * D + c * P + P)),
                                     cut(xeT, slice(None), at(half + c)), c == 0, c == KD - 1)
                last.then_inc(gu_full.sem, gu_full.step)

            def down_rows(k, m):
                q = m % 2
                pe.wait_ge(hlo_ok.sem, hlo_ok.at(k * KM + m))
                pe.wait_ge(wdnlo_ok.sem, wdnlo_ok.at(k * KM + m))
                if m == 0:
                    pe.wait_ge(ye_ok.sem, ye_ok.at(k, 1))
                for a in range(2):
                    last = three(pe, banks[:, 6 + a, :], cut(hT, slice(None), q, slice(a * P, a * P + P)), cut(wdn, slice(None), q), m == 0, m == KM - 1)
                last.then_inc(down.sem, down.step)

            def products(k, last):
                for m in range(KM - 1):
                    up(k, m + 1)
                    down_rows(k, m)
                    if m == NEXT_ROWS and not last:
                        turn_rows(k + 1)
                if not last:
                    up(k + 1, 0)
                down_rows(k, KM - 1)

            turn_rows(0)
            up(0, 0)
            with pe.Fori(0, NBLK - 1) as k:
                products(k, False)
            products(NBLK - 1, True)
            barrier(pe, 8)


def tables():
    f32 = np.float32
    inv = 1.0 / 10000.0 ** (np.arange(0, ROPE, 2, dtype=f32) / ROPE)
    ang = np.outer(np.arange(S, dtype=f32), inv).astype(f32)
    cos, sin = np.cos(ang).astype(f32), np.sin(ang).astype(f32)
    c4, s4 = np.tile(cos.T, (4, 1)), np.tile(sin.T, (4, 1))
    sign = np.where(np.arange(P) < 64, 1.0, -1.0).astype(f32)[:, None]
    turns = ((np.arange(P) // HALF) % 2 == 0)[:, None]
    k, q = np.arange(P)[None, :], np.arange(P)[:, None]
    return {
        "ident": np.eye(P, dtype=f32),
        "causal": np.where(k <= q, 0.0, MASKED).astype(f32),
        "upper": (q < k).astype(f32),
        "ones": np.ones((P, P), f32),
        "rope_c": np.ascontiguousarray(c4),
        "rope_s": np.ascontiguousarray(s4 * sign),
        "idx_c": np.where(turns, c4, 1.0).astype(f32),
        "nat_c": np.ascontiguousarray(cos.reshape(NT, P, HALF).transpose(1, 0, 2)),
        "nat_s": np.ascontiguousarray(sin.reshape(NT, P, HALF).transpose(1, 0, 2)),
    }


def kernel(**inputs):
    import concourse.bacc as bacc
    from concourse.bass_utils import run_bass_kernel_spmd

    g = {k.replace("L0_attn_", "").replace("L0_ffn_", ""): np.asarray(v) for k, v in inputs.items()}
    cc = np.ascontiguousarray

    def by_chunks(w, k):
        return cc(w.reshape(k, P, -1).transpose(1, 0, 2))

    wa = np.concatenate([g["q_a_w"].T, g["kv_a_w"].T, g["idx_wk_w"].T, g["idx_wproj_w"].T, g["gate_w"]], axis=1)
    qb = g["q_b_w"].reshape(H, NOPE + ROPE, QR)
    qn = qb[:, :NOPE, :].transpose(0, 2, 1).reshape(H, KQ, P, NOPE).transpose(0, 2, 1, 3).reshape(H, P, KQ * NOPE)
    qp = qb[:, NOPE:, :].reshape(PAIRS, 2, 2, HALF, QR).transpose(0, 2, 1, 3, 4).reshape(PAIRS, P, QR)
    qp = qp.transpose(0, 2, 1).reshape(PAIRS, KQ, P, P).transpose(0, 2, 1, 3)
    kvb = g["kv_b_w"].reshape(H, NOPE + VD, KVR).transpose(0, 2, 1)
    wh = np.concatenate([qn, kvb], axis=2)
    iq = g["idx_wq_b_w"].reshape(H, 4, HALF, QR)[:, [0, 2, 1, 3]].reshape(H, P, QR)
    wi = iq.transpose(0, 2, 1).reshape(H, KQ, P, P).transpose(0, 2, 1, 3)
    up = [g[w].reshape(NE, KD, P, KM, P).transpose(0, 3, 2, 1, 4).reshape(NE * KM, P, D) for w in ("w1", "w3")]
    arrays = {
        "x": g["hidden_states"],
        "wa": by_chunks(wa, KD),
        "wi": cc(wi),
        "wh": cc(wh),
        "wp": cc(qp),
        "ow": cc(g["o_w"].T.reshape(H, VD, D)),
        "we": cc(np.concatenate(up + [g["w2"].reshape(NE * KM, P, D)], axis=2)),
        "kn_w": cc(np.broadcast_to(g["idx_kn_w"], (P, ID))),
        "kn_b": cc(np.broadcast_to(g["idx_kn_b"], (P, ID))),
        "q_ln": cc(g["q_a_ln_w"].reshape(KQ, P).T),
        "kv_ln": cc(g["kv_a_ln_w"].reshape(P, 1)),
        **tables(),
    }
    nc = bacc.Bacc("TRN2", target_bir_lowering=False, num_devices=1)
    io = {n: nc.dram_tensor(f"in_{n}", a.shape, F32, kind="ExternalInput").ap() for n, a in arrays.items()}
    io["out"] = nc.dram_tensor("out_0", (B, S, D), F32, kind="ExternalOutput").ap()
    build(nc, io)
    r = run_bass_kernel_spmd(nc, [{f"in_{n}": a for n, a in arrays.items()}], core_ids=[0])
    return r.results[0]["out_0"]
```
